# Optimizing a Trainium2 kernel written in Bass

```python
import numpy as np
import jax
import jax.numpy as jnp

def _softmax(x, axis=-1):
    return jax.nn.softmax(x, axis=axis)

def _gelu(x):
    return jax.nn.gelu(x, approximate=True)

def _silu(x):
    return jax.nn.silu(x)

def _sigmoid(x):
    return jax.nn.sigmoid(x)

def _layernorm(x, axis=-1, eps=1e-05):
    m = jnp.mean(x, axis=axis, keepdims=True)
    v = jnp.var(x, axis=axis, keepdims=True)
    return (x - m) / jnp.sqrt(v + eps)

def _scatter_add(tgt, idx, src, axis=0):
    return tgt.at[idx].add(src)

def _segment_sum(src, seg, n):
    return jax.ops.segment_sum(src, seg, n)
kernel_name = 'mk_flamingo_gated_d4_seqx_r8_ae3f27'

def setup_inputs(seed: int=0):
    np.random.seed(seed)
    _w = jnp.asarray

    def _rec_inputs():
        import jax
        import jax.numpy as jnp
        _rk = jax.random.key(seed)
        x = -0.0002928 + 1 * jax.random.normal(jax.random.fold_in(_rk, 1), (32, 128, 128), jnp.float32)
        _lenS = 128 - jax.random.randint(jax.random.fold_in(_rk, 7), (32,), 0, max(1, 128 // 4) + 1, jnp.int32)
        _lenS2 = 128 - jax.random.randint(jax.random.fold_in(_rk, 8), (32,), 0, max(1, 128 // 4) + 1, jnp.int32)
        _ctx_1024P = jax.random.normal(jax.random.fold_in(_rk, 11), (32, 16, 128), jnp.float32)
        _ctx_1024c = jax.random.dirichlet(jax.random.fold_in(_rk, 511), 0.3 * jnp.ones((16,), jnp.float32), (32, 128))
        _ctx_1024t = jnp.einsum('bsk,bkd->bsd', _ctx_1024c, _ctx_1024P)
        _ctx_1024t = _ctx_1024t * jax.lax.rsqrt(jnp.mean(jnp.square(_ctx_1024t)) + 1e-12) * 0.953939
        ctx_1024 = -1.39393e-06 + 0.999914 * (_ctx_1024t + 0.3 * jax.random.normal(jax.random.fold_in(_rk, 611), (32, 128, 128), jnp.float32))
        _g = jax.random.normal(jax.random.fold_in(_rk, 9001), (2, 4), jnp.float32)
        _g = jnp.sign(_g) * jnp.maximum(jnp.abs(_g), 1.0) + (_g == 0) * 1.0
        g_xattn = _g[0]
        g_ffn = _g[1]
        return (x, ctx_1024, g_xattn, g_ffn)
    x, ctx_1024, g_xattn, g_ffn = _rec_inputs()

    def _L0_xattn_setup():
        import jax, jax.numpy as jnp
        import numpy as np
        D_MODEL = 128
        HEADS = 16
        D_K = D_MODEL // HEADS
        B, S = (2, 256)
        key = jax.random.key(seed)
        ks = jax.random.split(key, 11)
        sc = 1.0 / np.sqrt(D_MODEL)
        return {'q': jax.random.normal(ks[0], (B, S, D_MODEL), jnp.float32), 'k': jax.random.normal(ks[1], (B, S, D_MODEL), jnp.float32), 'v': jax.random.normal(ks[2], (B, S, D_MODEL), jnp.float32), 'Wq': jax.random.normal(ks[3], (D_MODEL, D_MODEL), jnp.float32) * sc, 'bq': jnp.zeros((D_MODEL,), jnp.float32), 'Wk': jax.random.normal(ks[4], (D_MODEL, D_MODEL), jnp.float32) * sc, 'bk': jnp.zeros((D_MODEL,), jnp.float32), 'Wv': jax.random.normal(ks[5], (D_MODEL, D_MODEL), jnp.float32) * sc, 'bv': jnp.zeros((D_MODEL,), jnp.float32), 'Wo': jax.random.normal(ks[6], (D_MODEL, D_MODEL), jnp.float32) * sc, 'bo': jnp.zeros((D_MODEL,), jnp.float32)}
    _L0_xattn_all = _L0_xattn_setup()
    _L0_xattn_in = {k: v for k, v in _L0_xattn_all.items() if k in ('Wq', 'bq', 'Wk', 'bk', 'Wv', 'bv', 'Wo', 'bo')}
    del _L0_xattn_all

    def _L0_ffn_setup():
        import jax, jax.numpy as jnp
        import numpy as np
        B, L, D = (4, 128, 128)
        E, H, K = (16, 64, 8)
        EPS = 1e-12

        def _l2norm(v, axis=-1):
            n = jnp.sqrt(jnp.sum(v * v, axis=axis, keepdims=True))
            return v / jnp.maximum(n, EPS)
        if __name__ == '__main__':
            out = reference(**setup_inputs())
            print(out.shape)
        key = jax.random.key(seed)
        ks = jax.random.split(key, 8)
        s = lambda fan_in: 1.0 / np.sqrt(fan_in)
        return {'x': jax.random.normal(ks[0], (B, L, D), jnp.float32), 'gate_w': jax.random.normal(ks[1], (E, D), jnp.float32) * s(D), 'w_gate': jax.random.normal(ks[2], (E, D, H), jnp.float32) * s(D), 'w_up': jax.random.normal(ks[3], (E, D, H), jnp.float32) * s(D), 'w_down': jax.random.normal(ks[4], (E, H, D), jnp.float32) * s(H), 'sw_gate': jax.random.normal(ks[5], (D, H), jnp.float32) * s(D), 'sw_up': jax.random.normal(ks[6], (D, H), jnp.float32) * s(D), 'sw_down': jax.random.normal(ks[7], (H, D), jnp.float32) * s(H)}
    _L0_ffn_all = _L0_ffn_setup()
    _L0_ffn_in = {k: v for k, v in _L0_ffn_all.items() if k in ('gate_w', 'w_gate', 'w_up', 'w_down', 'sw_gate', 'sw_up', 'sw_down')}
    del _L0_ffn_all

    def _L1_xattn_setup():
        import jax, jax.numpy as jnp
        import numpy as np
        B, LQ, LK = (8, 256, 256)
        HIST_DIM, COMB_DIM, FUSION_DIM = (128, 128, 128)

        def _linear_params(key, in_dim, out_dim):
            k1, k2 = jax.random.split(key)
            bound = 1.0 / np.sqrt(in_dim)
            W = jax.random.uniform(k1, (out_dim, in_dim), jnp.float32, -bound, bound)
            b = jax.random.uniform(k2, (out_dim,), jnp.float32, -bound, bound)
            return (W, b)

        def _lin(x, W, b):
            return jnp.einsum('bld,fd->blf', x, W) + b
        key = jax.random.key(seed)
        ks = jax.random.split(key, 8)
        hW, hb = _linear_params(ks[0], HIST_DIM, FUSION_DIM)
        cW, cb = _linear_params(ks[1], COMB_DIM, FUSION_DIM)
        qW, qb = _linear_params(ks[2], FUSION_DIM, FUSION_DIM)
        kW, kb = _linear_params(ks[3], FUSION_DIM, FUSION_DIM)
        vW, vb = _linear_params(ks[4], FUSION_DIM, FUSION_DIM)
        oW, ob = _linear_params(ks[5], FUSION_DIM, FUSION_DIM)
        return {'history_features': jax.random.normal(ks[6], (B, LQ, HIST_DIM), jnp.float32), 'combined_features': jax.random.normal(ks[7], (B, LK, COMB_DIM), jnp.float32), 'hW': hW, 'hb': hb, 'cW': cW, 'cb': cb, 'qW': qW, 'qb': qb, 'kW': kW, 'kb': kb, 'vW': vW, 'vb': vb, 'oW': oW, 'ob': ob}
    _L1_xattn_all = _L1_xattn_setup()
    _L1_xattn_in = {k: v for k, v in _L1_xattn_all.items() if k in ('hW', 'hb', 'cW', 'cb', 'qW', 'qb', 'kW', 'kb', 'vW', 'vb', 'oW', 'ob')}
    del _L1_xattn_all

    def _L1_ffn_setup():
        import jax, jax.numpy as jnp
        import numpy as np
        EPS = 1e-08

        def _ste(x, q):
            return x + jax.lax.stop_gradient(q - x)

        def quant_act_uint8(x):
            s = jax.lax.stop_gradient(jnp.maximum(jnp.max(x), EPS)) / 255.0
            q = jnp.clip(jnp.round(x / s), 0.0, 255.0) * s
            return (_ste(x, q), s)

        def quant_weight_int8_perchannel(w):
            s = jax.lax.stop_gradient(jnp.maximum(jnp.max(jnp.abs(w), axis=1, keepdims=True), EPS)) / 127.0
            q = jnp.clip(jnp.round(w / s), -128.0, 127.0) * s
            return (_ste(w, q), s[:, 0])

        def quant_bias_int32(b, s_in, s_w):
            s = jax.lax.stop_gradient(s_in * s_w)
            q = jnp.round(b / s) * s
            return _ste(b, q)

        def quant_linear(x, w, b):
            xq, s_in = quant_act_uint8(x)
            wq, s_w = quant_weight_int8_perchannel(w)
            bq = quant_bias_int32(b, s_in, s_w)
            return jnp.einsum('btd,fd->btf', xq, wq) + bq
        key = jax.random.key(seed)
        k1, k2, k3, k4, k5 = jax.random.split(key, 5)
        B, S, D, F = (4, 256, 128, 512)
        return {'x': jax.random.normal(k1, (B, S, D), dtype=jnp.float32), 'w1': jax.random.normal(k2, (F, D), dtype=jnp.float32) * (1.0 / np.sqrt(D)), 'b1': jax.random.normal(k3, (F,), dtype=jnp.float32) * 0.01, 'w2': jax.random.normal(k4, (D, F), dtype=jnp.float32) * (1.0 / np.sqrt(F)), 'b2': jax.random.normal(k5, (D,), dtype=jnp.float32) * 0.01}
    _L1_ffn_all = _L1_ffn_setup()
    _L1_ffn_in = {k: v for k, v in _L1_ffn_all.items() if k in ('w1', 'b1', 'w2', 'b2')}
    del _L1_ffn_all

    def _L2_xattn_setup():
        import jax, jax.numpy as jnp
        import numpy as np
        EMBED_DIM = 128
        NUM_HEADS = 16
        HEAD_DIM = EMBED_DIM // NUM_HEADS
        B, T_Q, T_K = (2, 256, 256)
        key = jax.random.key(seed)
        ks = jax.random.split(key, 11)
        s = 1.0 / np.sqrt(EMBED_DIM)
        return {'query': jax.random.normal(ks[0], (B, T_Q, EMBED_DIM), jnp.float32), 'key': jax.random.normal(ks[1], (B, T_K, EMBED_DIM), jnp.float32), 'value': jax.random.normal(ks[2], (B, T_K, EMBED_DIM), jnp.float32), 'Wq': jax.random.normal(ks[3], (EMBED_DIM, EMBED_DIM), jnp.float32) * s, 'bq': jnp.zeros((EMBED_DIM,), jnp.float32), 'Wk': jax.random.normal(ks[4], (EMBED_DIM, EMBED_DIM), jnp.float32) * s, 'bk': jnp.zeros((EMBED_DIM,), jnp.float32), 'Wv': jax.random.normal(ks[5], (EMBED_DIM, EMBED_DIM), jnp.float32) * s, 'bv': jnp.zeros((EMBED_DIM,), jnp.float32), 'Wo': jax.random.normal(ks[6], (EMBED_DIM, EMBED_DIM), jnp.float32) * s, 'bo': jnp.zeros((EMBED_DIM,), jnp.float32)}
    _L2_xattn_all = _L2_xattn_setup()
    _L2_xattn_in = {k: v for k, v in _L2_xattn_all.items() if k in ('Wq', 'bq', 'Wk', 'bk', 'Wv', 'bv', 'Wo', 'bo')}
    del _L2_xattn_all

    def _L2_ffn_setup():
        import jax, jax.numpy as jnp
        import numpy as np
        DIM = 128

        def _reference_tuple_inner(x, W_r, W_k, W_v, mu_r, mu_k):
            B, T, C = x.shape
            x_prev = jnp.concatenate([jnp.zeros((B, 1, C), x.dtype), x[:, :-1, :]], axis=1)
            xr = mu_r * x + (1.0 - mu_r) * x_prev
            xk = mu_k * x + (1.0 - mu_k) * x_prev
            r = jax.nn.sigmoid(jnp.einsum('btc,dc->btd', xr, W_r))
            k = jnp.einsum('btc,dc->btd', xk, W_k)
            k_act = jnp.square(jax.nn.relu(k))
            out = r * jnp.einsum('btc,dc->btd', k_act, W_v)
            new_state = x[:, -1, :]
            return (out, new_state)
        key = jax.random.key(seed)
        ks = jax.random.split(key, 6)
        B, T, C = (8, 256, DIM)
        x = jax.random.normal(ks[0], (B, T, C), dtype=jnp.float32)
        s = 1.0 / np.sqrt(C)
        W_r = jax.random.uniform(ks[1], (C, C), jnp.float32, -s, s)
        W_k = jax.random.uniform(ks[2], (C, C), jnp.float32, -s, s)
        W_v = jax.random.uniform(ks[3], (C, C), jnp.float32, -s, s)
        mu_r = jax.random.uniform(ks[4], (C,), jnp.float32)
        mu_k = jax.random.uniform(ks[5], (C,), jnp.float32)
        return {'x': x, 'W_r': W_r, 'W_k': W_k, 'W_v': W_v, 'mu_r': mu_r, 'mu_k': mu_k}
    _L2_ffn_all = _L2_ffn_setup()
    _L2_ffn_in = {k: v for k, v in _L2_ffn_all.items() if k in ('W_r', 'W_k', 'W_v', 'mu_r', 'mu_k')}
    del _L2_ffn_all

    def _L3_xattn_setup():
        import jax, jax.numpy as jnp
        import numpy as np
        DIM = 128
        NUM_HEADS = 8
        SCALE = (DIM // NUM_HEADS) ** (-0.5)
        key = jax.random.key(seed)
        ks = jax.random.split(key, 7)
        B, N, C = (4, 256, DIM)
        s = C ** (-0.5)
        return {'m_q': jax.random.normal(ks[0], (B, N, C), jnp.float32), 'm_kv': jax.random.normal(ks[1], (B, N, C), jnp.float32), 'Wq': jax.random.normal(ks[2], (C, C), jnp.float32) * s, 'Wk': jax.random.normal(ks[3], (C, C), jnp.float32) * s, 'Wv': jax.random.normal(ks[4], (C, C), jnp.float32) * s, 'Wp': jax.random.normal(ks[5], (C, C), jnp.float32) * s, 'bp': jax.random.normal(ks[6], (C,), jnp.float32) * 0.01}
    _L3_xattn_all = _L3_xattn_setup()
    _L3_xattn_in = {k: v for k, v in _L3_xattn_all.items() if k in ('Wq', 'Wk', 'Wv', 'Wp', 'bp')}
    del _L3_xattn_all

    def _L3_ffn_setup():
        import jax, jax.numpy as jnp
        import numpy as np
        B, N, D = (4, 256, 128)
        SPARSITY = 0.01
        key = jax.random.key(seed)
        k1, k2, k3 = jax.random.split(key, 3)
        x = jax.random.normal(k1, (B, N, D), dtype=jnp.float32)
        spatial = jax.random.normal(k2, (D, D), dtype=jnp.float32) * 0.02
        freq = jnp.fft.fft(spatial, axis=-1)
        k = int(D * SPARSITY)
        mag = jnp.abs(freq)
        kth = jax.lax.top_k(mag, k)[0][:, -1:]
        w_sparse = jnp.where(mag >= kth, freq, 0.0 + 0j)
        bias = jax.random.normal(k3, (D,), dtype=jnp.float32) * 0.01
        return {'x': x, 'w_freq_real': jnp.real(w_sparse).astype(jnp.float32), 'w_freq_imag': jnp.imag(w_sparse).astype(jnp.float32), 'bias': bias}
    _L3_ffn_all = _L3_ffn_setup()
    _L3_ffn_in = {k: v for k, v in _L3_ffn_all.items() if k in ('w_freq_real', 'w_freq_imag', 'bias')}
    del _L3_ffn_all
    return {'x': x, 'ctx_1024': ctx_1024, 'g_xattn': g_xattn, 'g_ffn': g_ffn, 'L0_xattn_Wq': _L0_xattn_in['Wq'], 'L0_xattn_bq': _L0_xattn_in['bq'], 'L0_xattn_Wk': _L0_xattn_in['Wk'], 'L0_xattn_bk': _L0_xattn_in['bk'], 'L0_xattn_Wv': _L0_xattn_in['Wv'], 'L0_xattn_bv': _L0_xattn_in['bv'], 'L0_xattn_Wo': _L0_xattn_in['Wo'], 'L0_xattn_bo': _L0_xattn_in['bo'], 'L0_ffn_gate_w': _L0_ffn_in['gate_w'], 'L0_ffn_w_gate': _L0_ffn_in['w_gate'], 'L0_ffn_w_up': _L0_ffn_in['w_up'], 'L0_ffn_w_down': _L0_ffn_in['w_down'], 'L0_ffn_sw_gate': _L0_ffn_in['sw_gate'], 'L0_ffn_sw_up': _L0_ffn_in['sw_up'], 'L0_ffn_sw_down': _L0_ffn_in['sw_down'], 'L1_xattn_hW': _L1_xattn_in['hW'], 'L1_xattn_hb': _L1_xattn_in['hb'], 'L1_xattn_cW': _L1_xattn_in['cW'], 'L1_xattn_cb': _L1_xattn_in['cb'], 'L1_xattn_qW': _L1_xattn_in['qW'], 'L1_xattn_qb': _L1_xattn_in['qb'], 'L1_xattn_kW': _L1_xattn_in['kW'], 'L1_xattn_kb': _L1_xattn_in['kb'], 'L1_xattn_vW': _L1_xattn_in['vW'], 'L1_xattn_vb': _L1_xattn_in['vb'], 'L1_xattn_oW': _L1_xattn_in['oW'], 'L1_xattn_ob': _L1_xattn_in['ob'], 'L1_ffn_w1': _L1_ffn_in['w1'], 'L1_ffn_b1': _L1_ffn_in['b1'], 'L1_ffn_w2': _L1_ffn_in['w2'], 'L1_ffn_b2': _L1_ffn_in['b2'], 'L2_xattn_Wq': _L2_xattn_in['Wq'], 'L2_xattn_bq': _L2_xattn_in['bq'], 'L2_xattn_Wk': _L2_xattn_in['Wk'], 'L2_xattn_bk': _L2_xattn_in['bk'], 'L2_xattn_Wv': _L2_xattn_in['Wv'], 'L2_xattn_bv': _L2_xattn_in['bv'], 'L2_xattn_Wo': _L2_xattn_in['Wo'], 'L2_xattn_bo': _L2_xattn_in['bo'], 'L2_ffn_W_r': _L2_ffn_in['W_r'], 'L2_ffn_W_k': _L2_ffn_in['W_k'], 'L2_ffn_W_v': _L2_ffn_in['W_v'], 'L2_ffn_mu_r': _L2_ffn_in['mu_r'], 'L2_ffn_mu_k': _L2_ffn_in['mu_k'], 'L3_xattn_Wq': _L3_xattn_in['Wq'], 'L3_xattn_Wk': _L3_xattn_in['Wk'], 'L3_xattn_Wv': _L3_xattn_in['Wv'], 'L3_xattn_Wp': _L3_xattn_in['Wp'], 'L3_xattn_bp': _L3_xattn_in['bp'], 'L3_ffn_w_freq_real': _L3_ffn_in['w_freq_real'], 'L3_ffn_w_freq_imag': _L3_ffn_in['w_freq_imag'], 'L3_ffn_bias': _L3_ffn_in['bias']}

def reference(x, ctx_1024, g_xattn, g_ffn, L0_xattn_Wq, L0_xattn_bq, L0_xattn_Wk, L0_xattn_bk, L0_xattn_Wv, L0_xattn_bv, L0_xattn_Wo, L0_xattn_bo, L0_ffn_gate_w, L0_ffn_w_gate, L0_ffn_w_up, L0_ffn_w_down, L0_ffn_sw_gate, L0_ffn_sw_up, L0_ffn_sw_down, L1_xattn_hW, L1_xattn_hb, L1_xattn_cW, L1_xattn_cb, L1_xattn_qW, L1_xattn_qb, L1_xattn_kW, L1_xattn_kb, L1_xattn_vW, L1_xattn_vb, L1_xattn_oW, L1_xattn_ob, L1_ffn_w1, L1_ffn_b1, L1_ffn_w2, L1_ffn_b2, L2_xattn_Wq, L2_xattn_bq, L2_xattn_Wk, L2_xattn_bk, L2_xattn_Wv, L2_xattn_bv, L2_xattn_Wo, L2_xattn_bo, L2_ffn_W_r, L2_ffn_W_k, L2_ffn_W_v, L2_ffn_mu_r, L2_ffn_mu_k, L3_xattn_Wq, L3_xattn_Wk, L3_xattn_Wv, L3_xattn_Wp, L3_xattn_bp, L3_ffn_w_freq_real, L3_ffn_w_freq_imag, L3_ffn_bias):
    import jax
    import jax.numpy as jnp

    def _L0_xattn_ref(q, k, v, Wq, bq, Wk, bk, Wv, bv, Wo, bo):
        import jax, jax.numpy as jnp
        import numpy as np
        D_MODEL = 128
        HEADS = 16
        D_K = D_MODEL // HEADS
        B, S = (2, 256)
        bs = q.shape[0]

        def proj(x, W, b):
            y = x @ W.T + b
            return y.reshape(bs, -1, HEADS, D_K).transpose(0, 2, 1, 3)
        qh = proj(q, Wq, bq)
        kh = proj(k, Wk, bk)
        vh = proj(v, Wv, bv)
        scores = jnp.einsum('bhqd,bhkd->bhqk', qh, kh) / jnp.sqrt(jnp.asarray(D_K, jnp.float32))
        attn = jax.nn.softmax(scores, axis=-1)
        out = jnp.einsum('bhqk,bhkd->bhqd', attn, vh)
        concat = out.transpose(0, 2, 1, 3).reshape(bs, -1, D_MODEL)
        return concat @ Wo.T + bo

    def _L0_ffn_ref(x, gate_w, w_gate, w_up, w_down, sw_gate, sw_up, sw_down):
        import jax, jax.numpy as jnp
        import numpy as np
        B, L, D = (4, 128, 128)
        E, H, K = (16, 64, 8)
        EPS = 1e-12

        def _l2norm(v, axis=-1):
            n = jnp.sqrt(jnp.sum(v * v, axis=axis, keepdims=True))
            return v / jnp.maximum(n, EPS)
        if __name__ == '__main__':
            out = reference(**setup_inputs())
            print(out.shape)
        b, l, d = x.shape
        xf = x.reshape(-1, d)
        logits = _l2norm(xf) @ _l2norm(gate_w).T
        scores = jax.nn.sigmoid(logits)
        topk_scores, topk_idx = jax.lax.top_k(scores, K)
        topk_w = topk_scores / jnp.sum(topk_scores, axis=-1, keepdims=True)
        combine = jnp.sum(jax.nn.one_hot(topk_idx, E, dtype=xf.dtype) * topk_w[..., None], axis=1)
        g = jnp.einsum('nd,edh->neh', xf, w_gate)
        u = jnp.einsum('nd,edh->neh', xf, w_up)
        y = jnp.einsum('neh,ehd->ned', jax.nn.silu(g) * u, w_down)
        routed = jnp.einsum('ned,ne->nd', y, combine)
        shared = jax.nn.silu(xf @ sw_gate) * (xf @ sw_up) @ sw_down
        return (routed + shared).reshape(b, l, d)

    def _L1_xattn_ref(history_features, combined_features, hW, hb, cW, cb, qW, qb, kW, kb, vW, vb, oW, ob):
        import jax, jax.numpy as jnp
        import numpy as np
        B, LQ, LK = (8, 256, 256)
        HIST_DIM, COMB_DIM, FUSION_DIM = (128, 128, 128)

        def _linear_params(key, in_dim, out_dim):
            k1, k2 = jax.random.split(key)
            bound = 1.0 / np.sqrt(in_dim)
            W = jax.random.uniform(k1, (out_dim, in_dim), jnp.float32, -bound, bound)
            b = jax.random.uniform(k2, (out_dim,), jnp.float32, -bound, bound)
            return (W, b)

        def _lin(x, W, b):
            return jnp.einsum('bld,fd->blf', x, W) + b
        h = _lin(history_features, hW, hb)
        c = _lin(combined_features, cW, cb)
        q = _lin(h, qW, qb)
        k = _lin(c, kW, kb)
        v = _lin(c, vW, vb)
        scale = 1.0 / jnp.sqrt(jnp.float32(FUSION_DIM))
        scores = jnp.einsum('bqf,bkf->bqk', q, k) * scale
        attn = jax.nn.softmax(scores, axis=-1)
        attn_out = jnp.einsum('bqk,bkf->bqf', attn, v)
        return _lin(attn_out + q, oW, ob)

    def _L1_ffn_ref(x, w1, b1, w2, b2):
        import jax, jax.numpy as jnp
        import numpy as np
        EPS = 1e-08

        def _ste(x, q):
            return x + jax.lax.stop_gradient(q - x)

        def quant_act_uint8(x):
            s = jax.lax.stop_gradient(jnp.maximum(jnp.max(x), EPS)) / 255.0
            q = jnp.clip(jnp.round(x / s), 0.0, 255.0) * s
            return (_ste(x, q), s)

        def quant_weight_int8_perchannel(w):
            s = jax.lax.stop_gradient(jnp.maximum(jnp.max(jnp.abs(w), axis=1, keepdims=True), EPS)) / 127.0
            q = jnp.clip(jnp.round(w / s), -128.0, 127.0) * s
            return (_ste(w, q), s[:, 0])

        def quant_bias_int32(b, s_in, s_w):
            s = jax.lax.stop_gradient(s_in * s_w)
            q = jnp.round(b / s) * s
            return _ste(b, q)

        def quant_linear(x, w, b):
            xq, s_in = quant_act_uint8(x)
            wq, s_w = quant_weight_int8_perchannel(w)
            bq = quant_bias_int32(b, s_in, s_w)
            return jnp.einsum('btd,fd->btf', xq, wq) + bq
        h = jax.nn.relu(quant_linear(x, w1, b1))
        return quant_linear(h, w2, b2)

    def _L2_xattn_ref(query, key, value, Wq, bq, Wk, bk, Wv, bv, Wo, bo):
        import jax, jax.numpy as jnp
        import numpy as np
        EMBED_DIM = 128
        NUM_HEADS = 16
        HEAD_DIM = EMBED_DIM // NUM_HEADS
        B, T_Q, T_K = (2, 256, 256)
        b, tq, _ = query.shape
        tk = key.shape[1]
        q = (query @ Wq.T + bq).reshape(b, tq, NUM_HEADS, HEAD_DIM).transpose(0, 2, 1, 3)
        k = (key @ Wk.T + bk).reshape(b, tk, NUM_HEADS, HEAD_DIM).transpose(0, 2, 1, 3)
        v = (value @ Wv.T + bv).reshape(b, tk, NUM_HEADS, HEAD_DIM).transpose(0, 2, 1, 3)
        scores = jnp.einsum('bhqd,bhkd->bhqk', q, k) / np.sqrt(HEAD_DIM)
        attn = jax.nn.softmax(scores, axis=-1)
        attn = jnp.nan_to_num(attn, nan=0.0)
        out = jnp.einsum('bhqk,bhkd->bhqd', attn, v)
        out = out.transpose(0, 2, 1, 3).reshape(b, tq, EMBED_DIM)
        return out @ Wo.T + bo

    def _L2_ffn_ref(x, W_r, W_k, W_v, mu_r, mu_k):
        import jax, jax.numpy as jnp
        import numpy as np
        DIM = 128

        def _reference_tuple_inner(x, W_r, W_k, W_v, mu_r, mu_k):
            B, T, C = x.shape
            x_prev = jnp.concatenate([jnp.zeros((B, 1, C), x.dtype), x[:, :-1, :]], axis=1)
            xr = mu_r * x + (1.0 - mu_r) * x_prev
            xk = mu_k * x + (1.0 - mu_k) * x_prev
            r = jax.nn.sigmoid(jnp.einsum('btc,dc->btd', xr, W_r))
            k = jnp.einsum('btc,dc->btd', xk, W_k)
            k_act = jnp.square(jax.nn.relu(k))
            out = r * jnp.einsum('btc,dc->btd', k_act, W_v)
            new_state = x[:, -1, :]
            return (out, new_state)
        return _reference_tuple_inner(x, W_r, W_k, W_v, mu_r, mu_k)[0]

    def _L3_xattn_ref(m_q, m_kv, Wq, Wk, Wv, Wp, bp):
        import jax, jax.numpy as jnp
        import numpy as np
        DIM = 128
        NUM_HEADS = 8
        SCALE = (DIM // NUM_HEADS) ** (-0.5)
        B, N, C = m_q.shape
        q = m_q @ Wq
        k = m_kv @ Wk
        v = m_kv @ Wv
        attn = jnp.einsum('bnc,bmc->bnm', q, k) * SCALE
        attn = jax.nn.softmax(attn, axis=-1)
        x = jnp.einsum('bnm,bmc->bnc', attn, v)
        x = jnp.swapaxes(x, 1, 2).reshape(B, N, C)
        return x @ Wp + bp

    def _L3_ffn_ref(x, w_freq_real, w_freq_imag, bias):
        import jax, jax.numpy as jnp
        import numpy as np
        B, N, D = (4, 256, 128)
        SPARSITY = 0.01
        w = jax.lax.complex(w_freq_real, w_freq_imag)
        x_freq = jnp.fft.fft(x, axis=-1)
        y_freq = jnp.einsum('bnd,do->bno', x_freq, w)
        y = jnp.real(jnp.fft.ifft(y_freq, axis=-1))
        return y + bias
    x = x + jnp.tanh(g_xattn[0]) * _L0_xattn_ref(_layernorm(x, axis=-1), ctx_1024, ctx_1024, L0_xattn_Wq, L0_xattn_bq, L0_xattn_Wk, L0_xattn_bk, L0_xattn_Wv, L0_xattn_bv, L0_xattn_Wo, L0_xattn_bo)
    x = x + jnp.tanh(g_ffn[0]) * _L0_ffn_ref(_layernorm(x, axis=-1), L0_ffn_gate_w, L0_ffn_w_gate, L0_ffn_w_up, L0_ffn_w_down, L0_ffn_sw_gate, L0_ffn_sw_up, L0_ffn_sw_down)
    x = x + jnp.tanh(g_xattn[1]) * _L1_xattn_ref(_layernorm(x, axis=-1), ctx_1024, L1_xattn_hW, L1_xattn_hb, L1_xattn_cW, L1_xattn_cb, L1_xattn_qW, L1_xattn_qb, L1_xattn_kW, L1_xattn_kb, L1_xattn_vW, L1_xattn_vb, L1_xattn_oW, L1_xattn_ob)
    x = x + jnp.tanh(g_ffn[1]) * _L1_ffn_ref(_layernorm(x, axis=-1), L1_ffn_w1, L1_ffn_b1, L1_ffn_w2, L1_ffn_b2)
    x = x + jnp.tanh(g_xattn[2]) * _L2_xattn_ref(_layernorm(x, axis=-1), ctx_1024, ctx_1024, L2_xattn_Wq, L2_xattn_bq, L2_xattn_Wk, L2_xattn_bk, L2_xattn_Wv, L2_xattn_bv, L2_xattn_Wo, L2_xattn_bo)
    x = x + jnp.tanh(g_ffn[2]) * _L2_ffn_ref(_layernorm(x, axis=-1), L2_ffn_W_r, L2_ffn_W_k, L2_ffn_W_v, L2_ffn_mu_r, L2_ffn_mu_k)
    x = x + jnp.tanh(g_xattn[3]) * _L3_xattn_ref(_layernorm(x, axis=-1), ctx_1024, L3_xattn_Wq, L3_xattn_Wk, L3_xattn_Wv, L3_xattn_Wp, L3_xattn_bp)
    x = x + jnp.tanh(g_ffn[3]) * _L3_ffn_ref(_layernorm(x, axis=-1), L3_ffn_w_freq_real, L3_ffn_w_freq_imag, L3_ffn_bias)
    return x

_drawn_inputs = setup_inputs


def setup_inputs(seed=0):
    import zlib

    import numpy as np

    out = dict(_drawn_inputs(seed))
    spreads = {'L0_xattn_bq': (0.0, 0.302),
     'L0_xattn_bk': (0.0, 2.0),
     'L0_xattn_bv': (0.0, 0.1),
     'L0_xattn_bo': (0.0, 0.1),
     'L2_xattn_bq': (0.0, 0.558),
     'L2_xattn_bk': (0.0, 2.0),
     'L2_xattn_bv': (0.0, 0.1),
     'L2_xattn_bo': (0.0, 0.1)}
    factors = {'g_ffn': 24.936,
     'L1_xattn_hb': 4.431,
     'L1_xattn_cb': 4.25,
     'L1_xattn_kW': 8.0,
     'L1_xattn_kb': 64.0,
     'L1_ffn_b1': 8.0,
     'L1_ffn_b2': 7.173,
     'L2_ffn_W_r': 4.566,
     'L2_ffn_mu_r': 8.0,
     'L3_xattn_bp': 8.0,
     'L3_ffn_bias': 8.0}
    for name, (base, spread) in spreads.items():
        noise = np.random.default_rng([zlib.crc32(name.encode()), seed]).standard_normal(out[name].shape)
        drawn = base * np.exp(spread * noise) if base else spread * noise
        out[name] = jnp.asarray(drawn.astype(out[name].dtype))
    for name, factor in factors.items():
        out[name] = (out[name] * factor).astype(out[name].dtype)
    return out
```

```python
from contextlib import ExitStack

import concourse.bass as bass
from concourse import mybir

F32 = mybir.dt.float32
BF16 = mybir.dt.bfloat16
ALU = mybir.AluOpType
ACT = mybir.ActivationFunctionType
AX = mybir.AxisListType
MAX_OVER_PARTITIONS = bass.bass_isa.ReduceOp.max

B = 32
T = 128
D = 128
LN_EPS = 1e-5
ATT_BUFS = 4
GB = 4
GROUPS = B // GB
GT = GB * T


class Slot:

    def __init__(self, loop, fixed, total=B, bufs=ATT_BUFS):
        self.loop, self.fixed, self.total, self.bufs = loop, fixed, total, bufs

    def count(self):
        return self.fixed if self.loop is None else self.loop * self.bufs + self.fixed

    def batch(self, lag):
        c = self.fixed - lag
        return c if self.loop is None else self.loop * self.bufs + c

    def turn(self, lag):
        c = (self.fixed - lag) // self.bufs
        return c if self.loop is None else self.loop + c

    def buf(self, lag):
        return (self.fixed - lag) % self.bufs

    def live(self, lag):
        return self.loop is not None or 0 <= self.fixed - lag < self.total


def run_slots(eng, step, lags, peel, total=B, bufs=ATT_BUFS):
    for it in range(peel):
        step(Slot(None, it, total, bufs))
    with eng.Fori(0, (total - peel) // bufs) as i:
        for u in range(bufs):
            step(Slot(i, peel + u, total, bufs))
    for it in range(total, total + lags):
        step(Slot(None, it, total, bufs))


def reach(eng, sem, value):
    if not isinstance(value, int) or value > 0:
        eng.wait_ge(sem, value)


def reach_carried(eng, sem, value, scratch):
    reach(eng, sem, value)
    if not isinstance(value, int):
        eng.tensor_tensor(scratch, scratch, scratch, ALU.mult)


def many_head_attention(nc, tag, g, x, stats, mean, rstd, tg, ctx_t, w):
    H, DK = 16, 8
    PAIRS = H // 2
    SCALE = float(DK) ** -0.5
    LAGS = 8
    with ExitStack() as ctx:
        def sb(name, shape, dt=F32):
            return ctx.enter_context(nc.sbuf_tensor(f"{tag}_{name}", shape, dt))

        def sem(name):
            return ctx.enter_context(nc.semaphore(f"{tag}_{name}"))

        R = range(ATT_BUFS)
        xn = [sb(f"xn{i}", [T, D]) for i in R]
        xn_t = [sb(f"xn_t{i}", [D, T]) for i in R]
        ctx_b = [sb(f"ctx_b{i}", [D, T]) for i in R]
        qk = [sb(f"qk{i}", [T, 2, H, DK]) for i in R]
        rest = [sb(f"rest{i}", [T, 2, H, DK]) for i in R]
        parts = [sb(f"parts{i}", [T, 2 * H, 64], BF16) for i in R]
        parts_t = [sb(f"parts_t{i}", [128, 2, PAIRS, T], BF16) for i in R]
        v_aug = [sb(f"v_aug{i}", [T, H, 32]) for i in R]
        rowmax = [sb(f"rowmax{i}", [T, 2, PAIRS]) for i in R]
        maxrest = [sb(f"maxrest{i}", [T, 2, PAIRS]) for i in R]
        negmax = [sb(f"negmax{i}", [T, 2, 64], BF16) for i in R]
        negmax_t = [sb(f"negmax_t{i}", [128, T], BF16) for i in R]
        probs = [sb(f"probs{i}", [T, 2, 4, T]) for i in range(2)]
        out_h = [sb(f"out_h{i}", [128, 4, T]) for i in R]
        rden = [sb(f"rden{i}", [T, H]) for i in R]
        out_n = [sb(f"out_n{i}", [T, H, DK]) for i in R]
        out_t = [sb(f"out_t{i}", [D, T]) for i in R]
        ys = [sb(f"ys{i}", [T, D]) for i in range(2)]
        zeros = sb("zeros", [128, 2, H, DK])
        biases = sb("biases", [128, 3, D], BF16)

        ctx_in = [sem(f"ctx_in{i}") for i in R]
        q_turned, q_taken, k_turned, k_taken = sem("q_turned"), sem("q_taken"), sem("k_turned"), sem("k_taken")
        xn_ready, turned, turn_taken = sem("xn_ready"), sem("turned"), sem("turn_taken")
        mapped, mapped_taken, qk_ready = sem("mapped"), sem("mapped_taken"), sem("qk_ready")
        cut_step, parts_ready = sem("cut_step"), sem("parts_ready")
        s_ready, max_ready = sem("s_ready"), sem("max_ready")
        neg_step, negmax_rest, negmax_ready = sem("neg_step"), sem("negmax_rest"), sem("negmax_ready")
        e_ready, probs_ready, pv_done = sem("e_ready"), sem("probs_ready"), sem("pv_done")
        out_h_ready, o2_ready, v_ready = sem("out_h_ready"), sem("o2_ready"), sem("v_ready")
        rden_ready, out_n_ready = sem("rden_ready"), sem("out_n_ready")
        y_taken, x_ready, stats_ready = sem("y_taken"), sem("x_ready"), sem("stats_ready")

        ident, ones_bf, pick = g["ident"], g["ones_bf"], g["pick"]
        ident_bf = g["ident_bf"]

        bias_parts(nc, f"{tag}_bias", g, [[(w["bq"], ident[:])], [(w["bk"], ident[:])],
                                          [(w["bv"], w["wo_t"]), (w["bo"], ident[:])]], biases[:])
        with nc.Block() as block:
            @block.gpsimd
            def _(pool):
                for i in R:
                    pool.memset(parts[i][:], 0.0)
                    pool.memset(negmax[i][:], 0.0)
                    pool.memset(v_aug[i][:, :, DK + 1:32], 0.0)
                    pool.memset(v_aug[i][:, :, DK:DK + 1], 1.0)
                pool.memset(zeros[:], 0.0)

        ps_s = ctx.enter_context(nc.psum_tensor(f"{tag}_ps_s", [128, 2, 4, 128], F32))
        ps_e = ctx.enter_context(nc.psum_tensor(f"{tag}_ps_e", [128, 2, 4, 128], F32))
        ps_o = ctx.enter_context(nc.psum_tensor(f"{tag}_ps_o", [128, 4, 128], F32))
        ps_q = ctx.enter_context(nc.psum_tensor(f"{tag}_ps_q", [128, PAIRS, 128], BF16))
        ps_t = ctx.enter_context(nc.psum_tensor(f"{tag}_ps_t", [128, 512], F32))
        ps_p = ctx.enter_context(nc.psum_tensor(f"{tag}_ps_p", [128, 512], F32))

        with nc.Block() as block:
            @block.sync
            def _(sp):
                def step(it):
                    if it.live(0):
                        n, b = it.batch(0), it.buf(0)
                        if it.loop is not None or n >= ATT_BUFS:
                            reach(sp, mapped, n)
                        sp.dma_start(ctx_b[b][:], ctx_t[n]).then_inc(ctx_in[b], 16)

                run_slots(sp, step, LAGS, 8)

            @block.vector
            def _(dve):
                def step(it):
                    def row_maxima(half):
                        if it.live(3):
                            n, b = it.batch(3), it.buf(3)
                            reach(dve, s_ready, 2 * n + half + 1)
                            if half == 0:
                                reach(dve, negmax_ready, n - ATT_BUFS + 1)
                            dve.tensor_reduce(rowmax[b][:, :, 4 * half:4 * half + 4], ps_s[:], AX.X,
                                              ALU.max).then_inc(max_ready, 1)

                    row_maxima(0)
                    if it.live(0):
                        n, b = it.batch(0), it.buf(0)
                        reach(dve, turned, n - ATT_BUFS + 1)
                        dve.tensor_scalar(xn[b][:], x[:, n, :], mean[:, bass.ds(n, 1)], rstd[:, bass.ds(n, 1)],
                                          ALU.subtract, ALU.mult).then_inc(xn_ready, 1)
                    if it.live(6):
                        n, b = it.batch(6), it.buf(6)
                        reach(dve, o2_ready, n + 1)
                        o2 = ps_o[:].rearrange("p c (h r) -> p (c h) r", r=32)
                        dve.reciprocal(rden[b][:], o2[:, :, DK]).then_inc(rden_ready, 1)
                        if it.loop is not None or n >= ATT_BUFS:
                            reach(dve, turned, n + 7 - ATT_BUFS)
                        reach(dve, rden_ready, n + 1)
                        dve.tensor_tensor(out_n[b][:], o2[:, :, 0:DK],
                                          rden[b][:].unsqueeze(2).to_broadcast([T, H, DK]),
                                          ALU.mult).then_inc(out_n_ready, 1)
                    row_maxima(1)
                    if it.live(2):
                        n, b = it.batch(2), it.buf(2)
                        reach(dve, k_turned, n + 1)
                        dve.tensor_copy(parts_t[b][:, 1], ps_q[:]).then_inc(k_taken, 1)
                    if it.live(8):
                        n = it.batch(8)
                        reach(dve, x_ready, n + 1)
                        dve.bn_stats(stats[:, n, :], x[:, n, :]).then_inc(stats_ready, 1)

                run_slots(dve, step, LAGS, 8)

            @block.gpsimd
            def _(pool):
                def step(it):
                    if it.live(4):
                        n, b = it.batch(4), it.buf(4)
                        neg, m, r = negmax[b], rowmax[b], maxrest[b]
                        zero = zeros[:, :, 0]
                        reach(pool, max_ready, 2 * n + 2)
                        if it.loop is not None or n >= ATT_BUFS:
                            reach(pool, turned, n + 5 - ATT_BUFS)
                        pool.tensor_tensor(neg[:, :, 0:8], zero, m[:], ALU.subtract).then_inc(neg_step, 1)
                        reach(pool, neg_step, 3 * n + 1)
                        pool.tensor_tensor(r[:], m[:], neg[:, :, 0:8], ALU.add).then_inc(neg_step, 1)
                        reach(pool, neg_step, 3 * n + 2)
                        pool.tensor_tensor(neg[:, :, 8:16], zero, r[:], ALU.subtract).then_inc(neg_step, 1)
                        reach(pool, neg_step, 3 * n + 3)
                        pool.tensor_tensor(r[:], r[:], neg[:, :, 8:16], ALU.add).then_inc(negmax_rest, 1)
                        reach(pool, negmax_rest, n + 1)
                        pool.tensor_tensor(neg[:, :, 16:24], zero, r[:], ALU.subtract).then_inc(negmax_ready, 1)
                    if it.live(7):
                        n = it.batch(7)
                        reach(pool, y_taken, n + 1)
                        pool.tensor_tensor(x[:, n, :], x[:, n, :], ys[it.buf(7) % 2][:], ALU.add).then_inc(x_ready, 1)
                    if it.live(1):
                        n, b = it.batch(1), it.buf(1)
                        st, f, r = parts[b], qk[b], rest[b]
                        flat = st[:].rearrange("t g r -> t (g r)")
                        k0 = flat[:, H * 64 - 16:2 * H * 64 - 16].rearrange("t (h r) -> t h r", r=64)
                        r2 = r[:].rearrange("t s h d -> t (s h) d")
                        reach(pool, qk_ready, n + 1)
                        pool.tensor_tensor(r2, f[:].rearrange("t s h d -> t (s h) d"), st[:, :, 0:DK],
                                           ALU.subtract).then_inc(cut_step, 1)
                        reach(pool, cut_step, 2 * n + 1)
                        pool.tensor_tensor(st[:, :, 24:32], r2, zeros[:].rearrange("t s h d -> t (s h) d"),
                                           ALU.add).then_inc(cut_step, 1)
                        pool.tensor_tensor(st[:, 0:H, 40:48], r[:, 0], zeros[:, 0], ALU.add)
                        pool.tensor_tensor(k0[:, :, 0:8], r[:, 1], zeros[:, 0], ALU.add)
                        reach(pool, cut_step, 2 * n + 2)
                        pool.tensor_tensor(st[:, 0:H, 32:40], r[:, 0], st[:, 0:H, 24:32], ALU.subtract)
                        pool.tensor_tensor(k0[:, :, 8:16], r[:, 1], st[:, H:2 * H, 24:32],
                                           ALU.subtract).then_inc(parts_ready, 1)

                run_slots(pool, step, LAGS, 8)

            @block.scalar
            def _(act):
                def step(it):
                    last = None
                    if it.live(1) or it.live(5) or it.live(7):
                        reach(act, turned, it.count())
                    if it.live(1):
                        last = act.activation(xn_t[it.buf(1)][:], ps_t[:, 0:T], ACT.Copy)
                    if it.live(7):
                        last = act.activation(out_t[it.buf(7)][:], ps_t[:, 256:384], ACT.Copy)
                    if it.live(5):
                        last = act.activation(negmax_t[it.buf(5)][:], ps_t[:, 128:192].bitcast(BF16), ACT.Copy)
                    if last is not None:
                        last.then_inc(turn_taken, 1)
                    if it.live(6):
                        n, b = it.batch(6), it.buf(6)
                        reach(act, pv_done, 2 * n + 2)
                        act.activation(out_h[b][:], ps_o[:], ACT.Copy).then_inc(out_h_ready, 1)
                    last = None
                    if it.live(1) or it.live(4) or it.live(7):
                        reach(act, mapped, it.count())
                    if it.live(1):
                        n, b = it.batch(1), it.buf(1)
                        reach(act, parts_ready, n - ATT_BUFS + 1)
                        q_and_k = ps_p[:, 0:2 * D]
                        act.activation(parts[b][:, :, 0:24].rearrange("t g (r d) -> t g r d", d=DK),
                                       q_and_k.rearrange("p (g d) -> p g d", d=DK).unsqueeze(2)
                                       .to_broadcast([T, 2 * H, 3, DK]), ACT.Copy)
                        last = act.activation(qk[b][:].rearrange("t s h d -> t (s h d)"), q_and_k, ACT.Copy)
                        last.then_inc(qk_ready, 1)
                    if it.live(4):
                        act.activation(v_aug[it.buf(4)][:, :, 0:DK],
                                       ps_p[:, 2 * D:3 * D].rearrange("p (h d) -> p h d", d=DK),
                                       ACT.Copy).then_inc(v_ready, 1)
                    if it.live(7):
                        n = it.batch(7)
                        reach(act, x_ready, n)
                        act.activation(ys[it.buf(7) % 2][:], ps_p[:, 3 * D:4 * D], ACT.Copy, scale=tg).then_inc(y_taken, 1)
                    for half in range(2):
                        if it.live(5):
                            n, b = it.batch(5), it.buf(5)
                            reach(act, e_ready, 2 * n + half + 1)
                            reach(act, pv_done, 2 * n + half - 1)
                            act.activation(probs[half][:], ps_e[:], ACT.Exp, scale=SCALE).then_inc(probs_ready, 1)
                        if half == 0 and it.live(2):
                            n, b = it.batch(2), it.buf(2)
                            reach(act, q_turned, n + 1)
                            act.activation(parts_t[b][:, 0], ps_q[:], ACT.Copy).then_inc(q_taken, 1)

                run_slots(act, step, LAGS, 8)

            @block.tensor
            def _(pe):
                def turn(it):
                    if it.live(1) or it.live(5) or it.live(7):
                        reach(pe, turn_taken, it.count() - 1)
                    last = None
                    if it.live(1):
                        reach(pe, xn_ready, it.batch(1) + 1)
                        last = pe.transpose(ps_t[:, 0:T], xn[it.buf(1)][:], ident[:])
                    if it.live(7):
                        reach(pe, out_n_ready, it.batch(7) + 1)
                        last = pe.transpose(ps_t[:, 256:384], out_n[it.buf(7)][:].rearrange("t h d -> t (h d)"),
                                            ident[:])
                    if it.live(5):
                        reach(pe, negmax_ready, it.batch(5) + 1)
                        last = pe.transpose(ps_t[:, 128:192].bitcast(BF16),
                                            negmax[it.buf(5)][:].rearrange("t a r -> t (a r)"), ident_bf[:])
                    if last is not None:
                        last.then_inc(turned, 1)

                def maps(it):
                    last = None
                    if it.live(1) or it.live(4) or it.live(7):
                        if it.live(1):
                            reach(pe, qk_ready, it.batch(1))
                        if it.live(4):
                            reach(pe, v_ready, it.batch(4))
                        if it.live(7):
                            reach(pe, y_taken, it.batch(7))
                        if it.live(1) or it.live(7):
                            reach(pe, turn_taken, it.count())
                    if it.live(4):
                        last = pe.matmul(ps_p[:, 2 * D:3 * D], ctx_b[it.buf(4)][:], w["wkv_t"][:, D:2 * D], start=True, stop=True)
                    if it.live(1):
                        b = it.buf(1)
                        pe.matmul(ps_p[:, 0:D], xn_t[b][:], w["wq_t"], start=True, stop=False)
                        pe.matmul(ps_p[:, 0:D], ones_bf[:], biases[:, 0], start=False, stop=True)
                        pe.wait_ge(ctx_in[b], 16 * (it.turn(1) + 1))
                        pe.matmul(ps_p[:, D:2 * D], ctx_b[b][:], w["wkv_t"][:, 0:D], start=True, stop=False)
                        last = pe.matmul(ps_p[:, D:2 * D], ones_bf[:], biases[:, 1], start=False, stop=True)
                    if it.live(7):
                        pe.matmul(ps_p[:, 3 * D:4 * D], out_t[it.buf(7)][:], w["wo_t"], start=True, stop=False)
                        last = pe.matmul(ps_p[:, 3 * D:4 * D], ones_bf[:], biases[:, 2], start=False, stop=True)
                    if last is not None:
                        last.then_inc(mapped, 1)

                def turn_parts(it, side):
                    if it.live(2):
                        n, b = it.batch(2), it.buf(2)
                        flat = parts[b][:].rearrange("t g r -> t (g r)")
                        if side == 0:
                            reach(pe, parts_ready, n + 1)
                            reach(pe, k_taken, n)
                        else:
                            reach(pe, q_taken, n + 1)
                        for p in range(PAIRS):
                            at = side * (H * 64 - 16) + 128 * p
                            last = pe.transpose(ps_q[:, p], flat[:, at:at + 128], ident_bf[:])
                        last.then_inc(k_turned if side else q_turned, 1)

                def scores(it, half):
                    if it.live(3):
                        n, b = it.batch(3), it.buf(3)
                        if half == 0:
                            reach(pe, k_taken, n + 1)
                        reach(pe, max_ready, 2 * n + half)
                        for j in range(4):
                            for a in range(2):
                                lo, p = 64 * a, 4 * half + j
                                last = pe.matmul(ps_s[:, a, j], parts_t[b][lo:lo + 48, 0, p],
                                                 parts_t[b][lo:lo + 48, 1, p], start=True, stop=True)
                        last.then_inc(s_ready, 1)

                def shifted(it, half):
                    if it.live(5):
                        n, b = it.batch(5), it.buf(5)
                        if half == 0:
                            reach(pe, turn_taken, it.count())
                        reach(pe, probs_ready, 2 * n + half)
                        for j in range(4):
                            p = 4 * half + j
                            for a in range(2):
                                lo = 64 * a
                                pe.matmul(ps_e[:, a, j], parts_t[b][lo:lo + 48, 1, p],
                                          parts_t[b][lo:lo + 48, 0, p], start=True, stop=False)
                            for a in range(2):
                                lo = 64 * a
                                last = pe.matmul(ps_e[:, a, j], pick[lo:lo + 48, p], negmax_t[b][lo:lo + 48],
                                                 start=False, stop=True)
                        last.then_inc(e_ready, 1)

                def values(it, half, lag):
                    if it.live(lag):
                        n, b = it.batch(lag), it.buf(lag)
                        if half == 0:
                            reach(pe, v_ready, n + 1)
                            reach(pe, out_n_ready, n)
                        reach(pe, probs_ready, 2 * n + half + 1)
                        for j in range(4):
                            for a in range(2):
                                h = 2 * (4 * half + j) + a
                                q = 32 * (h % 4)
                                last = pe.matmul(ps_o[q:q + 32, h // 4], v_aug[b][:, h], probs[half][:, a, j],
                                                 start=True, stop=True)
                        last.then_inc(pv_done, 1)

                def step(it):
                    turn(it)
                    scores(it, 0)
                    values(it, 1, 6)
                    maps(it)
                    shifted(it, 0)
                    turn_parts(it, 0)
                    if it.live(6):
                        n, b = it.batch(6), it.buf(6)
                        reach(pe, out_h_ready, n + 1)
                        for c in range(4):
                            last = pe.transpose(ps_o[:, c], out_h[b][:, c], ident[:])
                        last.then_inc(o2_ready, 1)
                    scores(it, 1)
                    values(it, 0, 5)
                    turn_parts(it, 1)
                    shifted(it, 1)

                run_slots(pe, step, LAGS, 8)


class Front:

    def __init__(self, nc, ctx, tag, g, x, mean, rstd):
        self.x, self.mean, self.rstd, self.ident = x, mean, rstd, g["ident"]
        self.rows = [ctx.enter_context(nc.sbuf_tensor(f"{tag}_rows{i}", [T, GB, D], F32)) for i in range(2)]
        self.ps = ctx.enter_context(nc.psum_tensor(f"{tag}_ps_rows", [D, GB, T], F32))
        self.rows_ready = ctx.enter_context(nc.semaphore(f"{tag}_rows_ready"))
        self.turned = ctx.enter_context(nc.semaphore(f"{tag}_rows_turned"))
        self.taken = ctx.enter_context(nc.semaphore(f"{tag}_rows_taken"))

    def normalise(self, dve, it):
        if it.live(0):
            n, b = it.batch(0), it.buf(0)
            reach(dve, self.turned, n - 1)
            for j in range(GB):
                last = dve.tensor_scalar(self.rows[b][:, j], self.x[:, n * GB + j, :],
                                         self.mean[:, bass.ds(n * GB + j, 1)], self.rstd[:, bass.ds(n * GB + j, 1)],
                                         ALU.subtract, ALU.mult)
            last.then_inc(self.rows_ready, 1)

    def turn(self, pe, it, taken=None):
        if it.live(1):
            n, b = it.batch(1), it.buf(1)
            reach(pe, taken or self.taken, n)
            reach(pe, self.rows_ready, n + 1)
            for j in range(GB):
                last = pe.transpose(self.ps[:, j], self.rows[b][:, j], self.ident[:])
            last.then_inc(self.turned, 1)


def bias_parts(nc, tag, g, columns, parts):
    n = len(columns)
    with ExitStack() as ctx:
        row = ctx.enter_context(nc.sbuf_tensor(f"{tag}_row", [128, n, D], F32))
        rest = ctx.enter_context(nc.sbuf_tensor(f"{tag}_rest", [128, n, D], F32))
        part_of = ctx.enter_context(nc.sbuf_tensor(f"{tag}_part", [128, n, D], BF16))
        ps = ctx.enter_context(nc.psum_tensor(f"{tag}_ps", [128, n, D], F32))
        made = ctx.enter_context(nc.semaphore(f"{tag}_made"))
        step = ctx.enter_context(nc.semaphore(f"{tag}_step"))
        with nc.Block() as block:
            @block.tensor
            def _(pe):
                for i, pairs in enumerate(columns):
                    for k, (column, rhs) in enumerate(pairs):
                        last = pe.matmul(ps[:, i], column.to_broadcast([128, 128]), rhs,
                                         start=(k == 0), stop=(k == len(pairs) - 1))
                last.then_inc(made, 1)

            @block.vector
            def _(dve):
                dve.wait_ge(made, 1)
                dve.tensor_copy(row[:], ps[:]).then_inc(step, 1)
                for part in range(3):
                    at = 1 + 4 * part
                    dve.wait_ge(step, at)
                    dve.tensor_copy(part_of[:], row[:]).then_inc(step, 1)
                    dve.wait_ge(step, at + 1)
                    dve.tensor_tensor(rest[:], row[:], part_of[:], ALU.subtract).then_inc(step, 1)
                    sel = g["ident"][:, part:part + 1]
                    if part == 0:
                        dve.tensor_scalar(parts, part_of[:], sel, None, ALU.mult).then_inc(step, 1)
                    else:
                        dve.scalar_tensor_tensor(parts, part_of[:], sel, parts, ALU.mult, ALU.add).then_inc(step, 1)
                    dve.wait_ge(step, at + 3)
                    dve.tensor_copy(row[:], rest[:]).then_inc(step, 1)


def mixture_of_experts(nc, tag, g, x, stats, mean, rstd, row_inv, tg, w, shared_down, gate_rows):
    E, HID, TILES = 16, 64, 9
    with ExitStack() as ctx:
        def sb(name, shape, dt=F32):
            return ctx.enter_context(nc.sbuf_tensor(f"{tag}_{name}", shape, dt))

        def ps(name, shape):
            return ctx.enter_context(nc.psum_tensor(f"{tag}_{name}", shape, F32))

        def sem(name):
            return ctx.enter_context(nc.semaphore(f"{tag}_{name}"))

        R = range(2)
        gate_t = sb("gate_t", [D, E])
        sd = sb("sd", [HID, D])
        spread = sb("spread", [128, 8, 128], BF16)
        gr, gsq, gn = sb("gr", [E, D]), sb("gsq", [E, D]), sb("gn", [E, 4])
        xs = [sb(f"xs{i}", [D, GB, T]) for i in R]
        z, th, sc, left = (sb(k, [T, GB, E]) for k in ("z", "th", "sc", "left"))
        top = sb("top", [T, GB, 8])
        cw, crest = sb("cw", [T, GB, E]), sb("crest", [T, GB, E])
        csum, cinv = sb("csum", [T, GB]), sb("cinv", [T, GB])
        cparts = sb("cparts", [T, GB, 128], BF16)
        cw_t = [sb(f"cw_t{i}", [128, GB, T], BF16) for i in R]
        silu = [sb(f"silu{i}", [128, GT]) for i in R]
        prod = [sb(f"prod{i}", [128, GT]) for i in R]
        hid = [sb(f"hid{i}", [128, GB, T]) for i in R]
        scratch_t = sb("scratch", [128, 1])
        scratch = scratch_t[:]

        gate_in, gate_step, gate_turned = sem("gate_in"), sem("gate_step"), sem("gate_turned")
        ps_gate = ctx.enter_context(nc.psum_tensor(f"{tag}_ps_gate", [D, 128], F32))

        with nc.Block() as block:
            @block.sync
            def _(sp):
                sp.dma_start(gr[:], gate_rows).then_inc(gate_in, 16)
                sp.dma_start(sd[:], shared_down).then_inc(gate_in, 16)
                sp.wait_ge(gate_in, 32)

            @block.vector
            def _(dve):
                dve.wait_ge(gate_in, 32)
                dve.tensor_tensor(gsq[:], gr[:], gr[:], ALU.mult).then_inc(gate_step, 1)
                dve.wait_ge(gate_step, 1)
                dve.tensor_reduce(gn[:, 0:1], gsq[:], AX.X, ALU.add).then_inc(gate_step, 1)
                dve.wait_ge(gate_step, 3)
                dve.tensor_scalar(gn[:, 1:2], gn[:, 1:2], 1e-12, None, ALU.max).then_inc(gate_step, 1)
                dve.wait_ge(gate_step, 4)
                dve.reciprocal(gn[:, 2:3], gn[:, 1:2]).then_inc(gate_step, 1)
                dve.wait_ge(gate_step, 5)
                dve.scalar_tensor_tensor(gn[:, 2:3], gn[:, 2:3], gn[:, 0:1], gn[:, 1:2], ALU.mult, ALU.add).then_inc(gate_step, 1)
                dve.wait_ge(gate_step, 6)
                dve.tensor_scalar(gn[:, 2:3], gn[:, 2:3], 0.5, 1e-12, ALU.mult, ALU.max).then_inc(gate_step, 1)
                dve.wait_ge(gate_step, 7)
                dve.reciprocal(gn[:, 3:4], gn[:, 2:3]).then_inc(gate_step, 1)
                dve.wait_ge(gate_step, 8)
                dve.tensor_scalar(gr[:], gr[:], gn[:, 3:4], None, ALU.mult).then_inc(gate_step, 1)
                dve.wait_ge(gate_turned, 1)
                dve.tensor_copy(gate_t[:], ps_gate[:, 0:E]).then_inc(gate_step, 1)

            @block.scalar
            def _(act):
                act.wait_ge(gate_step, 2)
                act.activation(gn[:, 1:2], gn[:, 0:1], ACT.Sqrt).then_inc(gate_step, 1)

            @block.tensor
            def _(pe):
                pe.wait_ge(gate_step, 9)
                pe.transpose(ps_gate[:, 0:E], gr[:], g["ident"][0:E, 0:E]).then_inc(gate_turned, 1)

            @block.gpsimd
            def _(pool):
                pool.memset(cparts[:], 0.0)
                pool.memset(scratch, 0.0)
                pool.tensor_copy(spread[:].rearrange("p a b -> p (a b)"), w["spread"])

        front = Front(nc, ctx, tag, g, x, mean, rstd)
        ps_g = [ps(f"ps_g{i}", [128, GT]) for i in R]
        ps_u = [ps(f"ps_u{i}", [128, GT]) for i in R]
        ps_c = ps("ps_c", [128, GT])
        ps_y = ps("ps_y", [T, GB, D])

        xs_ready, logits_ready, logits_taken = sem("xs_ready"), sem("logits_ready"), sem("logits_taken")
        tanh_ready, route_step, cparts_ready = sem("tanh_ready"), sem("route_step"), sem("cparts_ready")
        cparts_mid = sem("cparts_mid")
        cparts_turned, cw_t_ready = sem("cparts_turned"), sem("cw_t_ready")
        gate_up_ready, silu_ready, up_taken = sem("gate_up_ready"), sem("silu_ready"), sem("up_taken")
        spread_ready, hid_ready, down_done = sem("spread_ready"), sem("hid_ready"), sem("down_done")
        x_ready, stats_ready = sem("x_ready"), sem("stats_ready")
        LAGS, PEEL, ROUTE = 3, 4, 9

        with nc.Block() as block:
            @block.vector
            def _(dve):
                def scale_logits(it):
                    if it.live(1):
                        n = it.batch(1)
                        reach(dve, logits_ready, n + 1)
                        dve.tensor_tensor(z[:], front.ps[:, 0, 0:GB * E].rearrange("t (j e) -> t j e", e=E),
                                          row_inv[:, bass.ds(n * GB, GB)].unsqueeze(2).to_broadcast([T, GB, E]),
                                          ALU.mult).then_inc(logits_taken, 1)

                def route(it):
                    if it.live(1):
                        n = it.batch(1)
                        s = n * ROUTE
                        reach(dve, tanh_ready, n + 1)
                        dve.tensor_scalar(sc[:], th[:], 0.5, 0.5, ALU.mult, ALU.add).then_inc(route_step, 1)
                        reach_carried(dve, route_step, s + 1, scratch)
                        for j in range(GB):
                            last = dve.max(top[:, j], sc[:, j])
                        last.then_inc(route_step, 1)
                        reach_carried(dve, route_step, s + 2, scratch)
                        for j in range(GB):
                            last = dve.match_replace(left[:, j], top[:, j], sc[:, j], 0.0)
                        last.then_inc(route_step, 1)
                        reach(dve, route_step, s + 3)
                        dve.tensor_tensor(cw[:], sc[:], left[:], ALU.subtract).then_inc(route_step, 1)
                        reach(dve, route_step, s + 4)
                        dve.tensor_reduce(csum[:], cw[:], AX.X, ALU.add).then_inc(route_step, 1)
                        reach(dve, route_step, s + 5)
                        dve.reciprocal(cinv[:], csum[:]).then_inc(route_step, 1)
                        reach(dve, route_step, s + 6)
                        dve.tensor_tensor(cw[:], cw[:], cinv[:].unsqueeze(2).to_broadcast([T, GB, E]),
                                          ALU.mult).then_inc(route_step, 1)
                        reach(dve, route_step, s + 7)
                        reach(dve, cparts_turned, n)
                        dve.tensor_copy(cparts[:, :, 0:E], cw[:]).then_inc(route_step, 1)
                        reach(dve, route_step, s + 8)
                        dve.tensor_tensor(crest[:], cw[:], cparts[:, :, 0:E], ALU.subtract).then_inc(route_step, 1)
                        reach(dve, route_step, s + 9)
                        dve.tensor_copy(cparts[:, :, E:2 * E], crest[:]).then_inc(cparts_mid, 1)
                        reach(dve, cparts_mid, n + 1)
                        dve.tensor_tensor(cparts[:, :, 2 * E:3 * E], crest[:], cparts[:, :, E:2 * E],
                                          ALU.subtract).then_inc(cparts_ready, 1)

                def step(it):
                    front.normalise(dve, it)
                    for e in range(TILES):
                        if it.live(2):
                            n = it.batch(2)
                            k = n * TILES + e
                            reach(dve, silu_ready, k + 1)
                            if e < 8:
                                dve.tensor_tensor(prod[e % 2][:], silu[e % 2][:], ps_u[e % 2][:], ALU.mult).then_inc(up_taken, 1)
                                reach(dve, spread_ready, n * 8 + e + 1)
                                reach(dve, down_done, k - 1)
                                reach(dve, up_taken, n * 8 + e + 1)
                                dve.tensor_tensor(hid[e % 2][:].rearrange("h j t -> h (j t)"), prod[e % 2][:], ps_c[:],
                                                  ALU.mult).then_inc(hid_ready, 1)
                            else:
                                reach(dve, down_done, k - 1)
                                dve.tensor_tensor(hid[e % 2][0:HID].rearrange("h j t -> h (j t)"), silu[e % 2][0:HID],
                                                  ps_u[e % 2][0:HID], ALU.mult).then_inc(hid_ready, 1)
                        if e == 3:
                            scale_logits(it)
                        if e == 5:
                            route(it)
                        if e == 1 and it.live(3):
                            n = it.batch(3)
                            reach(dve, down_done, (n + 1) * TILES)
                            dve.scalar_tensor_tensor(x[:, bass.ds(n * GB, GB), :], ps_y[:], tg, x[:, bass.ds(n * GB, GB), :],
                                                     ALU.mult, ALU.add).then_inc(x_ready, 1)
                            reach(dve, x_ready, n + 1)
                            for j in range(GB):
                                last = dve.bn_stats(stats[:, n * GB + j, :], x[:, n * GB + j, :])
                            last.then_inc(stats_ready, 1)

                run_slots(dve, step, LAGS, PEEL, GROUPS, 2)

            @block.scalar
            def _(act):
                def step(it):
                    for e in range(TILES):
                        if it.live(2):
                            n = it.batch(2)
                            k = n * TILES + e
                            rows = 128 if e < 8 else HID
                            reach(act, gate_up_ready, k + 1)
                            reach(act, hid_ready, k - 1)
                            act.activation(silu[e % 2][0:rows], ps_g[e % 2][0:rows], ACT.Silu).then_inc(silu_ready, 1)
                        if e == 1 and it.live(1):
                            n, b = it.batch(1), it.buf(1)
                            reach(act, front.turned, n + 1)
                            reach(act, gate_up_ready, (n - 1) * TILES)
                            act.activation(xs[b][:], front.ps[:], ACT.Copy).then_inc(xs_ready, 1)
                        if e == 4 and it.live(1):
                            n = it.batch(1)
                            reach(act, logits_taken, n + 1)
                            reach(act, route_step, n * ROUTE)
                            act.activation(th[:], z[:], ACT.Tanh, scale=0.5).then_inc(tanh_ready, 1)
                        if e == 8 and it.live(1):
                            n, b = it.batch(1), it.buf(1)
                            reach(act, cparts_turned, n + 1)
                            reach(act, spread_ready, 8 * (n - 1))
                            act.activation(cw_t[b][:], front.ps[:].rearrange("p j t -> p (j t)")[:, 0:GT // 2].bitcast(BF16)
                                           .rearrange("p (j t) -> p j t", j=GB), ACT.Copy).then_inc(cw_t_ready, 1)

                run_slots(act, step, LAGS, PEEL, GROUPS, 2)

            @block.tensor
            def _(pe):
                def gate_up(it, e):
                    n, b = it.batch(2), it.buf(2)
                    k = n * TILES + e
                    rows = 128 if e < 8 else HID
                    reach(pe, hid_ready, k - 1)
                    reach(pe, silu_ready, k - 1)
                    if e == 0:
                        reach(pe, cw_t_ready, n + 1)
                    pe.matmul(ps_g[e % 2][0:rows], w["eg"][:, 128 * e:128 * e + rows], xs[b][:].rearrange("d j t -> d (j t)"),
                              start=True, stop=True)
                    pe.matmul(ps_u[e % 2][0:rows], w["eu"][:, 128 * e:128 * e + rows], xs[b][:].rearrange("d j t -> d (j t)"),
                              start=True, stop=True).then_inc(gate_up_ready, 1)
                    if e < 8:
                        reach(pe, hid_ready, k if e else k - 1)
                        pe.matmul(ps_c[:], spread[0:3 * E, e], cw_t[b][0:3 * E].rearrange("p j t -> p (j t)"),
                                  start=True, stop=True).then_inc(spread_ready, 1)

                def down(it, e):
                    n = it.batch(2)
                    k = n * TILES + e
                    if e == 0:
                        reach(pe, x_ready, n)
                    reach(pe, hid_ready, k + 1)
                    for j in range(GB):
                        lhs = hid[e % 2][:, j] if e < 8 else hid[e % 2][0:HID, j]
                        rhs = w["ed"][:, 128 * e:128 * e + 128] if e < 8 else sd[:]
                        last = pe.matmul(ps_y[:, j], lhs, rhs, start=(e == 0 and j == 0), stop=(e == 8),
                                         skip_group_check=True)
                    last.then_inc(down_done, 1)

                def step(it):
                    for e in range(TILES):
                        if it.live(2):
                            gate_up(it, e)
                            if e:
                                down(it, e - 1)
                        if e == 0:
                            front.turn(pe, it, cw_t_ready)
                        if e == 3 and it.live(1):
                            n, b = it.batch(1), it.buf(1)
                            reach(pe, xs_ready, n + 1)
                            for j in range(GB):
                                last = pe.matmul(front.ps[:, 0, E * j:E * j + E], xs[b][:, j], gate_t[:],
                                                 start=True, stop=True)
                            last.then_inc(logits_ready, 1)
                        if e == 8 and it.live(1):
                            n = it.batch(1)
                            reach(pe, cparts_ready, n + 1)
                            for j in range(GB):
                                last = pe.transpose(front.ps[:].rearrange("p j t -> p (j t)")[:, 64 * j:64 * j + 64].bitcast(BF16),
                                                    cparts[:, j], g["ident_bf"][:])
                            last.then_inc(cparts_turned, 1)
                    if it.live(2):
                        down(it, TILES - 1)

                run_slots(pe, step, LAGS, PEEL, GROUPS, 2)


def single_head_attention(nc, tag, g, x, stats, mean, rstd, tg, ctx_t, w, scale, swapped):
    with ExitStack() as ctx:
        def sb(name, shape, dt=F32):
            return ctx.enter_context(nc.sbuf_tensor(f"{tag}_{name}", shape, dt))

        def ps(name, shape):
            return ctx.enter_context(nc.psum_tensor(f"{tag}_{name}", shape, F32))

        def sem(name):
            return ctx.enter_context(nc.semaphore(f"{tag}_{name}"))

        R = range(2)
        xs = [sb(f"xs{i}", [D, GB, T]) for i in R]
        cs = [sb(f"cs{i}", [D, GB, T]) for i in R]
        q_t = [sb(f"q_t{i}", [D, GB, T]) for i in R]
        k_t = [sb(f"k_t{i}", [D, GB, T]) for i in R]
        v = [sb(f"v{i}", [T, GB, D]) for i in R]
        top = [sb(f"top{i}", [T, GB]) for i in R]
        total = [sb(f"total{i}", [T, GB]) for i in R]
        share = [sb(f"share{i}", [T, GB]) for i in R]
        probs = [sb(f"probs{i}", [T, GB, T]) for i in R]
        normed = [sb(f"normed{i}", [T, GB, T]) for i in R]
        probs_t = [sb(f"probs_t{i}", [T, GB, T]) for i in R]
        mixed = [sb(f"mixed{i}", [128, GB, 128]) for i in R]
        bo = sb("bo", [128, 1, D], BF16)
        bias_parts(nc, f"{tag}_bias", g, [w["bo"]], bo[:])

        front = Front(nc, ctx, tag, g, x, mean, rstd)
        ps_q, ps_k, ps_v = ps("ps_q", [D, GB, T]), ps("ps_k", [D, GB, T]), ps("ps_v", [T, GB, D])
        ps_s, ps_t = ps("ps_s", [T, GB, T]), ps("ps_t", [T, GB, T])
        ps_m, ps_y = ps("ps_m", [128, GB, 128]), ps("ps_y", [T, GB, D])
        ctx_in = [sem(f"ctx_in{i}") for i in R]
        q_made, k_made, v_made = sem("q_made"), sem("k_made"), sem("v_made")
        q_ready, k_ready, v_ready = sem("q_ready"), sem("k_ready"), sem("v_ready")
        top_step = sem("top_step")
        s_ready, top_ready, exp_ready = sem("s_ready"), sem("top_ready"), sem("exp_ready")
        share_ready, normed_ready = sem("share_ready"), sem("normed_ready")
        probs_turned, probs_t_ready = sem("probs_turned"), sem("probs_t_ready")
        mix_made, mix_ready, y_ready = sem("mix_made"), sem("mix_ready"), sem("y_ready")
        x_ready, stats_ready = sem("x_ready"), sem("stats_ready")
        LAGS, PEEL = 4, 6

        with nc.Block() as block:
            @block.sync
            def _(sp):
                def step(it):
                    if it.live(0):
                        n, b = it.batch(0), it.buf(0)
                        reach(sp, v_made, n - 1)
                        sp.dma_start(cs[b][:], ctx_t[bass.ds(n * GB, GB)].rearrange("j d t -> d j t")).then_inc(ctx_in[b], 16)

                run_slots(sp, step, LAGS, PEEL, GROUPS, 2)

            @block.vector
            def _(dve):
                def step(it):
                    if it.live(4):
                        n = it.batch(4)
                        reach(dve, y_ready, n + 1)
                        dve.scalar_tensor_tensor(x[:, bass.ds(n * GB, GB), :], ps_y[:], tg, x[:, bass.ds(n * GB, GB), :],
                                                 ALU.mult, ALU.add).then_inc(x_ready, 1)
                        reach(dve, x_ready, n + 1)
                        for j in range(GB):
                            last = dve.bn_stats(stats[:, n * GB + j, :], x[:, n * GB + j, :])
                        last.then_inc(stats_ready, 1)
                    if it.live(2):
                        n, b = it.batch(2), it.buf(2)
                        reach(dve, s_ready, n + 1)
                        reach(dve, exp_ready, n - 1)
                        dve.tensor_reduce(top[b][:], ps_s[:], AX.X, ALU.max).then_inc(top_step, 1)
                        reach(dve, top_step, n + 1)
                        dve.tensor_scalar(top[b][:], top[b][:], -scale, None, ALU.mult).then_inc(top_ready, 1)
                    if it.live(1):
                        n, b = it.batch(1), it.buf(1)
                        reach(dve, k_made, n + 1)
                        reach(dve, s_ready, n - 1)
                        dve.tensor_scalar(k_t[b][:], ps_k[:], w["bk"], None, ALU.add).then_inc(k_ready, 1)
                    front.normalise(dve, it)
                    if it.live(2):
                        n, b = it.batch(2), it.buf(2)
                        reach(dve, exp_ready, n + 1)
                        dve.reciprocal(share[b][:], total[b][:]).then_inc(share_ready, 1)
                        reach(dve, share_ready, n + 1)
                        reach(dve, probs_turned, n - 1)
                        dve.tensor_tensor(normed[b][:], probs[b][:], share[b][:].unsqueeze(2).to_broadcast([T, GB, T]),
                                          ALU.mult).then_inc(normed_ready, 1)
                    if it.live(3):
                        n, b = it.batch(3), it.buf(3)
                        reach(dve, mix_made, n + 1)
                        reach(dve, y_ready, n - 1)
                        if swapped:
                            dve.tensor_copy(mixed[b][:], ps_m[:]).then_inc(mix_ready, 1)
                        else:
                            dve.scalar_tensor_tensor(mixed[b][:], ps_m[:], w["bv"], q_t[b][:],
                                                     ALU.add, ALU.add).then_inc(mix_ready, 1)

                run_slots(dve, step, LAGS, PEEL, GROUPS, 2)

            @block.scalar
            def _(act):
                def step(it):
                    if it.live(3):
                        n, b = it.batch(3), it.buf(3)
                        reach(act, probs_turned, n + 1)
                        reach(act, mix_made, n - 1)
                        act.activation(probs_t[b][:], ps_t[:], ACT.Copy).then_inc(probs_t_ready, 1)
                    if it.live(1):
                        n, b = it.batch(1), it.buf(1)
                        reach(act, front.turned, n + 1)
                        reach(act, q_made, n - 1)
                        act.activation(xs[b][:], front.ps[:], ACT.Copy).then_inc(front.taken, 1)
                    if it.live(2):
                        n, b = it.batch(2), it.buf(2)
                        reach(act, top_ready, n + 1)
                        reach(act, normed_ready, n - 1)
                        for j in range(GB):
                            last = act.activation(probs[b][:, j], ps_s[:, j], ACT.Exp, bias=top[b][:, j:j + 1],
                                                  scale=scale, accum_out=total[b][:, j:j + 1])
                        last.then_inc(exp_ready, 1)
                    if it.live(1):
                        n, b = it.batch(1), it.buf(1)
                        reach(act, q_made, n + 1)
                        reach(act, mix_ready, n - 1)
                        act.activation(q_t[b][:], ps_q[:], ACT.Identity, bias=w["bq"]).then_inc(q_ready, 1)
                        reach(act, v_made, n + 1)
                        reach(act, mix_made, n - 1)
                        act.activation(v[b][:], ps_v[:], ACT.Copy).then_inc(v_ready, 1)

                run_slots(act, step, LAGS, PEEL, GROUPS, 2)

            @block.tensor
            def _(pe):
                def step(it):
                    if it.live(3):
                        n, b = it.batch(3), it.buf(3)
                        reach(pe, normed_ready, n + 1)
                        reach(pe, probs_t_ready, n)
                        for j in range(GB):
                            last = pe.transpose(ps_t[:, j], normed[b][:, j], g["ident"][:])
                        last.then_inc(probs_turned, 1)
                    if it.live(2):
                        n, b = it.batch(2), it.buf(2)
                        reach(pe, q_ready, n + 1)
                        reach(pe, k_ready, n + 1)
                        reach(pe, exp_ready, n)
                        for j in range(GB):
                            last = pe.matmul(ps_s[:, j], q_t[b][:, j], k_t[b][:, j], start=True, stop=True)
                        last.then_inc(s_ready, 1)
                    front.turn(pe, it)
                    if it.live(1):
                        n, b = it.batch(1), it.buf(1)
                        pe.wait_ge(ctx_in[b], 16 * (it.turn(1) + 1))
                        reach(pe, k_ready, n)
                        pe.matmul(ps_k[:], w["wk"], cs[b][:], start=True, stop=True).then_inc(k_made, 1)
                        reach(pe, v_ready, n)
                        for j in range(GB):
                            last = pe.matmul(ps_v[:, j], cs[b][:, j], w["wv"], start=True, stop=True)
                        last.then_inc(v_made, 1)
                    if it.live(3):
                        n, b = it.batch(3), it.buf(3)
                        reach(pe, probs_t_ready, n + 1)
                        reach(pe, mix_ready, n)
                        for j in range(GB):
                            if swapped:
                                last = pe.matmul(ps_m[:, j], probs_t[b][:, j], v[b][:, j], start=True, stop=True)
                            else:
                                last = pe.matmul(ps_m[:, j], v[b][:, j], probs_t[b][:, j], start=True, stop=True)
                        last.then_inc(mix_made, 1)
                    if it.live(1):
                        n, b = it.batch(1), it.buf(1)
                        reach(pe, front.taken, n + 1)
                        reach(pe, q_ready, n)
                        pe.matmul(ps_q[:], w["wq"], xs[b][:], start=True, stop=True).then_inc(q_made, 1)
                    if it.live(3):
                        n, b = it.batch(3), it.buf(3)
                        reach(pe, mix_ready, n + 1)
                        reach(pe, x_ready, n)
                        for j in range(GB):
                            pe.matmul(ps_y[:, j], mixed[b][:, j], w["wo"], start=True, stop=False)
                            last = pe.matmul(ps_y[:, j], g["ones_bf"][:], bo[:, 0], start=False, stop=True)
                        last.then_inc(y_ready, 1)

                run_slots(pe, step, LAGS, PEEL, GROUPS, 2)


def fused_projections(nc, tag, g, w, made):
    names = (("q", "h"), ("k", "c"), ("v", "c"))
    with ExitStack() as ctx:
        ps_w = ctx.enter_context(nc.psum_tensor(f"{tag}_ps_w", [D, 3, D], F32))
        ps_b = ctx.enter_context(nc.psum_tensor(f"{tag}_ps_b", [D, 4], F32))
        multiplied = ctx.enter_context(nc.semaphore(f"{tag}_multiplied"))
        with nc.Block() as block:
            @block.tensor
            def _(pe):
                for i, (second, first) in enumerate(names):
                    pe.matmul(ps_w[:, i], w[first + "w"], w[second + "w_t"], start=True, stop=True)
                    last = pe.matmul(ps_b[:, i:i + 1], w[second + "w_t"], w[first + "b"], start=True, stop=True)
                last.then_inc(multiplied, 1)

            @block.vector
            def _(dve):
                dve.wait_ge(multiplied, 1)
                for i, (second, _) in enumerate(names):
                    dve.tensor_copy(made["w" + second], ps_w[:, i])
                    dve.tensor_tensor(made["b" + second], ps_b[:, i:i + 1], w[second + "b"], ALU.add)


def channel_mix(nc, tag, g, x, stats, mean, rstd, tg, w):
    with ExitStack() as ctx:
        def sb(name, shape, dt=F32):
            return ctx.enter_context(nc.sbuf_tensor(f"{tag}_{name}", shape, dt))

        def ps(name, shape):
            return ctx.enter_context(nc.psum_tensor(f"{tag}_{name}", shape, F32))

        def sem(name):
            return ctx.enter_context(nc.semaphore(f"{tag}_{name}"))

        R = range(2)
        xs = [sb(f"xs{i}", [D, GB, T]) for i in R]
        xr = [sb(f"xr{i}", [D, GB, T]) for i in R]
        xk = [sb(f"xk{i}", [D, GB, T]) for i in R]
        relu = [sb(f"relu{i}", [D, GB, T]) for i in R]
        squared = [sb(f"squared{i}", [D, GB, T]) for i in R]
        gate = [sb(f"gate{i}", [T, GB, D]) for i in R]
        gated = [sb(f"gated{i}", [T, GB, D]) for i in R]
        rest = sb("rest", [D, 2])
        front = Front(nc, ctx, tag, g, x, mean, rstd)
        ps_k, ps_r, ps_v = ps("ps_k", [D, GB, T]), ps("ps_r", [T, GB, D]), ps("ps_v", [T, GB, D])
        rest_ready = sem("rest_ready")
        xs_ready, mixed_ready = sem("xs_ready"), sem("mixed_ready")
        k_made, relu_ready, squared_ready = sem("k_made"), sem("relu_ready"), sem("squared_ready")
        r_made, gate_ready, v_made = sem("r_made"), sem("gate_ready"), sem("v_made")
        gated_ready, x_ready, stats_ready = sem("gated_ready"), sem("x_ready"), sem("stats_ready")
        LAGS, PEEL = 3, 6

        with nc.Block() as block:
            @block.vector
            def _(dve):
                dve.tensor_scalar(rest[:, 0:1], w["mu_r"], -1.0, 1.0, ALU.mult, ALU.add)
                dve.tensor_scalar(rest[:, 1:2], w["mu_k"], -1.0, 1.0, ALU.mult, ALU.add).then_inc(rest_ready, 1)
                dve.wait_ge(rest_ready, 1)

                def step(it):
                    if it.live(3):
                        n, b = it.batch(3), it.buf(3)
                        reach(dve, v_made, n + 1)
                        reach(dve, gate_ready, n + 1)
                        dve.tensor_tensor(gated[b][:], gate[b][:], ps_v[:], ALU.mult).then_inc(gated_ready, 1)
                        reach(dve, gated_ready, n + 1)
                        dve.scalar_tensor_tensor(x[:, bass.ds(n * GB, GB), :], gated[b][:], tg,
                                                 x[:, bass.ds(n * GB, GB), :], ALU.mult, ALU.add).then_inc(x_ready, 1)
                        reach(dve, x_ready, n + 1)
                        for j in range(GB):
                            last = dve.bn_stats(stats[:, n * GB + j, :], x[:, n * GB + j, :])
                        last.then_inc(stats_ready, 1)
                    if it.live(1):
                        n, b = it.batch(1), it.buf(1)
                        reach(dve, xs_ready, n + 1)
                        dve.scalar_tensor_tensor(xk[b][:, :, 1:T], xs[b][:, :, 0:T - 1], rest[:, 1:2], xk[b][:, :, 1:T],
                                                 ALU.mult, ALU.add)
                        dve.scalar_tensor_tensor(xr[b][:, :, 1:T], xs[b][:, :, 0:T - 1], rest[:, 0:1], xr[b][:, :, 1:T],
                                                 ALU.mult, ALU.add).then_inc(mixed_ready, 1)
                    front.normalise(dve, it)

                run_slots(dve, step, LAGS, PEEL, GROUPS, 2)

            @block.scalar
            def _(act):
                def step(it):
                    if it.live(1):
                        n, b = it.batch(1), it.buf(1)
                        reach(act, front.turned, n + 1)
                        reach(act, mixed_ready, n - 1)
                        reach(act, r_made, n - 1)
                        act.activation(xk[b][:], front.ps[:], ACT.Copy, scale=w["mu_k"])
                        act.activation(xr[b][:], front.ps[:], ACT.Copy, scale=w["mu_r"])
                        act.activation(xs[b][:], front.ps[:], ACT.Copy).then_inc(xs_ready, 1)
                    if it.live(2):
                        n, b = it.batch(2), it.buf(2)
                        reach(act, k_made, n + 1)
                        reach(act, squared_ready, n - 1)
                        act.activation(relu[b][:], ps_k[:], ACT.Relu).then_inc(relu_ready, 1)
                        reach(act, r_made, n + 1)
                        reach(act, gated_ready, n - 1)
                        act.activation(gate[b][:], ps_r[:], ACT.Sigmoid).then_inc(gate_ready, 1)

                run_slots(act, step, LAGS, PEEL, GROUPS, 2)

            @block.gpsimd
            def _(pool):
                def step(it):
                    if it.live(2):
                        n, b = it.batch(2), it.buf(2)
                        reach(pool, v_made, n - 1)
                        reach(pool, relu_ready, n + 1)
                        pool.tensor_tensor(squared[b][:], relu[b][:], relu[b][:], ALU.mult).then_inc(squared_ready, 1)

                run_slots(pool, step, LAGS, PEEL, GROUPS, 2)

            @block.tensor
            def _(pe):
                def step(it):
                    if it.live(2):
                        n, b = it.batch(2), it.buf(2)
                        reach(pe, mixed_ready, n + 1)
                        reach(pe, relu_ready, n)
                        pe.matmul(ps_k[:], w["wk_t"], xk[b][:], start=True, stop=True).then_inc(k_made, 1)
                        reach(pe, gate_ready, n)
                        for j in range(GB):
                            last = pe.matmul(ps_r[:, j], xr[b][:, j], w["wr_t"], start=True, stop=True)
                        last.then_inc(r_made, 1)
                    front.turn(pe, it, xs_ready)
                    if it.live(3):
                        n, b = it.batch(3), it.buf(3)
                        reach(pe, squared_ready, n + 1)
                        reach(pe, gated_ready, n)
                        for j in range(GB):
                            last = pe.matmul(ps_v[:, j], squared[b][:, j], w["wv_t"], start=True, stop=True)
                        last.then_inc(v_made, 1)

                run_slots(pe, step, LAGS, PEEL, GROUPS, 2)


def spectral_map(nc, tag, g, x, mean, rstd, tg, w, out_rows):
    with ExitStack() as ctx:
        def sb(name, shape, dt=F32):
            return ctx.enter_context(nc.sbuf_tensor(f"{tag}_{name}", shape, dt))

        def ps(name, shape):
            return ctx.enter_context(nc.psum_tensor(f"{tag}_{name}", shape, F32))

        def sem(name):
            return ctx.enter_context(nc.semaphore(f"{tag}_{name}"))

        R = range(2)
        fwd = sb("fwd", [D, 2, D])
        whole = sb("whole", [D, D])
        xs = [sb(f"xs{i}", [D, GB, T]) for i in R]
        bo = sb("bo", [128, 1, D], BF16)
        fwd_made, fwd_ready, whole_made = sem("fwd_made"), sem("fwd_ready"), sem("whole_made")
        bias_parts(nc, f"{tag}_bias", g, [[(w["fb"], g["ident"][:])]], bo[:])
        front = Front(nc, ctx, tag, g, x, mean, rstd)
        ps_y = ps("ps_y", [T, GB, D])
        ps_f = ps("ps_f", [D, 3, D])
        with nc.Block() as block:
            @block.tensor
            def _(pe):
                pe.matmul(ps_f[:, 0], w["fr"], w["dft_cos"], start=True, stop=False)
                pe.matmul(ps_f[:, 0], w["fi"], w["dft_sin"], start=False, stop=True)
                pe.matmul(ps_f[:, 1], w["fi"], w["dft_cos"], start=True, stop=False)
                pe.matmul(ps_f[:, 1], w["fr"], w["dft_nsin"], start=False, stop=True).then_inc(fwd_made, 1)
                pe.wait_ge(fwd_ready, 1)
                pe.matmul(ps_f[:, 2], fwd[:, 0], w["dft_cos"], start=True, stop=False)
                pe.matmul(ps_f[:, 2], fwd[:, 1], w["dft_nsin"], start=False, stop=True).then_inc(whole_made, 1)

            @block.vector
            def _(dve):
                dve.wait_ge(fwd_made, 1)
                dve.tensor_copy(fwd[:], ps_f[:, 0:2]).then_inc(fwd_ready, 1)
                dve.wait_ge(whole_made, 1)
                dve.tensor_scalar(whole[:], ps_f[:, 2], 1.0 / D, None, ALU.mult)

        y_ready, x_ready = sem("y_ready"), sem("x_ready")
        stored = [sem(f"stored{i}") for i in R]
        LAGS, PEEL = 2, 4
        with nc.Block() as block:
            @block.vector
            def _(dve):
                def step(it):
                    front.normalise(dve, it)
                    if it.live(2):
                        n = it.batch(2)
                        reach(dve, y_ready, n + 1)
                        dve.scalar_tensor_tensor(x[:, bass.ds(n * GB, GB), :], ps_y[:], tg, x[:, bass.ds(n * GB, GB), :],
                                                 ALU.mult, ALU.add).then_inc(x_ready, 1)

                run_slots(dve, step, LAGS, PEEL, GROUPS, 2)

            @block.scalar
            def _(act):
                def step(it):
                    if it.live(1):
                        n, b = it.batch(1), it.buf(1)
                        reach(act, front.turned, n + 1)
                        reach(act, y_ready, n - 1)
                        act.activation(xs[b][:], front.ps[:], ACT.Copy).then_inc(front.taken, 1)

                run_slots(act, step, LAGS, PEEL, GROUPS, 2)

            @block.tensor
            def _(pe):
                def step(it):
                    front.turn(pe, it)
                    if it.live(2):
                        n, b = it.batch(2), it.buf(2)
                        reach(pe, front.taken, n + 1)
                        reach(pe, x_ready, n)
                        for j in range(GB):
                            pe.matmul(ps_y[:, j], xs[b][:, j], whole[:], start=True, stop=False)
                            last = pe.matmul(ps_y[:, j], g["ones_bf"][:], bo[:, 0], start=False, stop=True)
                        last.then_inc(y_ready, 1)

                run_slots(pe, step, LAGS, PEEL, GROUPS, 2)

            @block.sync
            def _(sp):
                def step(it):
                    if it.live(2):
                        n, b = it.batch(2), it.buf(2)
                        reach(sp, x_ready, n + 1)
                        sp.dma_start(out_rows[:, bass.ds(n * GB, GB)], x[:, bass.ds(n * GB, GB), :]).then_inc(stored[b], 16)

                run_slots(sp, step, LAGS, PEEL, GROUPS, 2)
                for b in R:
                    sp.wait_ge(stored[b], 16 * GROUPS // 2)


def quantised_mlp(nc, tag, g, x, stats, mean, rstd, tg, w):
    F, FT = 512, 4
    MAGIC = 12582912.0
    with ExitStack() as ctx:
        def sb(name, shape, dt=F32):
            return ctx.enter_context(nc.sbuf_tensor(f"{tag}_{name}", shape, dt))

        def sem(name):
            return ctx.enter_context(nc.semaphore(f"{tag}_{name}"))

        R = range(2)
        row_max, row_min = sb("row_max", [128, 5]), sb("row_min", [128, 5])
        s_w, s_w_inv = sb("s_w", [128, 5]), sb("s_w_inv", [128, 5])
        w1q, w2q = sb("w1q", [128, FT, D]), sb("w2q", [D, F])
        w1_t, w2_t = sb("w1_t", [D, FT, 128], BF16), sb("w2_t", [128, FT, D], BF16)
        x_t = sb("x_t", [D, B * T])
        seen = sb("seen", [128, 2 * GROUPS])
        peak = sb("peak", [128, 2])
        s_x, s_x_inv = sb("s_x", [128, 2]), sb("s_x_inv", [128, 2])
        steps = sb("steps", [128, 5])
        steps_inv, b1q, b2q = sb("steps_inv", [128, 5]), sb("b1q", [128, FT]), sb("b2q", [128, 1])
        xi = [sb(f"xi{i}", [D, GT]) for i in R]
        xq = [sb(f"xq{i}", [D, GT], BF16) for i in R]
        hid = sb("hid", [128, GROUPS, FT, GT])
        rows = sb("rows", [128, 2, D])

        with ExitStack() as inner:
            ps_w = [inner.enter_context(nc.psum_tensor(f"{tag}_ps_w{i}", [128, FT, 128], F32)) for i in R]
            maxed, scaled, wq_step, w_turned = sem("maxed"), sem("scaled"), sem("wq_step"), sem("w_turned")
            with nc.Block() as block:
                @block.vector
                def _(dve):
                    w1 = w["w1"].rearrange("p (f d) -> p f d", f=FT)
                    dve.tensor_reduce(row_max[:, 0:FT], w1, AX.X, ALU.max)
                    dve.tensor_reduce(row_max[:, FT:5], w["w2"], AX.X, ALU.max)
                    dve.tensor_reduce(row_min[:, 0:FT], w1, AX.X, ALU.min)
                    dve.tensor_reduce(row_min[:, FT:5], w["w2"], AX.X, ALU.min).then_inc(maxed, 1)
                    dve.wait_ge(maxed, 1)
                    dve.scalar_tensor_tensor(row_max[:], row_min[:], -1.0, row_max[:], ALU.mult, ALU.max).then_inc(maxed, 1)
                    dve.wait_ge(maxed, 2)
                    dve.tensor_scalar(s_w[:], row_max[:], 1e-8, 1.0 / 127.0, ALU.max, ALU.mult).then_inc(scaled, 1)
                    dve.wait_ge(scaled, 1)
                    dve.reciprocal(s_w_inv[:], s_w[:]).then_inc(scaled, 1)
                    dve.wait_ge(scaled, 2)
                    for f in range(FT):
                        dve.tensor_scalar(w1q[:, f], w1[:, f], s_w_inv[:, f:f + 1], MAGIC, ALU.mult, ALU.add)
                    dve.tensor_scalar(w2q[:], w["w2"], s_w_inv[:, FT:5], MAGIC, ALU.mult, ALU.add).then_inc(wq_step, 1)
                    dve.wait_ge(wq_step, 1)
                    dve.tensor_scalar(w1q[:], w1q[:], MAGIC, -128.0, ALU.subtract, ALU.max)
                    dve.tensor_scalar(w2q[:], w2q[:], MAGIC, -128.0, ALU.subtract, ALU.max).then_inc(wq_step, 1)
                    dve.wait_ge(wq_step, 2)
                    dve.tensor_scalar(w1q[:], w1q[:], 127.0, None, ALU.min)
                    dve.tensor_scalar(w2q[:], w2q[:], 127.0, None, ALU.min).then_inc(wq_step, 1)
                    dve.wait_ge(w_turned, 1)
                    dve.tensor_copy(w1_t[:], ps_w[0][:])
                    dve.tensor_copy(w2_t[:], ps_w[1][:])

                @block.tensor
                def _(pe):
                    pe.wait_ge(wq_step, 3)
                    for f in range(FT):
                        pe.transpose(ps_w[0][:, f], w1q[:, f], g["ident"][:])
                        last = pe.transpose(ps_w[1][:, f], w2q[:, 128 * f:128 * f + 128], g["ident"][:])
                    last.then_inc(w_turned, 1)

        with ExitStack() as inner:
            front = Front(nc, inner, tag, g, x, mean, rstd)
            turned_ready, seen_ready = sem("turned_ready"), sem("seen_ready")
            LAGS, PEEL = 1, 4
            with nc.Block() as block:
                @block.vector
                def _(dve):
                    def step(it):
                        front.normalise(dve, it)
                        if it.live(1):
                            n = it.batch(1)
                            reach(dve, turned_ready, n + 1)
                            dve.tensor_reduce(seen[:, bass.ds(n, 1)], x_t[:, bass.ds(n * GT, GT)], AX.X, ALU.max)\
                               .then_inc(seen_ready, 1)

                    run_slots(dve, step, LAGS, PEEL, GROUPS, 2)

                @block.scalar
                def _(act):
                    def step(it):
                        if it.live(1):
                            n = it.batch(1)
                            reach(act, front.turned, n + 1)
                            act.activation(x_t[:, bass.ds(n * GT, GT)], front.ps[:].rearrange("d j t -> d (j t)"),
                                           ACT.Copy).then_inc(turned_ready, 1)

                    run_slots(act, step, LAGS, PEEL, GROUPS, 2)

                @block.tensor
                def _(pe):
                    def step(it):
                        front.turn(pe, it, turned_ready)

                    run_slots(pe, step, LAGS, PEEL, GROUPS, 2)

        def scales(which, col, b_of, b_to, first, last_):
            at = f"{tag}_{which}"
            with ExitStack() as inner:
                local_max, whole_max, step = (inner.enter_context(nc.semaphore(f"{at}_{k}")) for k in ("local", "whole", "step"))
                local = inner.enter_context(nc.sbuf_tensor(f"{at}_localmax", [128, 1], F32))
                n = last_ - first
                with nc.Block() as block:
                    @block.vector
                    def _(dve):
                        dve.tensor_reduce(local[:], seen[:, 0:GROUPS], AX.X, ALU.max).then_inc(local_max, 1)
                        dve.wait_ge(whole_max, 1)
                        dve.tensor_scalar(s_x[:, col:col + 1], peak[:, col:col + 1], 1e-8, 1.0 / 255.0, ALU.max, ALU.mult).then_inc(step, 1)
                        dve.wait_ge(step, 1)
                        dve.reciprocal(s_x_inv[:, col:col + 1], s_x[:, col:col + 1])
                        dve.tensor_scalar(steps[:, first:last_], s_w[:, first:last_], s_x[:, col:col + 1], None, ALU.mult).then_inc(step, 1)
                        dve.wait_ge(step, 2)
                        dve.reciprocal(steps_inv[:, first:last_], steps[:, first:last_]).then_inc(step, 1)
                        dve.wait_ge(step, 3)
                        dve.tensor_tensor(b_to, b_of, steps_inv[:, first:last_], ALU.mult).then_inc(step, 1)
                        dve.wait_ge(step, 4)
                        dve.tensor_scalar(b_to, b_to, MAGIC, None, ALU.add).then_inc(step, 1)
                        dve.wait_ge(step, 5)
                        dve.tensor_scalar(b_to, b_to, MAGIC, None, ALU.subtract).then_inc(step, 1)
                        dve.wait_ge(step, 6)
                        dve.tensor_tensor(b_to, b_to, steps[:, first:last_], ALU.mult).then_inc(step, 1)

                    @block.gpsimd
                    def _(pool):
                        pool.wait_ge(local_max, 1)
                        pool.partition_all_reduce(peak[:, col:col + 1], local[:], 128, MAX_OVER_PARTITIONS).then_inc(whole_max, 1)

        scales("in", 0, w["b1"], b1q[:], 0, FT)

        with ExitStack() as inner:
            ps_h = [[inner.enter_context(nc.psum_tensor(f"{tag}_ps_h{i}{f}", [128, GT], F32)) for f in range(FT)] for i in R]
            scaled_x, rounded, xq_ready = sem("scaled_x"), sem("rounded"), sem("xq_ready")
            h_made, hid_ready, hid_seen = sem("h_made"), sem("hid_ready"), sem("hid_seen")
            LAGS, PEEL = 2, 4
            with nc.Block() as block:
                @block.vector
                def _(dve):
                    def step(it):
                        if it.live(2):
                            n = it.batch(2)
                            reach(dve, hid_ready, n + 1)
                            dve.tensor_reduce(seen[:, bass.ds(n, 1)], hid[:, n].rearrange("p f t -> p (f t)"), AX.X, ALU.max)\
                               .then_inc(hid_seen, 1)
                        if it.live(0):
                            n, b = it.batch(0), it.buf(0)
                            dve.tensor_scalar(xi[b][:], x_t[:, bass.ds(n * GT, GT)], s_x_inv[:, 0:1], 0.0,
                                              ALU.mult, ALU.max).then_inc(scaled_x, 1)
                            reach(dve, scaled_x, n + 1)
                            dve.tensor_scalar(xi[b][:], xi[b][:], 255.0, MAGIC, ALU.min, ALU.add).then_inc(rounded, 1)
                            reach(dve, rounded, n + 1)
                            reach(dve, h_made, n - 1)
                            dve.tensor_scalar(xq[b][:], xi[b][:], MAGIC, None, ALU.subtract).then_inc(xq_ready, 1)

                    run_slots(dve, step, LAGS, PEEL, GROUPS, 2)

                @block.tensor
                def _(pe):
                    def step(it):
                        if it.live(1):
                            n, b = it.batch(1), it.buf(1)
                            reach(pe, xq_ready, n + 1)
                            reach(pe, hid_ready, n - 1)
                            for f in range(FT):
                                last = pe.matmul(ps_h[b][f][:], w1_t[:, f], xq[b][:], start=True, stop=True)
                            last.then_inc(h_made, 1)

                    run_slots(pe, step, LAGS, PEEL, GROUPS, 2)

                @block.scalar
                def _(act):
                    def step(it):
                        if it.live(1):
                            n, b = it.batch(1), it.buf(1)
                            reach(act, h_made, n + 1)
                            for f in range(FT):
                                last = act.activation(hid[:, n, f], ps_h[b][f][:], ACT.Relu, bias=b1q[:, f:f + 1],
                                                      scale=steps[:, f:f + 1])
                            last.then_inc(hid_ready, 1)

                    run_slots(act, step, LAGS, PEEL, GROUPS, 2)

        scales("hid", 1, w["b2"], b2q[:], FT, 5)

        with ExitStack() as inner:
            ps_r = inner.enter_context(nc.psum_tensor(f"{tag}_ps_r", [128, 2, D], F32))
            rows_made = sem("rows_made")
            with nc.Block() as block:
                @block.tensor
                def _(pe):
                    pe.matmul(ps_r[:, 0], steps[:, FT:5].to_broadcast([128, 128]), g["ident"][:], start=True, stop=True)
                    pe.matmul(ps_r[:, 1], b2q[:].to_broadcast([128, 128]), g["ident"][:], start=True, stop=True)\
                      .then_inc(rows_made, 1)

                @block.vector
                def _(dve):
                    dve.wait_ge(rows_made, 1)
                    dve.tensor_scalar(rows[:], ps_r[:], tg, None, ALU.mult)

            ps_y = [inner.enter_context(nc.psum_tensor(f"{tag}_ps_y{i}", [T, GB, D], F32)) for i in R]
            hi = [sb(f"hi{i}", [128, FT, GT]) for i in R]
            hq = [sb(f"hq{i}", [128, FT, GT], BF16) for i in R]
            ys = [sb(f"ys{i}", [T, GB, D]) for i in R]
            scaled_h, rounded_h, hq_ready = sem("scaled_h"), sem("rounded_h"), sem("hq_ready")
            y_ready, y_step, x_ready, stats_ready, biased = (sem(k) for k in ("y_ready", "y_step", "x_ready", "stats_ready", "biased"))
            LAGS, PEEL = 2, 4
            with nc.Block() as block:
                @block.vector
                def _(dve):
                    def step(it):
                        if it.live(0):
                            n, b = it.batch(0), it.buf(0)
                            reach(dve, hq_ready, n - 1)
                            dve.tensor_scalar(hi[b][:], hid[:, n], s_x_inv[:, 1:2], 255.0, ALU.mult, ALU.min)\
                               .then_inc(scaled_h, 1)
                            reach(dve, scaled_h, n + 1)
                            dve.tensor_scalar(hi[b][:], hi[b][:], MAGIC, None, ALU.add).then_inc(rounded_h, 1)
                        if it.live(2):
                            n, b = it.batch(2), it.buf(2)
                            reach(dve, y_ready, n + 1)
                            dve.tensor_tensor(ys[b][:], ps_y[b][:], rows[:, 0:1].to_broadcast([T, GB, D]),
                                              ALU.mult).then_inc(y_step, 1)
                            reach(dve, y_step, n + 1)
                            reach(dve, biased, n + 1)
                            dve.tensor_tensor(x[:, bass.ds(n * GB, GB), :], ys[b][:], x[:, bass.ds(n * GB, GB), :],
                                              ALU.add).then_inc(x_ready, 1)
                            reach(dve, x_ready, n + 1)
                            for j in range(GB):
                                last = dve.bn_stats(stats[:, n * GB + j, :], x[:, n * GB + j, :])
                            last.then_inc(stats_ready, 1)

                    run_slots(dve, step, LAGS, PEEL, GROUPS, 2)

                @block.scalar
                def _(act):
                    def step(it):
                        if it.live(0):
                            n, b = it.batch(0), it.buf(0)
                            reach(act, rounded_h, n + 1)
                            reach(act, y_ready, n - 1)
                            act.activation(hq[b][:], hi[b][:], ACT.Copy, bias=-MAGIC).then_inc(hq_ready, 1)

                    run_slots(act, step, LAGS, PEEL, GROUPS, 2)

                @block.gpsimd
                def _(pool):
                    def step(it):
                        if it.live(0):
                            n = it.batch(0)
                            pool.tensor_tensor(x[:, bass.ds(n * GB, GB), :], x[:, bass.ds(n * GB, GB), :],
                                               rows[:, 1:2].to_broadcast([T, GB, D]), ALU.add).then_inc(biased, 1)

                    run_slots(pool, step, LAGS, PEEL, GROUPS, 2)

                @block.tensor
                def _(pe):
                    def step(it):
                        if it.live(1):
                            n, b = it.batch(1), it.buf(1)
                            reach(pe, hq_ready, n + 1)
                            reach(pe, y_step, n - 1)
                            for j in range(GB):
                                for f in range(FT):
                                    last = pe.matmul(ps_y[b][:, j], hq[b][:, f, T * j:T * j + T], w2_t[:, f],
                                                     start=(f == 0), stop=(f == FT - 1))
                            last.then_inc(y_ready, 1)

                    run_slots(pe, step, LAGS, PEEL, GROUPS, 2)


def layernorm_statistics(nc, tag, g, stats, mean, rstd, row_inv=None):
    with ExitStack() as ctx:
        def sb(name):
            return ctx.enter_context(nc.sbuf_tensor(f"{tag}_{name}", [128, B], F32))

        half, gap2, var, eps_var, root, inv = (sb(k) for k in ("half", "gap2", "var", "eps_var", "root", "inv"))
        step = ctx.enter_context(nc.semaphore(f"{tag}_step"))
        to_root = ctx.enter_context(nc.semaphore(f"{tag}_to_root"))
        rooted = ctx.enter_context(nc.semaphore(f"{tag}_rooted"))
        with nc.Block() as block:
            @block.vector
            def _(dve):
                even, odd = stats[:, :, 1], stats[:, :, 4]
                dve.tensor_tensor(half[:], even, odd, ALU.subtract).then_inc(step, 1)
                dve.tensor_tensor(mean[:], even, odd, ALU.add).then_inc(step, 1)
                dve.tensor_tensor(var[:], stats[:, :, 2], stats[:, :, 5], ALU.add).then_inc(step, 1)
                dve.wait_ge(step, 3)
                dve.scalar_tensor_tensor(gap2[:], half[:], 0.25, half[:], ALU.mult, ALU.mult).then_inc(step, 1)
                dve.tensor_scalar(mean[:], mean[:], 0.5, None, ALU.mult).then_inc(step, 1)
                dve.wait_ge(step, 4)
                dve.scalar_tensor_tensor(var[:], var[:], 1.0 / D, gap2[:], ALU.mult, ALU.add).then_inc(step, 1)
                dve.wait_ge(step, 6)
                dve.tensor_scalar(eps_var[:], var[:], LN_EPS, None, ALU.add).then_inc(to_root, 1)

                def newton(square, k):
                    dve.wait_ge(rooted, k)
                    dve.reciprocal(inv[:], root[:]).then_inc(step, 1)
                    at = 4 + 3 * k
                    dve.wait_ge(step, at)
                    dve.tensor_tensor(inv[:], inv[:], square, ALU.mult).then_inc(step, 1)
                    dve.wait_ge(step, at + 1)
                    dve.tensor_tensor(inv[:], inv[:], root[:], ALU.add).then_inc(step, 1)
                    dve.wait_ge(step, at + 2)

                newton(eps_var[:], 1)
                dve.tensor_scalar(inv[:], inv[:], 0.5, None, ALU.mult).then_inc(to_root, 1)
                dve.wait_ge(to_root, 2)
                dve.reciprocal(rstd[:], inv[:]).then_inc(to_root, 1)
                if row_inv is not None:
                    dve.wait_ge(to_root, 3)
                    dve.tensor_tensor(var[:], var[:], rstd[:], ALU.mult).then_inc(to_root, 1)
                    dve.wait_ge(to_root, 4)
                    dve.scalar_tensor_tensor(var[:], var[:], float(D), rstd[:], ALU.mult, ALU.mult).then_inc(to_root, 1)
                    dve.wait_ge(rooted, 2)
                    dve.tensor_scalar(root[:], root[:], 1e-12, None, ALU.max).then_inc(rooted, 1)
                    dve.wait_ge(rooted, 3)
                    dve.reciprocal(inv[:], root[:]).then_inc(step, 1)
                    dve.wait_ge(step, 10)
                    dve.tensor_tensor(inv[:], inv[:], var[:], ALU.mult).then_inc(step, 1)
                    dve.wait_ge(step, 11)
                    dve.tensor_tensor(inv[:], inv[:], root[:], ALU.add).then_inc(step, 1)
                    dve.wait_ge(step, 12)
                    dve.tensor_scalar(inv[:], inv[:], 0.5, 1e-12, ALU.mult, ALU.max).then_inc(step, 1)
                    dve.wait_ge(step, 13)
                    dve.reciprocal(row_inv[:], inv[:]).then_inc(step, 1)

            @block.scalar
            def _(act):
                act.wait_ge(to_root, 1)
                act.activation(root[:], eps_var[:], ACT.Sqrt).then_inc(rooted, 1)
                if row_inv is not None:
                    act.wait_ge(to_root, 5)
                    act.activation(root[:], var[:], ACT.Sqrt).then_inc(rooted, 1)


PACK = [
    ("ident", 128), ("pick", 1024), ("spread", 1024), ("dft_cos", 128), ("dft_sin", 128), ("dft_nsin", 128),
    ("wq0", 128), ("wkv0", 256), ("wo0", 128), ("bq0", 1), ("bk0", 1), ("bv0", 1), ("bo0", 1),
    ("eg", 1088), ("eu", 1088), ("ed", 1024),
    ("hw", 128), ("cw", 128), ("qw_t", 128), ("kw_t", 128), ("vw_t", 128), ("ow_t", 128),
    ("hb", 1), ("cb", 1), ("qb", 1), ("kb", 1), ("vb", 1), ("ob", 1),
    ("w1", 512), ("b1", 4), ("w2", 512), ("b2", 1),
    ("wq2", 128), ("wkv2", 256), ("wo2", 128), ("bq2", 1), ("bk2", 1), ("bv2", 1), ("bo2", 1),
    ("wr_t", 128), ("wk_t", 128), ("wv_t", 128), ("mu_r", 1), ("mu_k", 1),
    ("q3", 128), ("k3", 128), ("v3", 128), ("p3", 128), ("bp", 1),
    ("fr", 128), ("fi", 128), ("fb", 1),
    ("gates", 8),
]
PACKED = sum(n for _, n in PACK)


def build(nc, x_in, ctx_t, pack, gate_in, down_in, out):
    x_rows = x_in.rearrange("b t d -> t b d")
    out_rows = out.rearrange("b t d -> t b d")
    with ExitStack() as ctx:
        def sb(name, shape, dt=F32):
            return ctx.enter_context(nc.sbuf_tensor(name, shape, dt))

        wp = sb("wp", [128, PACKED])
        w, at = {}, 0
        for name, n in PACK:
            w[name] = wp[:, at:at + n]
            at += n
        x = sb("x", [T, B, D])
        stats, mean, rstd = sb("stats", [T, B, 6]), sb("mean", [T, B]), sb("rstd", [T, B])
        tg = sb("tg", [128, 8])
        ident_bf, ones_bf = sb("ident_bf", [128, 128], BF16), sb("ones_bf", [128, 128], BF16)
        pick = sb("pick", [128, 8, 128], BF16)
        g = {"ident": w["ident"], "ident_bf": ident_bf, "ones_bf": ones_bf, "pick": pick}

        x_loaded = [ctx.enter_context(nc.semaphore(f"x_loaded{i}")) for i in range(4)]
        w_loaded = ctx.enter_context(nc.semaphore("w_loaded"))
        setup = ctx.enter_context(nc.semaphore("setup"))
        with nc.Block() as block:
            @block.sync
            def _(sp):
                for i in range(4):
                    sp.dma_start(x[:, 8 * i:8 * i + 8], x_rows[:, 8 * i:8 * i + 8]).then_inc(x_loaded[i], 16)

            @block.scalar
            def _(act):
                act.dma_start(wp[:], pack).then_inc(w_loaded, 16)
                act.wait_ge(w_loaded, 16)
                act.activation(tg[:], w["gates"], ACT.Tanh).then_inc(setup, 1)

            @block.gpsimd
            def _(pool):
                pool.wait_ge(w_loaded, 16)
                pool.memset(ones_bf[:], 1.0).then_inc(setup, 1)
                pool.tensor_copy(ident_bf[:], w["ident"]).then_inc(setup, 1)
                pool.tensor_copy(pick[:].rearrange("p a b -> p (a b)"), w["pick"]).then_inc(setup, 1)

            @block.vector
            def _(dve):
                for n in range(B):
                    if n % 8 == 0:
                        dve.wait_ge(x_loaded[n // 8], 16)
                    dve.bn_stats(stats[:, n, :], x[:, n, :]).then_inc(setup, 1)

        def att(tag, i):
            return {"wq_t": w[f"wq{i}"], "wkv_t": w[f"wkv{i}"], "wo_t": w[f"wo{i}"], "bq": w[f"bq{i}"],
                    "bk": w[f"bk{i}"], "bv": w[f"bv{i}"], "bo": w[f"bo{i}"]}

        layernorm_statistics(nc, "n0a", g, stats, mean, rstd)
        many_head_attention(nc, "a0", g, x, stats, mean, rstd, tg[:, 0:1], ctx_t, att("a0", 0))
        row_inv = ctx.enter_context(nc.sbuf_tensor("row_inv", [T, B], F32))
        layernorm_statistics(nc, "n0b", g, stats, mean, rstd, row_inv)
        mixture_of_experts(nc, "m0", g, x, stats, mean, rstd, row_inv, tg[:, 4:5], w, down_in, gate_in)
        made = ctx.enter_context(nc.sbuf_tensor("made", [D, 3 * D + 3], F32))
        fused = {"wq": made[:, 0:D], "wk": made[:, D:2 * D], "wv": made[:, 2 * D:3 * D], "bq": made[:, 384:385],
                 "bk": made[:, 385:386], "bv": made[:, 386:387], "wo": w["ow_t"], "bo": [(w["ob"], w["ident"])]}
        fused_projections(nc, "f1", g, w, fused)
        layernorm_statistics(nc, "n1a", g, stats, mean, rstd)
        single_head_attention(nc, "a1", g, x, stats, mean, rstd, tg[:, 1:2], ctx_t, fused, float(D) ** -0.5, False)
        layernorm_statistics(nc, "n1b", g, stats, mean, rstd)
        quantised_mlp(nc, "m1", g, x, stats, mean, rstd, tg[:, 5:6], w)
        used = sorted(nc.released_uncleared_semaphores)
        with nc.Block() as block:
            @block.gpsimd
            def _(pool):
                for number in used:
                    if number - 1 not in used:
                        end = number
                        while end in used:
                            end += 1
                        pool.sem_clear(range(number, end))
        layernorm_statistics(nc, "n2a", g, stats, mean, rstd)
        many_head_attention(nc, "a2", g, x, stats, mean, rstd, tg[:, 2:3], ctx_t, att("a2", 2))
        layernorm_statistics(nc, "n2b", g, stats, mean, rstd)
        channel_mix(nc, "m2", g, x, stats, mean, rstd, tg[:, 6:7], w)
        none = made[:, 386:387]
        layernorm_statistics(nc, "n3a", g, stats, mean, rstd)
        with nc.Block() as block:
            @block.vector
            def _(dve):
                dve.memset(none, 0.0)
        plain = {"wq": w["q3"], "wk": w["k3"], "wv": w["v3"], "wo": w["p3"], "bq": none, "bk": none,
                 "bo": [(w["bp"], w["ident"])]}
        single_head_attention(nc, "a3", g, x, stats, mean, rstd, tg[:, 3:4], ctx_t, plain, 0.25, True)
        layernorm_statistics(nc, "n3b", g, stats, mean, rstd)
        spectral_map(nc, "m3", g, x, mean, rstd, tg[:, 7:8], w, out_rows)


def kernel(**inputs):
    import numpy as np
    import concourse.bacc as bacc
    from concourse.bass_utils import run_bass_kernel_spmd

    a = {k: np.asarray(v) for k, v in inputs.items()}
    p = {}
    p["ident"] = np.eye(128)
    pick = np.zeros((128, 8, 128))
    for row in range(128):
        if row % 64 < 24:
            pick[row, row % 8] = 1.0
    p["pick"] = pick
    spread = np.zeros((128, 8, 128))
    for row in range(48):
        e = row % 16
        spread[row, e // 2, 64 * (e % 2):64 * (e % 2) + 64] = 1.0
    p["spread"] = spread
    k = np.arange(128)
    turn = 2 * np.pi * (np.outer(k, k) % 128) / 128
    p["dft_cos"], p["dft_sin"], p["dft_nsin"] = np.cos(turn), np.sin(turn), -np.sin(turn)
    for i in (0, 2):
        q = f"L{i}_xattn_"
        p[f"wq{i}"] = a[q + "Wq"].T
        p[f"wkv{i}"] = np.concatenate([a[q + "Wk"].T, a[q + "Wv"].T], 1)
        p[f"wo{i}"] = a[q + "Wo"].T
        for b in "qkvo":
            p[f"b{b}{i}"] = a[q + "b" + b]
    q = "L0_ffn_"
    p["eg"] = np.concatenate([a[q + "w_gate"].transpose(1, 0, 2).reshape(128, 1024), a[q + "sw_gate"]], 1)
    p["eu"] = np.concatenate([a[q + "w_up"].transpose(1, 0, 2).reshape(128, 1024), a[q + "sw_up"]], 1)
    p["ed"] = a[q + "w_down"].reshape(8, 128, 128).transpose(1, 0, 2)
    q = "L1_xattn_"
    p["hw"], p["cw"] = a[q + "hW"], a[q + "cW"]
    for n in "qkvo":
        p[n + "w_t"] = a[q + n + "W"].T
    for n in "hcqkvo":
        p[n + "b"] = a[q + n + "b"]
    q = "L1_ffn_"
    p["w1"] = a[q + "w1"].reshape(4, 128, 128).transpose(1, 0, 2)
    p["b1"] = a[q + "b1"].reshape(4, 128).T
    p["w2"], p["b2"] = a[q + "w2"], a[q + "b2"]
    q = "L2_ffn_"
    for n in "rkv":
        p[f"w{n}_t"] = a[q + "W_" + n].T
    p["mu_r"], p["mu_k"] = a[q + "mu_r"], a[q + "mu_k"]
    q = "L3_xattn_"
    for n in "qkvp":
        p[n + "3"] = a[q + "W" + n]
    p["bp"] = a[q + "bp"]
    q = "L3_ffn_"
    p["fr"], p["fi"], p["fb"] = a[q + "w_freq_real"], a[q + "w_freq_imag"], a[q + "bias"]
    p["gates"] = np.broadcast_to(np.concatenate([a["g_xattn"], a["g_ffn"]]), (128, 8))
    pack = np.concatenate([np.asarray(p[n], np.float32).reshape(128, c) for n, c in PACK], 1)
    arrays = {
        "x_in": np.ascontiguousarray(a["x"]),
        "ctx_t": np.ascontiguousarray(a["ctx_1024"].transpose(0, 2, 1)),
        "pack": np.ascontiguousarray(pack),
        "gate_in": np.ascontiguousarray(a["L0_ffn_gate_w"]),
        "down_in": np.ascontiguousarray(a["L0_ffn_sw_down"]),
    }
    nc = bacc.Bacc("TRN2", target_bir_lowering=False, num_devices=1)
    args = [nc.dram_tensor(n, v.shape, mybir.dt.from_np(v.dtype), kind="ExternalInput").ap() for n, v in arrays.items()]
    args.append(nc.dram_tensor("out", (B, T, D), F32, kind="ExternalOutput").ap())
    build(nc, *args)
    return run_bass_kernel_spmd(nc, [arrays], core_ids=[0]).results[0]["out"]
```

```python
from contextlib import ExitStack

import concourse.bass as bass
from concourse import mybir

F32 = mybir.dt.float32
BF16 = mybir.dt.bfloat16
ALU = mybir.AluOpType
ACT = mybir.ActivationFunctionType
AX = mybir.AxisListType
MAX_OVER_PARTITIONS = bass.bass_isa.ReduceOp.max

B = 32
T = 128
D = 128
LN_EPS = 1e-5
ATT_BUFS = 4
GB = 4
GROUPS = B // GB
GT = GB * T


class Slot:

    def __init__(self, loop, fixed, total=B, bufs=ATT_BUFS):
        self.loop, self.fixed, self.total, self.bufs = loop, fixed, total, bufs

    def count(self):
        return self.fixed if self.loop is None else self.loop * self.bufs + self.fixed

    def batch(self, lag):
        c = self.fixed - lag
        return c if self.loop is None else self.loop * self.bufs + c

    def turn(self, lag):
        c = (self.fixed - lag) // self.bufs
        return c if self.loop is None else self.loop + c

    def buf(self, lag):
        return (self.fixed - lag) % self.bufs

    def live(self, lag):
        return self.loop is not None or 0 <= self.fixed - lag < self.total


def run_slots(eng, step, lags, peel, total=B, bufs=ATT_BUFS):
    for it in range(peel):
        step(Slot(None, it, total, bufs))
    with eng.Fori(0, (total - peel) // bufs) as i:
        for u in range(bufs):
            step(Slot(i, peel + u, total, bufs))
    for it in range(total, total + lags):
        step(Slot(None, it, total, bufs))


def reach(eng, sem, value):
    if not isinstance(value, int) or value > 0:
        eng.wait_ge(sem, value)


def reach_carried(eng, sem, value, scratch):
    reach(eng, sem, value)
    if not isinstance(value, int):
        eng.tensor_tensor(scratch, scratch, scratch, ALU.mult)


def many_head_attention(nc, tag, g, x, stats, mean, rstd, tg, ctx_t, w, biases):
    H, DK = 16, 8
    PAIRS = H // 2
    SCALE = float(DK) ** -0.5
    LAGS = 8
    with ExitStack() as ctx:
        def sb(name, shape, dt=F32):
            return ctx.enter_context(nc.sbuf_tensor(f"{tag}_{name}", shape, dt))

        def sem(name):
            return ctx.enter_context(nc.semaphore(f"{tag}_{name}"))

        R = range(ATT_BUFS)
        xn = [sb(f"xn{i}", [T, D]) for i in R]
        xn_t = [sb(f"xn_t{i}", [D, T]) for i in R]
        ctx_b = [sb(f"ctx_b{i}", [D, T]) for i in R]
        qk = [sb(f"qk{i}", [T, 2, H, DK]) for i in R]
        rest = [sb(f"rest{i}", [T, 2, H, DK]) for i in R]
        parts = [sb(f"parts{i}", [T, 2 * H, 64], BF16) for i in R]
        parts_t = [sb(f"parts_t{i}", [128, 2, PAIRS, T], BF16) for i in R]
        v_aug = [sb(f"v_aug{i}", [T, H, 32]) for i in R]
        rowmax = [sb(f"rowmax{i}", [T, 2, PAIRS]) for i in R]
        maxrest = [sb(f"maxrest{i}", [T, 2, PAIRS]) for i in R]
        negmax = [sb(f"negmax{i}", [T, 2, 64], BF16) for i in R]
        negmax_t = [sb(f"negmax_t{i}", [128, T], BF16) for i in R]
        probs = [sb(f"probs{i}", [T, 2, 4, T]) for i in range(2)]
        out_h = [sb(f"out_h{i}", [128, 4, T]) for i in R]
        rden = [sb(f"rden{i}", [T, H]) for i in R]
        out_n = [sb(f"out_n{i}", [T, H, DK]) for i in R]
        out_t = [sb(f"out_t{i}", [D, T]) for i in R]
        ys = [sb(f"ys{i}", [T, D]) for i in range(2)]
        zeros = sb("zeros", [128, 2, H, DK])

        ctx_in = [sem(f"ctx_in{i}") for i in R]
        q_turned, q_taken, k_turned, k_taken = sem("q_turned"), sem("q_taken"), sem("k_turned"), sem("k_taken")
        xn_ready, turned, turn_taken = sem("xn_ready"), sem("turned"), sem("turn_taken")
        mapped, mapped_taken, qk_ready = sem("mapped"), sem("mapped_taken"), sem("qk_ready")
        cut_step, parts_ready = sem("cut_step"), sem("parts_ready")
        s_ready, max_ready = sem("s_ready"), sem("max_ready")
        neg_step, negmax_rest, negmax_ready = sem("neg_step"), sem("negmax_rest"), sem("negmax_ready")
        e_ready, probs_ready, pv_done = sem("e_ready"), sem("probs_ready"), sem("pv_done")
        out_h_ready, o2_ready, v_ready = sem("out_h_ready"), sem("o2_ready"), sem("v_ready")
        rden_ready, out_n_ready = sem("rden_ready"), sem("out_n_ready")
        y_taken, x_ready, stats_ready = sem("y_taken"), sem("x_ready"), sem("stats_ready")

        ident, ones_bf, pick = g["ident"], g["ones_bf"], g["pick"]
        ident_bf = g["ident_bf"]

        def pads(pool):
            for i in R:
                pool.memset(parts[i][:, 0:H, 48:64], 0.0)
                pool.memset(parts[i][:, H:2 * H, 32:48], 0.0)
                pool.memset(negmax[i][:], 0.0)
                pool.memset(v_aug[i][:, :, DK + 1:32], 0.0)
                pool.memset(v_aug[i][:, :, DK:DK + 1], 1.0)
            pool.memset(zeros[:], 0.0)

        layernorm_statistics(nc, f"{tag}_norm", g, stats, mean, rstd, beside={"gpsimd": pads})

        ps_s = ctx.enter_context(nc.psum_tensor(f"{tag}_ps_s", [128, 2, 4, 128], F32))
        ps_e = ctx.enter_context(nc.psum_tensor(f"{tag}_ps_e", [128, 2, 4, 128], F32))
        ps_o = ctx.enter_context(nc.psum_tensor(f"{tag}_ps_o", [128, 4, 128], F32))
        ps_q = ctx.enter_context(nc.psum_tensor(f"{tag}_ps_q", [128, PAIRS, 128], BF16))
        ps_t = ctx.enter_context(nc.psum_tensor(f"{tag}_ps_t", [128, 512], F32))
        ps_p = ctx.enter_context(nc.psum_tensor(f"{tag}_ps_p", [128, 512], F32))

        with nc.Block() as block:
            @block.sync
            def _(sp):
                def step(it):
                    if it.live(0):
                        n, b = it.batch(0), it.buf(0)
                        if it.loop is not None or n >= ATT_BUFS:
                            reach(sp, mapped, n)
                        sp.dma_start(ctx_b[b][:], ctx_t[n]).then_inc(ctx_in[b], 16)

                run_slots(sp, step, LAGS, 8)

            @block.vector
            def _(dve):
                def step(it):
                    def row_maxima(half):
                        if it.live(3):
                            n, b = it.batch(3), it.buf(3)
                            reach(dve, s_ready, 2 * n + half + 1)
                            if half == 0:
                                reach(dve, negmax_ready, n - ATT_BUFS + 1)
                            dve.tensor_reduce(rowmax[b][:, :, 4 * half:4 * half + 4], ps_s[:], AX.X,
                                              ALU.max).then_inc(max_ready, 1)

                    last = None
                    if it.live(1) or it.live(5) or it.live(7):
                        reach(dve, turned, it.count())
                    if it.live(1):
                        last = dve.tensor_copy(xn_t[it.buf(1)][:], ps_t[:, 0:T])
                    if it.live(7):
                        last = dve.tensor_copy(out_t[it.buf(7)][:], ps_t[:, 256:384])
                    if it.live(5):
                        last = dve.tensor_copy(negmax_t[it.buf(5)][:], ps_t[:, 128:192].bitcast(BF16))
                    if last is not None:
                        last.then_inc(turn_taken, 1)
                    row_maxima(0)
                    if it.live(0):
                        n, b = it.batch(0), it.buf(0)
                        reach(dve, turned, n - ATT_BUFS + 1)
                        dve.tensor_scalar(xn[b][:], x[:, n, :], mean[:, bass.ds(n, 1)], rstd[:, bass.ds(n, 1)],
                                          ALU.subtract, ALU.mult).then_inc(xn_ready, 1)
                    if it.live(8):
                        n = it.batch(8)
                        reach(dve, x_ready, n + 1)
                        dve.bn_stats(stats[:, n, :], x[:, n, :]).then_inc(stats_ready, 1)
                    if it.live(2):
                        n, b = it.batch(2), it.buf(2)
                        reach(dve, q_turned, n + 1)
                        dve.tensor_copy(parts_t[b][:, 0], ps_q[:]).then_inc(q_taken, 1)
                    if it.live(6):
                        n, b = it.batch(6), it.buf(6)
                        reach(dve, o2_ready, n + 1)
                        o2 = ps_o[:].rearrange("p c (h r) -> p (c h) r", r=32)
                        dve.reciprocal(rden[b][:], o2[:, :, DK]).then_inc(rden_ready, 1)
                        if it.loop is not None or n >= ATT_BUFS:
                            reach(dve, turned, n + 7 - ATT_BUFS)
                        reach(dve, rden_ready, n + 1)
                        dve.tensor_tensor(out_n[b][:], o2[:, :, 0:DK],
                                          rden[b][:].unsqueeze(2).to_broadcast([T, H, DK]),
                                          ALU.mult).then_inc(out_n_ready, 1)
                    row_maxima(1)
                    if it.live(2):
                        n, b = it.batch(2), it.buf(2)
                        reach(dve, k_turned, n + 1)
                        dve.tensor_copy(parts_t[b][:, 1], ps_q[:]).then_inc(k_taken, 1)

                run_slots(dve, step, LAGS, 8)

            @block.gpsimd
            def _(pool):
                def step(it):
                    if it.live(4):
                        n, b = it.batch(4), it.buf(4)
                        neg, m, r = negmax[b], rowmax[b], maxrest[b]
                        zero = zeros[:, :, 0]
                        reach(pool, max_ready, 2 * n + 2)
                        if it.loop is not None or n >= ATT_BUFS:
                            reach(pool, turned, n + 5 - ATT_BUFS)
                        pool.tensor_tensor(neg[:, :, 0:8], zero, m[:], ALU.subtract).then_inc(neg_step, 1)
                        reach(pool, neg_step, 3 * n + 1)
                        pool.tensor_tensor(r[:], m[:], neg[:, :, 0:8], ALU.add).then_inc(neg_step, 1)
                        reach(pool, neg_step, 3 * n + 2)
                        pool.tensor_tensor(neg[:, :, 8:16], zero, r[:], ALU.subtract).then_inc(neg_step, 1)
                        reach(pool, neg_step, 3 * n + 3)
                        pool.tensor_tensor(r[:], r[:], neg[:, :, 8:16], ALU.add).then_inc(negmax_rest, 1)
                        reach(pool, negmax_rest, n + 1)
                        pool.tensor_tensor(neg[:, :, 16:24], zero, r[:], ALU.subtract).then_inc(negmax_ready, 1)
                    if it.live(7):
                        n = it.batch(7)
                        reach(pool, y_taken, n + 1)
                        pool.tensor_tensor(x[:, n, :], x[:, n, :], ys[it.buf(7) % 2][:], ALU.add).then_inc(x_ready, 1)
                    if it.live(1):
                        n, b = it.batch(1), it.buf(1)
                        st, f, r = parts[b], qk[b], rest[b]
                        flat = st[:].rearrange("t g r -> t (g r)")
                        k0 = flat[:, H * 64 - 16:2 * H * 64 - 16].rearrange("t (h r) -> t h r", r=64)
                        r2 = r[:].rearrange("t s h d -> t (s h) d")
                        reach(pool, qk_ready, n + 1)
                        pool.tensor_tensor(r2, f[:].rearrange("t s h d -> t (s h) d"), st[:, :, 0:DK],
                                           ALU.subtract).then_inc(cut_step, 1)
                        reach(pool, cut_step, 2 * n + 1)
                        pool.tensor_tensor(st[:, :, 24:32], r2, zeros[:].rearrange("t s h d -> t (s h) d"),
                                           ALU.add).then_inc(cut_step, 1)
                        pool.tensor_tensor(st[:, 0:H, 40:48], r[:, 0], zeros[:, 0], ALU.add)
                        pool.tensor_tensor(k0[:, :, 0:8], r[:, 1], zeros[:, 0], ALU.add)
                        reach(pool, cut_step, 2 * n + 2)
                        pool.tensor_tensor(st[:, 0:H, 32:40], r[:, 0], st[:, 0:H, 24:32], ALU.subtract)
                        pool.tensor_tensor(k0[:, :, 8:16], r[:, 1], st[:, H:2 * H, 24:32],
                                           ALU.subtract).then_inc(parts_ready, 1)

                run_slots(pool, step, LAGS, 8)

            @block.scalar
            def _(act):
                def exponentials(it, half, lag):
                    if it.live(lag):
                        n = it.batch(lag)
                        reach(act, e_ready, 2 * n + half + 1)
                        reach(act, pv_done, 2 * n + half - 1)
                        act.activation(probs[half][:], ps_e[:], ACT.Exp, scale=SCALE).then_inc(probs_ready, 1)

                def step(it):
                    exponentials(it, 1, 6)
                    if it.live(1) or it.live(4) or it.live(7):
                        reach(act, mapped, it.count())
                    if it.live(1):
                        n, b = it.batch(1), it.buf(1)
                        reach(act, parts_ready, n - ATT_BUFS + 1)
                        q_and_k = ps_p[:, 0:2 * D]
                        act.activation(parts[b][:, :, 0:24].rearrange("t g (r d) -> t g r d", d=DK),
                                       q_and_k.rearrange("p (g d) -> p g d", d=DK).unsqueeze(2)
                                       .to_broadcast([T, 2 * H, 3, DK]), ACT.Copy)
                        act.activation(qk[b][:].rearrange("t s h d -> t (s h d)"), q_and_k, ACT.Copy).then_inc(qk_ready, 1)
                    if it.live(6):
                        n, b = it.batch(6), it.buf(6)
                        reach(act, pv_done, 2 * n + 2)
                        act.activation(out_h[b][:], ps_o[:], ACT.Copy).then_inc(out_h_ready, 1)
                    if it.live(4):
                        act.activation(v_aug[it.buf(4)][:, :, 0:DK],
                                       ps_p[:, 2 * D:3 * D].rearrange("p (h d) -> p h d", d=DK),
                                       ACT.Copy).then_inc(v_ready, 1)
                    if it.live(7):
                        n = it.batch(7)
                        reach(act, x_ready, n)
                        act.activation(ys[it.buf(7) % 2][:], ps_p[:, 3 * D:4 * D], ACT.Copy, scale=tg).then_inc(y_taken, 1)
                    exponentials(it, 0, 5)

                run_slots(act, step, LAGS, 8)

            @block.tensor
            def _(pe):
                def turn(it):
                    if it.live(1) or it.live(5) or it.live(7):
                        reach(pe, turn_taken, it.count() - 1)
                    last = None
                    if it.live(1):
                        reach(pe, xn_ready, it.batch(1) + 1)
                        last = pe.transpose(ps_t[:, 0:T], xn[it.buf(1)][:], ident[:])
                    if it.live(7):
                        reach(pe, out_n_ready, it.batch(7) + 1)
                        last = pe.transpose(ps_t[:, 256:384], out_n[it.buf(7)][:].rearrange("t h d -> t (h d)"),
                                            ident[:])
                    if it.live(5):
                        reach(pe, negmax_ready, it.batch(5) + 1)
                        last = pe.transpose(ps_t[:, 128:192].bitcast(BF16),
                                            negmax[it.buf(5)][:].rearrange("t a r -> t (a r)"), ident_bf[:])
                    if last is not None:
                        last.then_inc(turned, 1)

                def maps(it):
                    last = None
                    if it.live(1) or it.live(4) or it.live(7):
                        if it.live(1):
                            reach(pe, qk_ready, it.batch(1))
                        if it.live(4):
                            reach(pe, v_ready, it.batch(4))
                        if it.live(7):
                            reach(pe, y_taken, it.batch(7))
                    if it.live(4):
                        last = pe.matmul(ps_p[:, 2 * D:3 * D], ctx_b[it.buf(4)][:], w["wkv_t"][:, D:2 * D], start=True, stop=True)
                    if it.live(1) or it.live(7):
                        reach(pe, turn_taken, it.count())
                    if it.live(1):
                        b = it.buf(1)
                        pe.matmul(ps_p[:, 0:D], xn_t[b][:], w["wq_t"], start=True, stop=False)
                        pe.matmul(ps_p[:, 0:D], ones_bf[0:3], biases[:, 0], start=False, stop=True)
                        pe.wait_ge(ctx_in[b], 16 * (it.turn(1) + 1))
                        pe.matmul(ps_p[:, D:2 * D], ctx_b[b][:], w["wkv_t"][:, 0:D], start=True, stop=False)
                        last = pe.matmul(ps_p[:, D:2 * D], ones_bf[0:3], biases[:, 1], start=False, stop=True)
                    if it.live(7):
                        pe.matmul(ps_p[:, 3 * D:4 * D], out_t[it.buf(7)][:], w["wo_t"], start=True, stop=False)
                        last = pe.matmul(ps_p[:, 3 * D:4 * D], ones_bf[0:3], biases[:, 2], start=False, stop=True)
                    if last is not None:
                        last.then_inc(mapped, 1)

                def turn_parts(it, side):
                    if it.live(2):
                        n, b = it.batch(2), it.buf(2)
                        flat = parts[b][:].rearrange("t g r -> t (g r)")
                        if side == 0:
                            reach(pe, parts_ready, n + 1)
                            reach(pe, k_taken, n)
                        else:
                            reach(pe, q_taken, n + 1)
                        for p in range(PAIRS):
                            at = side * (H * 64 - 16) + 128 * p
                            last = pe.transpose(ps_q[:, p], flat[:, at:at + 128], ident_bf[:])
                        last.then_inc(k_turned if side else q_turned, 1)

                def scores(it, half):
                    if it.live(3):
                        n, b = it.batch(3), it.buf(3)
                        if half == 0:
                            reach(pe, k_taken, n + 1)
                        reach(pe, max_ready, 2 * n + half)
                        for j in range(4):
                            for a in range(2):
                                lo, p = 64 * a, 4 * half + j
                                last = pe.matmul(ps_s[:, a, j], parts_t[b][lo:lo + 48, 0, p],
                                                 parts_t[b][lo:lo + 48, 1, p], start=True, stop=True)
                        last.then_inc(s_ready, 1)

                def shifted(it, half, lag):
                    if it.live(lag):
                        n, b = it.batch(lag), it.buf(lag)
                        if half == 0:
                            reach(pe, turn_taken, it.count())
                        reach(pe, probs_ready, 2 * n + half)
                        for j in range(4):
                            p = 4 * half + j
                            for a in range(2):
                                lo = 64 * a
                                pe.matmul(ps_e[:, a, j], parts_t[b][lo:lo + 48, 1, p],
                                          parts_t[b][lo:lo + 48, 0, p], start=True, stop=False)
                            for a in range(2):
                                lo = 64 * a
                                last = pe.matmul(ps_e[:, a, j], pick[lo:lo + 48, p], negmax_t[b][lo:lo + 48],
                                                 start=False, stop=True)
                        last.then_inc(e_ready, 1)

                def values(it, half, lag):
                    if it.live(lag):
                        n, b = it.batch(lag), it.buf(lag)
                        if half == 0:
                            reach(pe, v_ready, n + 1)
                            reach(pe, out_n_ready, n)
                        reach(pe, probs_ready, 2 * n + half + 1)
                        for j in range(4):
                            for a in range(2):
                                h = 2 * (4 * half + j) + a
                                q = 32 * (h % 4)
                                last = pe.matmul(ps_o[q:q + 32, h // 4], v_aug[b][:, h], probs[half][:, a, j],
                                                 start=True, stop=True)
                        last.then_inc(pv_done, 1)

                def step(it):
                    turn(it)
                    shifted(it, 1, 6)
                    scores(it, 0)
                    maps(it)
                    values(it, 1, 6)
                    turn_parts(it, 0)
                    shifted(it, 0, 5)
                    if it.live(6):
                        n, b = it.batch(6), it.buf(6)
                        reach(pe, out_h_ready, n + 1)
                        for c in range(4):
                            last = pe.transpose(ps_o[:, c], out_h[b][:, c], ident[:])
                        last.then_inc(o2_ready, 1)
                    scores(it, 1)
                    turn_parts(it, 1)
                    values(it, 0, 5)

                run_slots(pe, step, LAGS, 8)


class Front:

    def __init__(self, nc, ctx, tag, g, x, mean, rstd):
        self.x, self.mean, self.rstd, self.ident = x, mean, rstd, g["ident"]
        self.rows = [ctx.enter_context(nc.sbuf_tensor(f"{tag}_rows{i}", [T, GB, D], F32)) for i in range(2)]
        self.ps = ctx.enter_context(nc.psum_tensor(f"{tag}_ps_rows", [D, GB, T], F32))
        self.rows_ready = ctx.enter_context(nc.semaphore(f"{tag}_rows_ready"))
        self.turned = ctx.enter_context(nc.semaphore(f"{tag}_rows_turned"))
        self.taken = ctx.enter_context(nc.semaphore(f"{tag}_rows_taken"))

    def normalise(self, dve, it):
        if it.live(0):
            n, b = it.batch(0), it.buf(0)
            reach(dve, self.turned, n - 1)
            for j in range(GB):
                last = dve.tensor_scalar(self.rows[b][:, j], self.x[:, n * GB + j, :],
                                         self.mean[:, bass.ds(n * GB + j, 1)], self.rstd[:, bass.ds(n * GB + j, 1)],
                                         ALU.subtract, ALU.mult)
            last.then_inc(self.rows_ready, 1)

    def turn(self, pe, it, taken=None):
        if it.live(1):
            n, b = it.batch(1), it.buf(1)
            reach(pe, taken or self.taken, n)
            reach(pe, self.rows_ready, n + 1)
            for j in range(GB):
                last = pe.transpose(self.ps[:, j], self.rows[b][:, j], self.ident[:])
            last.then_inc(self.turned, 1)


def bias_parts(nc, tag, g, columns, parts):
    n = len(columns)
    with ExitStack() as ctx:
        rest = ctx.enter_context(nc.sbuf_tensor(f"{tag}_rest", [128, n], F32))
        cut = ctx.enter_context(nc.sbuf_tensor(f"{tag}_cut", [128, n, 3], BF16))
        ps_c = ctx.enter_context(nc.psum_tensor(f"{tag}_ps_c", [128, 512], F32))
        ps_r = ctx.enter_context(nc.psum_tensor(f"{tag}_ps_r", [3, n, D], F32))
        mapped, step, rows_made = (ctx.enter_context(nc.semaphore(f"{tag}_{k}")) for k in ("mapped", "step", "rows_made"))
        with nc.Block() as block:
            @block.tensor
            def _(pe):
                for i, c in enumerate(columns):
                    if isinstance(c, tuple):
                        pe.matmul(ps_c[:, i:i + 1], c[1], c[2], start=True, stop=True).then_inc(mapped, 1)
                pe.wait_ge(step, n + 5)
                for i in range(n):
                    last = pe.matmul(ps_r[:, i], cut[:, i], g["ident_bf"][:], start=True, stop=True)
                last.then_inc(rows_made, 1)

            @block.vector
            def _(dve):
                for i, c in enumerate(columns):
                    if isinstance(c, tuple):
                        dve.wait_ge(mapped, sum(isinstance(k, tuple) for k in columns))
                        dve.tensor_tensor(rest[:, i:i + 1], ps_c[:, i:i + 1], c[0], ALU.add).then_inc(step, 1)
                    else:
                        dve.tensor_copy(rest[:, i:i + 1], c).then_inc(step, 1)
                for part in range(3):
                    dve.wait_ge(step, n + 2 * part)
                    dve.tensor_copy(cut[:, :, part], rest[:]).then_inc(step, 1)
                    if part < 2:
                        dve.wait_ge(step, n + 2 * part + 1)
                        dve.tensor_tensor(rest[:], rest[:], cut[:, :, part], ALU.subtract).then_inc(step, 1)
                dve.wait_ge(rows_made, 1)
                dve.tensor_copy(parts, ps_r[:])


def mixture_of_experts(nc, tag, g, x, stats, mean, rstd, tg, w, gate_t, sd, late_loaded):
    E, HID, TILES = 16, 64, 9
    with ExitStack() as ctx:
        def sb(name, shape, dt=F32):
            return ctx.enter_context(nc.sbuf_tensor(f"{tag}_{name}", shape, dt))

        def ps(name, shape):
            return ctx.enter_context(nc.psum_tensor(f"{tag}_{name}", shape, F32))

        def sem(name):
            return ctx.enter_context(nc.semaphore(f"{tag}_{name}"))

        R = range(2)
        row_inv = sb("row_inv", [T, B])
        spread = sb("spread", [128, 8, 128], BF16)
        xs = [sb(f"xs{i}", [D, GB, T]) for i in R]
        z, th, sc, left = (sb(k, [T, GB, E]) for k in ("z", "th", "sc", "left"))
        top = sb("top", [T, GB, 8])
        cw, crest = sb("cw", [T, GB, E]), sb("crest", [T, GB, E])
        csum, cinv = sb("csum", [T, GB]), sb("cinv", [T, GB])
        cparts = sb("cparts", [T, GB, 128], BF16)
        cw_t = [sb(f"cw_t{i}", [128, GB, T], BF16) for i in R]
        silu = [sb(f"silu{i}", [128, GT]) for i in R]
        prod = [sb(f"prod{i}", [128, GT]) for i in R]
        hid = [sb(f"hid{i}", [128, GB, T]) for i in R]
        scratch_t = sb("scratch", [128, 1])
        scratch = scratch_t[:]

        def constants(pool):
            pool.memset(cparts[:], 0.0)
            pool.memset(scratch, 0.0)
            pool.wait_ge(late_loaded, 16)
            pool.tensor_copy(spread[:].rearrange("p a b -> p (a b)"), w["spread"])

        layernorm_statistics(nc, f"{tag}_norm", g, stats, mean, rstd, row_inv[:],
                             {"gpsimd": constants, "sync": lambda sp: sp.wait_ge(late_loaded, 16)})
        front = Front(nc, ctx, tag, g, x, mean, rstd)
        ps_g = [ps(f"ps_g{i}", [128, GT]) for i in R]
        ps_u = [ps(f"ps_u{i}", [128, GT]) for i in R]
        ps_c = ps("ps_c", [128, GT])
        ps_y = ps("ps_y", [T, GB, D])

        xs_ready, logits_ready, logits_taken = sem("xs_ready"), sem("logits_ready"), sem("logits_taken")
        tanh_ready, route_step, cparts_ready = sem("tanh_ready"), sem("route_step"), sem("cparts_ready")
        cparts_mid = sem("cparts_mid")
        cparts_turned, cw_t_ready = sem("cparts_turned"), sem("cw_t_ready")
        gate_up_ready, silu_ready, up_taken = sem("gate_up_ready"), sem("silu_ready"), sem("up_taken")
        spread_ready, hid_ready, down_done = sem("spread_ready"), sem("hid_ready"), sem("down_done")
        x_ready, stats_ready = sem("x_ready"), sem("stats_ready")
        LAGS, PEEL, ROUTE = 3, 4, 9

        with nc.Block() as block:
            @block.vector
            def _(dve):
                def scale_logits(it):
                    if it.live(1):
                        n = it.batch(1)
                        reach(dve, logits_ready, n + 1)
                        dve.tensor_tensor(z[:], front.ps[:, 0, 0:GB * E].rearrange("t (j e) -> t j e", e=E),
                                          row_inv[:, bass.ds(n * GB, GB)].unsqueeze(2).to_broadcast([T, GB, E]),
                                          ALU.mult).then_inc(logits_taken, 1)

                def route(it, piece):
                    if it.live(1):
                        n = it.batch(1)
                        s = n * ROUTE
                        if piece == 0:
                            reach(dve, tanh_ready, n + 1)
                            dve.tensor_scalar(sc[:], th[:], 0.5, 0.5, ALU.mult, ALU.add).then_inc(route_step, 1)
                            reach_carried(dve, route_step, s + 1, scratch)
                            for j in range(GB):
                                last = dve.max(top[:, j], sc[:, j])
                            last.then_inc(route_step, 1)
                        if piece == 1:
                            reach_carried(dve, route_step, s + 2, scratch)
                            for j in range(GB):
                                last = dve.match_replace(left[:, j], top[:, j], sc[:, j], 0.0)
                            last.then_inc(route_step, 1)
                            reach(dve, route_step, s + 3)
                            dve.tensor_tensor(cw[:], sc[:], left[:], ALU.subtract).then_inc(route_step, 1)
                        if piece == 2:
                            reach(dve, route_step, s + 4)
                            dve.tensor_reduce(csum[:], cw[:], AX.X, ALU.add).then_inc(route_step, 1)
                            reach(dve, route_step, s + 5)
                            dve.reciprocal(cinv[:], csum[:]).then_inc(route_step, 1)
                        if piece == 3:
                            reach(dve, route_step, s + 6)
                            dve.tensor_tensor(cw[:], cw[:], cinv[:].unsqueeze(2).to_broadcast([T, GB, E]),
                                              ALU.mult).then_inc(route_step, 1)
                            reach(dve, route_step, s + 7)
                            reach(dve, cparts_turned, n)
                            dve.tensor_copy(cparts[:, :, 0:E], cw[:]).then_inc(route_step, 1)
                        if piece == 4:
                            reach(dve, route_step, s + 8)
                            dve.tensor_tensor(crest[:], cw[:], cparts[:, :, 0:E], ALU.subtract).then_inc(route_step, 1)
                            reach(dve, route_step, s + 9)
                            dve.tensor_copy(cparts[:, :, E:2 * E], crest[:]).then_inc(cparts_mid, 1)
                            reach(dve, cparts_mid, n + 1)
                            dve.tensor_tensor(cparts[:, :, 2 * E:3 * E], crest[:], cparts[:, :, E:2 * E],
                                              ALU.subtract).then_inc(cparts_ready, 1)

                def update(it):
                    if it.live(3):
                        n = it.batch(3)
                        reach(dve, down_done, (n + 1) * TILES)
                        dve.scalar_tensor_tensor(x[:, bass.ds(n * GB, GB), :], ps_y[:], tg, x[:, bass.ds(n * GB, GB), :],
                                                 ALU.mult, ALU.add).then_inc(x_ready, 1)

                def statistics(it):
                    if it.live(3):
                        n = it.batch(3)
                        reach(dve, x_ready, n + 1)
                        for j in range(GB):
                            last = dve.bn_stats(stats[:, n * GB + j, :], x[:, n * GB + j, :])
                        last.then_inc(stats_ready, 1)

                def step(it):
                    update(it)
                    for e in range(TILES):
                        if it.live(2):
                            n = it.batch(2)
                            k = n * TILES + e
                            reach(dve, silu_ready, k + 1)
                            if e < 8:
                                dve.tensor_tensor(prod[e % 2][:], silu[e % 2][:], ps_u[e % 2][:], ALU.mult).then_inc(up_taken, 1)
                                reach(dve, spread_ready, n * 8 + e + 1)
                                reach(dve, down_done, k - 1)
                                reach(dve, up_taken, n * 8 + e + 1)
                                dve.tensor_tensor(hid[e % 2][:].rearrange("h j t -> h (j t)"), prod[e % 2][:], ps_c[:],
                                                  ALU.mult).then_inc(hid_ready, 1)
                            else:
                                reach(dve, down_done, k - 1)
                                dve.tensor_tensor(hid[e % 2][HID:2 * HID].rearrange("h j t -> h (j t)"), silu[e % 2][HID:2 * HID],
                                                  ps_g[e % 2][HID:2 * HID], ALU.mult).then_inc(hid_ready, 1)
                        if e == 1:
                            scale_logits(it)
                        if e == 2:
                            statistics(it)
                        if 3 <= e < 8:
                            route(it, e - 3)
                        if e == 8:
                            front.normalise(dve, it)

                run_slots(dve, step, LAGS, PEEL, GROUPS, 2)

            @block.scalar
            def _(act):
                def step(it):
                    for e in range(TILES):
                        if it.live(2):
                            n = it.batch(2)
                            k = n * TILES + e
                            reach(act, gate_up_ready, k + 1)
                            reach(act, hid_ready, k - 1)
                            if e < 8:
                                act.activation(silu[e % 2][:], ps_g[e % 2][:], ACT.Silu).then_inc(silu_ready, 1)
                            else:
                                act.activation(silu[e % 2][HID:2 * HID], ps_g[e % 2][0:HID], ACT.Silu).then_inc(silu_ready, 1)
                        if e == 0 and it.live(1):
                            n, b = it.batch(1), it.buf(1)
                            reach(act, front.turned, n + 1)
                            reach(act, gate_up_ready, (n - 1) * TILES)
                            act.activation(xs[b][:], front.ps[:], ACT.Copy).then_inc(xs_ready, 1)
                        if e == 2 and it.live(1):
                            n = it.batch(1)
                            reach(act, logits_taken, n + 1)
                            reach(act, route_step, n * ROUTE)
                            act.activation(th[:], z[:], ACT.Tanh, scale=0.5).then_inc(tanh_ready, 1)
                        if e == 8 and it.live(1):
                            n, b = it.batch(1), it.buf(1)
                            reach(act, cparts_turned, n + 1)
                            reach(act, spread_ready, 8 * (n - 1))
                            act.activation(cw_t[b][:], front.ps[:].rearrange("p j t -> p (j t)")[:, 0:GT // 2].bitcast(BF16)
                                           .rearrange("p (j t) -> p j t", j=GB), ACT.Copy).then_inc(cw_t_ready, 1)

                run_slots(act, step, LAGS, PEEL, GROUPS, 2)

            @block.tensor
            def _(pe):
                def gate_up(it, e):
                    n, b = it.batch(2), it.buf(2)
                    k = n * TILES + e
                    reach(pe, hid_ready, k - 1)
                    reach(pe, silu_ready, k - 1)
                    rows_in = xs[b][:].rearrange("d j t -> d (j t)")
                    if e < 8:
                        pe.matmul(ps_g[e % 2][:], w["eg"][:, 128 * e:128 * e + 128], rows_in, start=True, stop=True)
                        pe.matmul(ps_u[e % 2][:], w["eu"][:, 128 * e:128 * e + 128], rows_in, start=True, stop=True)\
                          .then_inc(gate_up_ready, 1)
                    else:
                        pe.matmul(ps_g[e % 2][:], w["es"], rows_in, start=True, stop=True).then_inc(gate_up_ready, 1)
                    if e < 8:
                        reach(pe, hid_ready, k if e else k - 1)
                        if e == 0:
                            reach(pe, cw_t_ready, n + 1)
                        pe.matmul(ps_c[:], spread[0:3 * E, e], cw_t[b][0:3 * E].rearrange("p j t -> p (j t)"),
                                  start=True, stop=True).then_inc(spread_ready, 1)

                def down(it, e):
                    n = it.batch(2)
                    k = n * TILES + e
                    if e == 0:
                        reach(pe, x_ready, n)
                    reach(pe, hid_ready, k + 1)
                    for j in range(GB):
                        lhs = hid[e % 2][:, j] if e < 8 else hid[e % 2][HID:2 * HID, j]
                        rhs = w["ed"][:, 128 * e:128 * e + 128] if e < 8 else sd[HID:2 * HID]
                        last = pe.matmul(ps_y[:, j], lhs, rhs, start=(e == 0 and j == 0), stop=(e == 8),
                                         skip_group_check=True)
                    last.then_inc(down_done, 1)

                def step(it):
                    for e in range(TILES):
                        if it.live(2):
                            gate_up(it, e)
                            if e:
                                down(it, e - 1)
                        if e == 0:
                            front.turn(pe, it, cw_t_ready)
                        if e == 1 and it.live(1):
                            n, b = it.batch(1), it.buf(1)
                            reach(pe, xs_ready, n + 1)
                            for j in range(GB):
                                last = pe.matmul(front.ps[:, 0, E * j:E * j + E], xs[b][:, j], gate_t[:],
                                                 start=True, stop=True)
                            last.then_inc(logits_ready, 1)
                        if e == 8 and it.live(1):
                            n = it.batch(1)
                            reach(pe, cparts_ready, n + 1)
                            for j in range(GB):
                                last = pe.transpose(front.ps[:].rearrange("p j t -> p (j t)")[:, 64 * j:64 * j + 64].bitcast(BF16),
                                                    cparts[:, j], g["ident_bf"][:])
                            last.then_inc(cparts_turned, 1)
                    if it.live(2):
                        down(it, TILES - 1)

                run_slots(pe, step, LAGS, PEEL, GROUPS, 2)


def single_head_attention(nc, tag, g, x, stats, mean, rstd, tg, ctx_t, w, bo, scale, swapped):
    mapped_keys = w["wk"] is not None
    with ExitStack() as ctx:
        def sb(name, shape, dt=F32):
            return ctx.enter_context(nc.sbuf_tensor(f"{tag}_{name}", shape, dt))

        def ps(name, shape):
            return ctx.enter_context(nc.psum_tensor(f"{tag}_{name}", shape, F32))

        def sem(name):
            return ctx.enter_context(nc.semaphore(f"{tag}_{name}"))

        R = range(2)
        xs = [sb(f"xs{i}", [D, GB, T]) for i in R]
        cs = [sb(f"cs{i}", [D, GB, T]) for i in R]
        q_t = [sb(f"q_t{i}", [D, GB, T]) for i in R]
        k_t = [sb(f"k_t{i}", [D, GB, T]) for i in R]
        v = [sb(f"v{i}", [T, GB, D]) for i in R]
        top = [sb(f"top{i}", [T, GB]) for i in R]
        total = [sb(f"total{i}", [T, GB]) for i in R]
        share = [sb(f"share{i}", [T, GB]) for i in R]
        probs = [sb(f"probs{i}", [T, GB, T]) for i in R]
        normed = [sb(f"normed{i}", [T, GB, T]) for i in R]
        probs_t = [sb(f"probs_t{i}", [T, GB, T]) for i in R]
        mixed = [sb(f"mixed{i}", [128, GB, 128]) for i in R]

        front = Front(nc, ctx, tag, g, x, mean, rstd)
        ps_q, ps_k, ps_v = ps("ps_q", [D, GB, T]), ps("ps_k", [D, GB, T]), ps("ps_v", [T, GB, D])
        ps_s, ps_t = ps("ps_s", [T, GB, T]), ps("ps_t", [T, GB, T])
        ps_m, ps_y = ps("ps_m", [128, GB, 128]), ps("ps_y", [T, GB, D])
        ctx_in = [sem(f"ctx_in{i}") for i in R]
        q_made, k_made, v_made = sem("q_made"), sem("k_made"), sem("v_made")
        q_ready, k_ready, v_ready = sem("q_ready"), sem("k_ready"), sem("v_ready")
        top_step = sem("top_step")
        s_ready, top_ready, exp_ready = sem("s_ready"), sem("top_ready"), sem("exp_ready")
        share_ready, normed_ready = sem("share_ready"), sem("normed_ready")
        probs_turned, probs_t_ready = sem("probs_turned"), sem("probs_t_ready")
        mix_made, mix_ready, y_ready = sem("mix_made"), sem("mix_ready"), sem("y_ready")
        x_ready, stats_ready = sem("x_ready"), sem("stats_ready")
        LAGS, PEEL = 4, 6

        with nc.Block() as block:
            @block.sync
            def _(sp):
                def step(it):
                    if it.live(0):
                        n, b = it.batch(0), it.buf(0)
                        reach(sp, v_made if mapped_keys else s_ready, n - 1)
                        sp.dma_start(cs[b][:], ctx_t[bass.ds(n * GB, GB)].rearrange("j d t -> d j t")).then_inc(ctx_in[b], 16)

                run_slots(sp, step, LAGS, PEEL, GROUPS, 2)

            @block.vector
            def _(dve):
                def step(it):
                    if it.live(4):
                        n = it.batch(4)
                        reach(dve, y_ready, n + 1)
                        dve.scalar_tensor_tensor(x[:, bass.ds(n * GB, GB), :], ps_y[:], tg, x[:, bass.ds(n * GB, GB), :],
                                                 ALU.mult, ALU.add).then_inc(x_ready, 1)
                        reach(dve, x_ready, n + 1)
                        for j in range(GB):
                            last = dve.bn_stats(stats[:, n * GB + j, :], x[:, n * GB + j, :])
                        last.then_inc(stats_ready, 1)
                    if it.live(2):
                        n, b = it.batch(2), it.buf(2)
                        reach(dve, s_ready, n + 1)
                        reach(dve, exp_ready, n - 1)
                        dve.tensor_reduce(top[b][:], ps_s[:], AX.X, ALU.max).then_inc(top_step, 1)
                        reach(dve, top_step, n + 1)
                        dve.tensor_scalar(top[b][:], top[b][:], -scale, None, ALU.mult).then_inc(top_ready, 1)
                    if mapped_keys and it.live(1):
                        n, b = it.batch(1), it.buf(1)
                        reach(dve, k_made, n + 1)
                        reach(dve, s_ready, n - 1)
                        dve.tensor_scalar(k_t[b][:], ps_k[:], w["bk"], None, ALU.add).then_inc(k_ready, 1)
                    if it.live(3):
                        n, b = it.batch(3), it.buf(3)
                        reach(dve, mix_made, n + 1)
                        reach(dve, y_ready, n - 1)
                        if swapped:
                            dve.tensor_copy(mixed[b][:], ps_m[:]).then_inc(mix_ready, 1)
                        else:
                            dve.scalar_tensor_tensor(mixed[b][:], ps_m[:], w["bv"], q_t[b][:],
                                                     ALU.add, ALU.add).then_inc(mix_ready, 1)
                    if it.live(2):
                        n, b = it.batch(2), it.buf(2)
                        reach(dve, exp_ready, n + 1)
                        dve.reciprocal(share[b][:], total[b][:]).then_inc(share_ready, 1)
                        reach(dve, share_ready, n + 1)
                        reach(dve, probs_turned, n - 1)
                        dve.tensor_tensor(normed[b][:], probs[b][:], share[b][:].unsqueeze(2).to_broadcast([T, GB, T]),
                                          ALU.mult).then_inc(normed_ready, 1)
                    front.normalise(dve, it)

                run_slots(dve, step, LAGS, PEEL, GROUPS, 2)

            @block.scalar
            def _(act):
                def step(it):
                    if it.live(3):
                        n, b = it.batch(3), it.buf(3)
                        reach(act, probs_turned, n + 1)
                        reach(act, mix_made, n - 1)
                        act.activation(probs_t[b][:], ps_t[:], ACT.Copy).then_inc(probs_t_ready, 1)
                    if it.live(1):
                        n, b = it.batch(1), it.buf(1)
                        reach(act, front.turned, n + 1)
                        reach(act, q_made, n - 1)
                        act.activation(xs[b][:], front.ps[:], ACT.Copy).then_inc(front.taken, 1)
                    if it.live(2):
                        n, b = it.batch(2), it.buf(2)
                        reach(act, top_ready, n + 1)
                        reach(act, normed_ready, n - 1)
                        for j in range(GB):
                            last = act.activation(probs[b][:, j], ps_s[:, j], ACT.Exp, bias=top[b][:, j:j + 1],
                                                  scale=scale, accum_out=total[b][:, j:j + 1])
                        last.then_inc(exp_ready, 1)
                    if it.live(1):
                        n, b = it.batch(1), it.buf(1)
                        reach(act, q_made, n + 1)
                        reach(act, mix_ready, n - 1)
                        act.activation(q_t[b][:], ps_q[:], ACT.Identity, bias=w["bq"]).then_inc(q_ready, 1)
                        reach(act, v_made, n + 1)
                        reach(act, mix_made, n - 1)
                        act.activation(v[b][:], ps_v[:], ACT.Copy).then_inc(v_ready, 1)

                run_slots(act, step, LAGS, PEEL, GROUPS, 2)

            @block.tensor
            def _(pe):
                def step(it):
                    if it.live(3):
                        n, b = it.batch(3), it.buf(3)
                        reach(pe, normed_ready, n + 1)
                        reach(pe, probs_t_ready, n)
                        for j in range(GB):
                            last = pe.transpose(ps_t[:, j], normed[b][:, j], g["ident"][:])
                        last.then_inc(probs_turned, 1)
                    if it.live(2):
                        n, b = it.batch(2), it.buf(2)
                        reach(pe, q_ready, n + 1)
                        if mapped_keys:
                            reach(pe, k_ready, n + 1)
                        keys = k_t[b] if mapped_keys else cs[b]
                        reach(pe, exp_ready, n)
                        for j in range(GB):
                            last = pe.matmul(ps_s[:, j], q_t[b][:, j], keys[:, j], start=True, stop=True)
                        last.then_inc(s_ready, 1)
                    front.turn(pe, it)
                    if it.live(1):
                        n, b = it.batch(1), it.buf(1)
                        pe.wait_ge(ctx_in[b], 16 * (it.turn(1) + 1))
                        if mapped_keys:
                            reach(pe, k_ready, n)
                            pe.matmul(ps_k[:], w["wk"], cs[b][:], start=True, stop=True).then_inc(k_made, 1)
                        reach(pe, v_ready, n)
                        for j in range(GB):
                            last = pe.matmul(ps_v[:, j], cs[b][:, j], w["wv"], start=True, stop=True)
                        last.then_inc(v_made, 1)
                    if it.live(3):
                        n, b = it.batch(3), it.buf(3)
                        reach(pe, probs_t_ready, n + 1)
                        reach(pe, mix_ready, n)
                        for j in range(GB):
                            if swapped:
                                last = pe.matmul(ps_m[:, j], probs_t[b][:, j], v[b][:, j], start=True, stop=True)
                            else:
                                last = pe.matmul(ps_m[:, j], v[b][:, j], probs_t[b][:, j], start=True, stop=True)
                        last.then_inc(mix_made, 1)
                    if it.live(1):
                        n, b = it.batch(1), it.buf(1)
                        reach(pe, front.taken, n + 1)
                        reach(pe, q_ready, n)
                        pe.matmul(ps_q[:], w["wq"], xs[b][:], start=True, stop=True).then_inc(q_made, 1)
                    if it.live(3):
                        n, b = it.batch(3), it.buf(3)
                        reach(pe, mix_ready, n + 1)
                        reach(pe, x_ready, n)
                        for j in range(GB):
                            pe.matmul(ps_y[:, j], mixed[b][:, j], w["wo"], start=True, stop=False)
                            last = pe.matmul(ps_y[:, j], g["ones_bf"][0:3], bo, start=False, stop=True)
                        last.then_inc(y_ready, 1)

                run_slots(pe, step, LAGS, PEEL, GROUPS, 2)


def fused_projections(nc, ctx, tag, w, made):
    names = (("q", "h"), ("k", "c"), ("v", "c"))
    ps_w = ctx.enter_context(nc.psum_tensor(f"{tag}_ps_w", [D, 3, D], F32))
    ps_b = ctx.enter_context(nc.psum_tensor(f"{tag}_ps_b", [D, 4], F32))
    multiplied = ctx.enter_context(nc.semaphore(f"{tag}_multiplied"))

    def products(pe):
        for i, (second, first) in enumerate(names):
            pe.matmul(ps_w[:, i], w[first + "w"], w[second + "w_t"], start=True, stop=True)
            last = pe.matmul(ps_b[:, i:i + 1], w[second + "w_t"], w[first + "b"], start=True, stop=True)
        last.then_inc(multiplied, 1)

    def copies(act):
        act.wait_ge(multiplied, 1)
        for i, (second, _) in enumerate(names):
            act.activation(made["w" + second], ps_w[:, i], ACT.Copy)
            act.activation(made["b" + second], ps_b[:, i:i + 1], ACT.Identity, bias=w[second + "b"])

    return {"tensor": products, "scalar": copies}


def channel_mix(nc, tag, g, x, stats, mean, rstd, tg, w):
    with ExitStack() as ctx:
        def sb(name, shape, dt=F32):
            return ctx.enter_context(nc.sbuf_tensor(f"{tag}_{name}", shape, dt))

        def ps(name, shape):
            return ctx.enter_context(nc.psum_tensor(f"{tag}_{name}", shape, F32))

        def sem(name):
            return ctx.enter_context(nc.semaphore(f"{tag}_{name}"))

        R = range(2)
        xs = [sb(f"xs{i}", [D, GB, T]) for i in R]
        xr = [sb(f"xr{i}", [D, GB, T]) for i in R]
        xk = [sb(f"xk{i}", [D, GB, T]) for i in R]
        relu = [sb(f"relu{i}", [D, GB, T]) for i in R]
        squared = [sb(f"squared{i}", [D, GB, T]) for i in R]
        gate = [sb(f"gate{i}", [T, GB, D]) for i in R]
        gated = [sb(f"gated{i}", [T, GB, D]) for i in R]
        rest = sb("rest", [D, 2])
        front = Front(nc, ctx, tag, g, x, mean, rstd)
        ps_k, ps_r, ps_v = ps("ps_k", [D, GB, T]), ps("ps_r", [T, GB, D]), ps("ps_v", [T, GB, D])
        rest_ready = sem("rest_ready")
        xs_ready, mixed_ready = sem("xs_ready"), sem("mixed_ready")
        k_made, relu_ready, squared_ready = sem("k_made"), sem("relu_ready"), sem("squared_ready")
        r_made, gate_ready, v_made = sem("r_made"), sem("gate_ready"), sem("v_made")
        gated_ready, x_ready, stats_ready = sem("gated_ready"), sem("x_ready"), sem("stats_ready")
        LAGS, PEEL = 3, 6

        with nc.Block() as block:
            @block.vector
            def _(dve):
                dve.tensor_scalar(rest[:, 0:1], w["mu_r"], -1.0, 1.0, ALU.mult, ALU.add)
                dve.tensor_scalar(rest[:, 1:2], w["mu_k"], -1.0, 1.0, ALU.mult, ALU.add).then_inc(rest_ready, 1)
                dve.wait_ge(rest_ready, 1)

                def step(it):
                    front.normalise(dve, it)
                    if it.live(1):
                        n, b = it.batch(1), it.buf(1)
                        reach(dve, xs_ready, n + 1)
                        dve.scalar_tensor_tensor(xk[b][:, :, 1:T], xs[b][:, :, 0:T - 1], rest[:, 1:2], xk[b][:, :, 1:T],
                                                 ALU.mult, ALU.add)
                        dve.scalar_tensor_tensor(xr[b][:, :, 1:T], xs[b][:, :, 0:T - 1], rest[:, 0:1], xr[b][:, :, 1:T],
                                                 ALU.mult, ALU.add).then_inc(mixed_ready, 1)
                    if it.live(3):
                        n, b = it.batch(3), it.buf(3)
                        reach(dve, v_made, n + 1)
                        reach(dve, gate_ready, n + 1)
                        dve.tensor_tensor(gated[b][:], gate[b][:], ps_v[:], ALU.mult).then_inc(gated_ready, 1)
                        reach(dve, gated_ready, n + 1)
                        dve.scalar_tensor_tensor(x[:, bass.ds(n * GB, GB), :], gated[b][:], tg,
                                                 x[:, bass.ds(n * GB, GB), :], ALU.mult, ALU.add).then_inc(x_ready, 1)
                        reach(dve, x_ready, n + 1)
                        for j in range(GB):
                            last = dve.bn_stats(stats[:, n * GB + j, :], x[:, n * GB + j, :])
                        last.then_inc(stats_ready, 1)

                run_slots(dve, step, LAGS, PEEL, GROUPS, 2)

            @block.scalar
            def _(act):
                def step(it):
                    if it.live(1):
                        n, b = it.batch(1), it.buf(1)
                        reach(act, front.turned, n + 1)
                        reach(act, mixed_ready, n - 1)
                        reach(act, r_made, n - 1)
                        act.activation(xk[b][:], front.ps[:], ACT.Copy, scale=w["mu_k"])
                        act.activation(xr[b][:], front.ps[:], ACT.Copy, scale=w["mu_r"])
                        act.activation(xs[b][:], front.ps[:], ACT.Copy).then_inc(xs_ready, 1)
                    if it.live(2):
                        n, b = it.batch(2), it.buf(2)
                        reach(act, k_made, n + 1)
                        reach(act, squared_ready, n - 1)
                        act.activation(relu[b][:], ps_k[:], ACT.Relu).then_inc(relu_ready, 1)
                        reach(act, r_made, n + 1)
                        reach(act, gated_ready, n - 1)
                        act.activation(gate[b][:], ps_r[:], ACT.Sigmoid).then_inc(gate_ready, 1)

                run_slots(act, step, LAGS, PEEL, GROUPS, 2)

            @block.gpsimd
            def _(pool):
                def step(it):
                    if it.live(2):
                        n, b = it.batch(2), it.buf(2)
                        reach(pool, v_made, n - 1)
                        reach(pool, relu_ready, n + 1)
                        pool.tensor_tensor(squared[b][:], relu[b][:], relu[b][:], ALU.mult).then_inc(squared_ready, 1)

                run_slots(pool, step, LAGS, PEEL, GROUPS, 2)

            @block.tensor
            def _(pe):
                def step(it):
                    front.turn(pe, it, xs_ready)
                    if it.live(2):
                        n, b = it.batch(2), it.buf(2)
                        reach(pe, mixed_ready, n + 1)
                        reach(pe, relu_ready, n)
                        pe.matmul(ps_k[:], w["wk_t"], xk[b][:], start=True, stop=True).then_inc(k_made, 1)
                        reach(pe, gate_ready, n)
                        for j in range(GB):
                            last = pe.matmul(ps_r[:, j], xr[b][:, j], w["wr_t"], start=True, stop=True)
                        last.then_inc(r_made, 1)
                    if it.live(3):
                        n, b = it.batch(3), it.buf(3)
                        reach(pe, squared_ready, n + 1)
                        reach(pe, gated_ready, n)
                        for j in range(GB):
                            last = pe.matmul(ps_v[:, j], squared[b][:, j], w["wv_t"], start=True, stop=True)
                        last.then_inc(v_made, 1)

                run_slots(pe, step, LAGS, PEEL, GROUPS, 2)


def spectral_map(nc, tag, g, x, stats, mean, rstd, tg, w, bo, out_rows):
    with ExitStack() as ctx:
        def sb(name, shape, dt=F32):
            return ctx.enter_context(nc.sbuf_tensor(f"{tag}_{name}", shape, dt))

        def ps(name, shape):
            return ctx.enter_context(nc.psum_tensor(f"{tag}_{name}", shape, F32))

        def sem(name):
            return ctx.enter_context(nc.semaphore(f"{tag}_{name}"))

        R = range(2)
        fwd = sb("fwd", [D, 2, D])
        whole = sb("whole", [D, D])
        xs = [sb(f"xs{i}", [D, GB, T]) for i in R]
        fwd_made, fwd_ready, whole_made = sem("fwd_made"), sem("fwd_ready"), sem("whole_made")
        front = Front(nc, ctx, tag, g, x, mean, rstd)
        ps_y = [ps(f"ps_y{i}", [T, GB, D]) for i in R]
        ps_f = ps("ps_f", [D, 3, D])

        def products(pe):
            pe.matmul(ps_f[:, 0], w["fr"], w["dft_cos"], start=True, stop=False)
            pe.matmul(ps_f[:, 0], w["fi"], w["dft_sin"], start=False, stop=True)
            pe.matmul(ps_f[:, 1], w["fi"], w["dft_cos"], start=True, stop=False)
            pe.matmul(ps_f[:, 1], w["fr"], w["dft_nsin"], start=False, stop=True).then_inc(fwd_made, 1)
            pe.wait_ge(fwd_ready, 1)
            pe.matmul(ps_f[:, 2], fwd[:, 0], w["dft_cos"], start=True, stop=False)
            pe.matmul(ps_f[:, 2], fwd[:, 1], w["dft_nsin"], start=False, stop=True).then_inc(whole_made, 1)

        def copies(act):
            act.wait_ge(fwd_made, 1)
            act.activation(fwd[:], ps_f[:, 0:2], ACT.Copy).then_inc(fwd_ready, 1)
            act.wait_ge(whole_made, 1)
            act.activation(whole[:], ps_f[:, 2], ACT.Copy, scale=1.0 / D)

        layernorm_statistics(nc, f"{tag}_norm", g, stats, mean, rstd, beside={"tensor": products, "scalar": copies})
        y_ready, x_ready = sem("y_ready"), sem("x_ready")
        stored = [sem(f"stored{i}") for i in R]
        LAGS, PEEL = 2, 4
        with nc.Block() as block:
            @block.vector
            def _(dve):
                def step(it):
                    front.normalise(dve, it)
                    if it.live(2):
                        n, b = it.batch(2), it.buf(2)
                        reach(dve, y_ready, n + 1)
                        dve.scalar_tensor_tensor(x[:, bass.ds(n * GB, GB), :], ps_y[b][:], tg, x[:, bass.ds(n * GB, GB), :],
                                                 ALU.mult, ALU.add).then_inc(x_ready, 1)

                run_slots(dve, step, LAGS, PEEL, GROUPS, 2)

            @block.scalar
            def _(act):
                def step(it):
                    if it.live(1):
                        n, b = it.batch(1), it.buf(1)
                        reach(act, front.turned, n + 1)
                        reach(act, y_ready, n - 1)
                        act.activation(xs[b][:], front.ps[:], ACT.Copy).then_inc(front.taken, 1)

                run_slots(act, step, LAGS, PEEL, GROUPS, 2)

            @block.tensor
            def _(pe):
                def step(it):
                    if it.live(2):
                        n, b = it.batch(2), it.buf(2)
                        reach(pe, front.taken, n + 1)
                        reach(pe, x_ready, n - 1)
                        for j in range(GB):
                            pe.matmul(ps_y[b][:, j], xs[b][:, j], whole[:], start=True, stop=False)
                            last = pe.matmul(ps_y[b][:, j], g["ones_bf"][0:3], bo, start=False, stop=True)
                        last.then_inc(y_ready, 1)
                    front.turn(pe, it)

                run_slots(pe, step, LAGS, PEEL, GROUPS, 2)

            @block.sync
            def _(sp):
                def step(it):
                    if it.live(2):
                        n, b = it.batch(2), it.buf(2)
                        reach(sp, x_ready, n + 1)
                        sp.dma_start(out_rows[:, bass.ds(n * GB, GB)], x[:, bass.ds(n * GB, GB), :]).then_inc(stored[b], 16)

                run_slots(sp, step, LAGS, PEEL, GROUPS, 2)
                for b in R:
                    sp.wait_ge(stored[b], 16 * GROUPS // 2)


def quantised_mlp(nc, tag, g, x, stats, mean, rstd, tg, w):
    F, FT = 512, 4
    MAGIC = 12582912.0
    with ExitStack() as ctx:
        def sb(name, shape, dt=F32):
            return ctx.enter_context(nc.sbuf_tensor(f"{tag}_{name}", shape, dt))

        def sem(name):
            return ctx.enter_context(nc.semaphore(f"{tag}_{name}"))

        R = range(2)
        row_max, row_min = sb("row_max", [128, 5]), sb("row_min", [128, 5])
        s_w, s_w_inv = sb("s_w", [128, 5]), sb("s_w_inv", [128, 5])
        w1q, w2q = sb("w1q", [128, FT, D]), sb("w2q", [D, F])
        w1_t, w2_t = sb("w1_t", [D, FT, 128], BF16), sb("w2_t", [128, FT, D], BF16)
        x_t = sb("x_t", [D, B * T])
        seen = sb("seen", [128, 2 * GROUPS])
        peak = sb("peak", [128, 2])
        s_x, s_x_inv = sb("s_x", [128, 2]), sb("s_x_inv", [128, 2])
        steps = sb("steps", [128, 5])
        steps_inv, b1q, b2q = sb("steps_inv", [128, 5]), sb("b1q", [128, FT]), sb("b2q", [128, 1])
        xi = [sb(f"xi{i}", [D, GT]) for i in R]
        xc = [sb(f"xc{i}", [D, GT]) for i in R]
        magic = sb("magic", [128, 1])
        xq = [sb(f"xq{i}", [D, GT], BF16) for i in R]
        hid = sb("hid", [128, GROUPS, FT, GT])
        rows = sb("rows", [128, 2, D])

        with ExitStack() as inner:
            ps_w = [inner.enter_context(nc.psum_tensor(f"{tag}_ps_w{i}", [128, FT, 128], F32)) for i in R]
            maxed, scaled, wq_step, w_turned = sem("maxed"), sem("scaled"), sem("wq_step"), sem("w_turned")
            with nc.Block() as block:
                @block.vector
                def _(dve):
                    w1 = w["w1"].rearrange("p (f d) -> p f d", f=FT)
                    dve.memset(magic[:], MAGIC)
                    dve.tensor_reduce(row_max[:, 0:FT], w1, AX.X, ALU.max)
                    dve.tensor_reduce(row_max[:, FT:5], w["w2"], AX.X, ALU.max)
                    dve.tensor_reduce(row_min[:, 0:FT], w1, AX.X, ALU.min)
                    dve.tensor_reduce(row_min[:, FT:5], w["w2"], AX.X, ALU.min).then_inc(maxed, 1)
                    dve.wait_ge(maxed, 1)
                    dve.scalar_tensor_tensor(row_max[:], row_min[:], -1.0, row_max[:], ALU.mult, ALU.max).then_inc(maxed, 1)
                    dve.wait_ge(maxed, 2)
                    dve.tensor_scalar(s_w[:], row_max[:], 1e-8, 1.0 / 127.0, ALU.max, ALU.mult).then_inc(scaled, 1)
                    dve.wait_ge(scaled, 1)
                    dve.reciprocal(s_w_inv[:], s_w[:]).then_inc(scaled, 1)
                    dve.wait_ge(scaled, 2)
                    for f in range(FT):
                        dve.tensor_scalar(w1q[:, f], w1[:, f], s_w_inv[:, f:f + 1], MAGIC, ALU.mult, ALU.add)
                    dve.tensor_scalar(w2q[:], w["w2"], s_w_inv[:, FT:5], MAGIC, ALU.mult, ALU.add).then_inc(wq_step, 1)
                    dve.wait_ge(wq_step, 1)
                    dve.tensor_scalar(w1q[:], w1q[:], MAGIC, -128.0, ALU.subtract, ALU.max)
                    dve.tensor_scalar(w2q[:], w2q[:], MAGIC, -128.0, ALU.subtract, ALU.max).then_inc(wq_step, 1)
                    dve.wait_ge(wq_step, 2)
                    dve.tensor_scalar(w1q[:], w1q[:], 127.0, None, ALU.min)
                    dve.tensor_scalar(w2q[:], w2q[:], 127.0, None, ALU.min).then_inc(wq_step, 1)
                    dve.wait_ge(w_turned, 1)
                    dve.tensor_copy(w1_t[:], ps_w[0][:])
                    dve.tensor_copy(w2_t[:], ps_w[1][:])

                @block.tensor
                def _(pe):
                    pe.wait_ge(wq_step, 3)
                    for f in range(FT):
                        pe.transpose(ps_w[0][:, f], w1q[:, f], g["ident"][:])
                        last = pe.transpose(ps_w[1][:, f], w2q[:, 128 * f:128 * f + 128], g["ident"][:])
                    last.then_inc(w_turned, 1)

        with ExitStack() as inner:
            front = Front(nc, inner, tag, g, x, mean, rstd)
            turned_ready, seen_ready = sem("turned_ready"), sem("seen_ready")
            LAGS, PEEL = 1, 4
            with nc.Block() as block:
                @block.vector
                def _(dve):
                    def step(it):
                        front.normalise(dve, it)
                        if it.live(1):
                            n = it.batch(1)
                            reach(dve, turned_ready, n + 1)
                            dve.tensor_reduce(seen[:, bass.ds(n, 1)], x_t[:, bass.ds(n * GT, GT)], AX.X, ALU.max)\
                               .then_inc(seen_ready, 1)

                    run_slots(dve, step, LAGS, PEEL, GROUPS, 2)

                @block.scalar
                def _(act):
                    def step(it):
                        if it.live(1):
                            n = it.batch(1)
                            reach(act, front.turned, n + 1)
                            act.activation(x_t[:, bass.ds(n * GT, GT)], front.ps[:].rearrange("d j t -> d (j t)"),
                                           ACT.Copy).then_inc(turned_ready, 1)

                    run_slots(act, step, LAGS, PEEL, GROUPS, 2)

                @block.tensor
                def _(pe):
                    def step(it):
                        front.turn(pe, it, turned_ready)

                    run_slots(pe, step, LAGS, PEEL, GROUPS, 2)

        def scales(which, col, b_of, b_to, first, last_):
            at = f"{tag}_{which}"
            with ExitStack() as inner:
                local_max, whole_max, step = (inner.enter_context(nc.semaphore(f"{at}_{k}")) for k in ("local", "whole", "step"))
                local = inner.enter_context(nc.sbuf_tensor(f"{at}_localmax", [128, 1], F32))
                n = last_ - first
                with nc.Block() as block:
                    @block.vector
                    def _(dve):
                        dve.tensor_reduce(local[:], seen[:, 0:GROUPS], AX.X, ALU.max).then_inc(local_max, 1)
                        dve.wait_ge(whole_max, 1)
                        dve.tensor_scalar(s_x[:, col:col + 1], peak[:, col:col + 1], 1e-8, 1.0 / 255.0, ALU.max, ALU.mult).then_inc(step, 1)
                        dve.wait_ge(step, 1)
                        dve.reciprocal(s_x_inv[:, col:col + 1], s_x[:, col:col + 1])
                        dve.tensor_scalar(steps[:, first:last_], s_w[:, first:last_], s_x[:, col:col + 1], None, ALU.mult).then_inc(step, 1)
                        dve.wait_ge(step, 2)
                        dve.reciprocal(steps_inv[:, first:last_], steps[:, first:last_]).then_inc(step, 1)
                        dve.wait_ge(step, 3)
                        dve.tensor_tensor(b_to, b_of, steps_inv[:, first:last_], ALU.mult).then_inc(step, 1)
                        dve.wait_ge(step, 4)
                        dve.tensor_scalar(b_to, b_to, MAGIC, None, ALU.add).then_inc(step, 1)
                        dve.wait_ge(step, 5)
                        dve.tensor_scalar(b_to, b_to, MAGIC, None, ALU.subtract).then_inc(step, 1)
                        dve.wait_ge(step, 6)
                        dve.tensor_tensor(b_to, b_to, steps[:, first:last_], ALU.mult).then_inc(step, 1)

                    @block.gpsimd
                    def _(pool):
                        pool.wait_ge(local_max, 1)
                        pool.partition_all_reduce(peak[:, col:col + 1], local[:], 128, MAX_OVER_PARTITIONS).then_inc(whole_max, 1)

        scales("in", 0, w["b1"], b1q[:], 0, FT)

        with ExitStack() as inner:
            ps_h = [[inner.enter_context(nc.psum_tensor(f"{tag}_ps_h{i}{f}", [128, GT], F32)) for f in range(FT)] for i in R]
            clipped, rounded, xq_ready = sem("clipped"), sem("rounded"), sem("xq_ready")
            h_made, hid_ready, hid_seen = sem("h_made"), sem("hid_ready"), sem("hid_seen")
            LAGS, PEEL = 2, 4
            with nc.Block() as block:
                @block.vector
                def _(dve):
                    def step(it):
                        if it.live(0):
                            n, b = it.batch(0), it.buf(0)
                            reach(dve, rounded, n + 1)
                            dve.tensor_scalar(xc[b][:], xi[b][:], MAGIC, MAGIC + 255.0, ALU.max, ALU.min).then_inc(clipped, 1)
                            reach(dve, clipped, n + 1)
                            reach(dve, h_made, n - 1)
                            dve.tensor_scalar(xq[b][:], xc[b][:], MAGIC, None, ALU.subtract).then_inc(xq_ready, 1)
                        if it.live(2):
                            n = it.batch(2)
                            reach(dve, hid_ready, n + 1)
                            dve.tensor_reduce(seen[:, bass.ds(n, 1)], hid[:, n].rearrange("p f t -> p (f t)"), AX.X,
                                              ALU.max).then_inc(hid_seen, 1)

                    run_slots(dve, step, LAGS, PEEL, GROUPS, 2)

                @block.tensor
                def _(pe):
                    def step(it):
                        if it.live(1):
                            n, b = it.batch(1), it.buf(1)
                            reach(pe, xq_ready, n + 1)
                            reach(pe, hid_ready, n - 1)
                            for f in range(FT):
                                last = pe.matmul(ps_h[b][f][:], w1_t[:, f], xq[b][:], start=True, stop=True)
                            last.then_inc(h_made, 1)

                    run_slots(pe, step, LAGS, PEEL, GROUPS, 2)

                @block.scalar
                def _(act):
                    def step(it):
                        if it.live(0):
                            n, b = it.batch(0), it.buf(0)
                            reach(act, clipped, n - 1)
                            act.activation(xi[b][:], x_t[:, bass.ds(n * GT, GT)], ACT.Identity, bias=magic[:],
                                           scale=s_x_inv[:, 0:1]).then_inc(rounded, 1)
                        if it.live(1):
                            n, b = it.batch(1), it.buf(1)
                            reach(act, h_made, n + 1)
                            for f in range(FT):
                                last = act.activation(hid[:, n, f], ps_h[b][f][:], ACT.Relu, bias=b1q[:, f:f + 1],
                                                      scale=steps[:, f:f + 1])
                            last.then_inc(hid_ready, 1)

                    run_slots(act, step, LAGS, PEEL, GROUPS, 2)

        scales("hid", 1, w["b2"], b2q[:], FT, 5)

        with ExitStack() as inner:
            ps_r = inner.enter_context(nc.psum_tensor(f"{tag}_ps_r", [128, 2, D], F32))
            rows_made = sem("rows_made")
            with nc.Block() as block:
                @block.tensor
                def _(pe):
                    pe.matmul(ps_r[:, 0], steps[:, FT:5].to_broadcast([128, 128]), g["ident"][:], start=True, stop=True)
                    pe.matmul(ps_r[:, 1], b2q[:].to_broadcast([128, 128]), g["ident"][:], start=True, stop=True)\
                      .then_inc(rows_made, 1)

                @block.vector
                def _(dve):
                    dve.wait_ge(rows_made, 1)
                    dve.tensor_scalar(rows[:], ps_r[:], tg, None, ALU.mult)

            ps_y = [inner.enter_context(nc.psum_tensor(f"{tag}_ps_y{i}", [T, GB, D], F32)) for i in R]
            hi = [sb(f"hi{i}", [128, FT, GT]) for i in R]
            hq = [sb(f"hq{i}", [128, FT, GT], BF16) for i in R]
            ys = [sb(f"ys{i}", [T, GB, D]) for i in R]
            rounded_h, hq_ready = sem("rounded_h"), sem("hq_ready")
            y_ready, y_step, x_ready, stats_ready, biased = (sem(k) for k in ("y_ready", "y_step", "x_ready", "stats_ready", "biased"))
            LAGS, PEEL = 3, 4
            with nc.Block() as block:
                @block.vector
                def _(dve):
                    def step(it):
                        if it.live(0):
                            n, b = it.batch(0), it.buf(0)
                            reach(dve, rounded_h, n + 1)
                            reach(dve, y_ready, n - 1)
                            dve.tensor_scalar(hq[b][:], hi[b][:], MAGIC + 255.0, MAGIC, ALU.min, ALU.subtract).then_inc(hq_ready, 1)
                        if it.live(2):
                            n, b = it.batch(2), it.buf(2)
                            reach(dve, y_ready, n + 1)
                            reach(dve, x_ready, n - 1)
                            dve.tensor_tensor(ys[b][:], ps_y[b][:], rows[:, 0:1].to_broadcast([T, GB, D]),
                                              ALU.mult).then_inc(y_step, 1)
                        if it.live(3):
                            n = it.batch(3)
                            reach(dve, x_ready, n + 1)
                            for j in range(GB):
                                last = dve.bn_stats(stats[:, n * GB + j, :], x[:, n * GB + j, :])
                            last.then_inc(stats_ready, 1)

                    run_slots(dve, step, LAGS, PEEL, GROUPS, 2)

                @block.scalar
                def _(act):
                    def step(it):
                        if it.live(0):
                            n, b = it.batch(0), it.buf(0)
                            reach(act, hq_ready, n - 1)
                            act.activation(hi[b][:], hid[:, n], ACT.Identity, bias=magic[:], scale=s_x_inv[:, 1:2])\
                               .then_inc(rounded_h, 1)

                    run_slots(act, step, LAGS, PEEL, GROUPS, 2)

                @block.gpsimd
                def _(pool):
                    def step(it):
                        if it.live(0):
                            n = it.batch(0)
                            pool.tensor_tensor(x[:, bass.ds(n * GB, GB), :], x[:, bass.ds(n * GB, GB), :],
                                               rows[:, 1:2].to_broadcast([T, GB, D]), ALU.add).then_inc(biased, 1)
                        if it.live(2):
                            n, b = it.batch(2), it.buf(2)
                            reach(pool, y_step, n + 1)
                            reach(pool, biased, n + 1)
                            pool.tensor_tensor(x[:, bass.ds(n * GB, GB), :], ys[b][:], x[:, bass.ds(n * GB, GB), :],
                                               ALU.add).then_inc(x_ready, 1)

                    run_slots(pool, step, LAGS, PEEL, GROUPS, 2)

                @block.tensor
                def _(pe):
                    def step(it):
                        if it.live(1):
                            n, b = it.batch(1), it.buf(1)
                            reach(pe, hq_ready, n + 1)
                            reach(pe, y_step, n - 1)
                            for j in range(GB):
                                for f in range(FT):
                                    last = pe.matmul(ps_y[b][:, j], hq[b][:, f, T * j:T * j + T], w2_t[:, f],
                                                     start=(f == 0), stop=(f == FT - 1))
                            last.then_inc(y_ready, 1)

                    run_slots(pe, step, LAGS, PEEL, GROUPS, 2)


def layernorm_statistics(nc, tag, g, stats, mean, rstd, row_inv=None, beside=None):
    beside = beside or {}
    with ExitStack() as ctx:
        def sb(name):
            return ctx.enter_context(nc.sbuf_tensor(f"{tag}_{name}", [128, B], F32))

        half, gap2, var, eps_var, root, inv = (sb(k) for k in ("half", "gap2", "var", "eps_var", "root", "inv"))
        step = ctx.enter_context(nc.semaphore(f"{tag}_step"))
        to_root = ctx.enter_context(nc.semaphore(f"{tag}_to_root"))
        rooted = ctx.enter_context(nc.semaphore(f"{tag}_rooted"))
        with nc.Block() as block:
            @block.vector
            def _(dve):
                even, odd = stats[:, :, 1], stats[:, :, 4]
                dve.tensor_tensor(half[:], even, odd, ALU.subtract).then_inc(step, 1)
                dve.tensor_tensor(mean[:], even, odd, ALU.add).then_inc(step, 1)
                dve.tensor_tensor(var[:], stats[:, :, 2], stats[:, :, 5], ALU.add).then_inc(step, 1)
                dve.wait_ge(step, 3)
                dve.scalar_tensor_tensor(gap2[:], half[:], 0.25, half[:], ALU.mult, ALU.mult).then_inc(step, 1)
                dve.tensor_scalar(mean[:], mean[:], 0.5, None, ALU.mult).then_inc(step, 1)
                dve.wait_ge(step, 4)
                dve.scalar_tensor_tensor(var[:], var[:], 1.0 / D, gap2[:], ALU.mult, ALU.add).then_inc(step, 1)
                dve.wait_ge(step, 6)
                dve.tensor_scalar(eps_var[:], var[:], LN_EPS, None, ALU.add).then_inc(to_root, 1)

                def newton(square, k):
                    dve.wait_ge(rooted, k)
                    dve.reciprocal(inv[:], root[:]).then_inc(step, 1)
                    at = 4 + 3 * k
                    dve.wait_ge(step, at)
                    dve.tensor_tensor(inv[:], inv[:], square, ALU.mult).then_inc(step, 1)
                    dve.wait_ge(step, at + 1)
                    dve.tensor_tensor(inv[:], inv[:], root[:], ALU.add).then_inc(step, 1)
                    dve.wait_ge(step, at + 2)

                newton(eps_var[:], 1)
                dve.tensor_scalar(inv[:], inv[:], 0.5, None, ALU.mult).then_inc(to_root, 1)
                dve.wait_ge(to_root, 2)
                dve.reciprocal(rstd[:], inv[:]).then_inc(to_root, 1)
                if row_inv is not None:
                    dve.wait_ge(to_root, 3)
                    dve.tensor_tensor(var[:], var[:], rstd[:], ALU.mult).then_inc(to_root, 1)
                    dve.wait_ge(to_root, 4)
                    dve.scalar_tensor_tensor(var[:], var[:], float(D), rstd[:], ALU.mult, ALU.mult).then_inc(to_root, 1)
                    dve.wait_ge(rooted, 2)
                    dve.tensor_scalar(root[:], root[:], 1e-12, None, ALU.max).then_inc(rooted, 1)
                    dve.wait_ge(rooted, 3)
                    dve.reciprocal(inv[:], root[:]).then_inc(step, 1)
                    dve.wait_ge(step, 10)
                    dve.tensor_tensor(inv[:], inv[:], var[:], ALU.mult).then_inc(step, 1)
                    dve.wait_ge(step, 11)
                    dve.tensor_tensor(inv[:], inv[:], root[:], ALU.add).then_inc(step, 1)
                    dve.wait_ge(step, 12)
                    dve.tensor_scalar(inv[:], inv[:], 0.5, 1e-12, ALU.mult, ALU.max).then_inc(step, 1)
                    dve.wait_ge(step, 13)
                    dve.reciprocal(row_inv[:], inv[:]).then_inc(step, 1)

            @block.scalar
            def _(act):
                act.wait_ge(to_root, 1)
                act.activation(root[:], eps_var[:], ACT.Sqrt).then_inc(rooted, 1)
                if row_inv is not None:
                    act.wait_ge(to_root, 5)
                    act.activation(root[:], var[:], ACT.Sqrt).then_inc(rooted, 1)
                if "scalar" in beside:
                    beside["scalar"](act)

            if "tensor" in beside:
                @block.tensor
                def _(pe):
                    beside["tensor"](pe)

            if "gpsimd" in beside:
                @block.gpsimd
                def _(pool):
                    beside["gpsimd"](pool)

            if "sync" in beside:
                @block.sync
                def _(sp):
                    beside["sync"](sp)


PACK = [
    ("ident", 128), ("gates", 8), ("wq0", 128), ("wkv0", 256), ("wo0", 128), ("wo2", 128),
    ("bq0", 1), ("bk0", 1), ("bv0", 1), ("bo0", 1), ("bq2", 1), ("bk2", 1), ("bv2", 1), ("bo2", 1),
    ("ob", 1), ("bp", 1), ("fb", 1), ("pick", 1024),
    ("spread", 1024), ("dft_cos", 128), ("dft_sin", 128), ("dft_nsin", 128),
    ("eg", 1024), ("eu", 1024), ("es", 128), ("ed", 1024),
    ("hw", 128), ("cw", 128), ("qw_t", 128), ("kw_t", 128), ("vw_t", 128), ("ow_t", 128),
    ("hb", 1), ("cb", 1), ("qb", 1), ("kb", 1), ("vb", 1),
    ("w1", 512), ("b1", 4), ("w2", 512), ("b2", 1),
    ("wq2", 128), ("wkv2", 256),
    ("wr_t", 128), ("wk_t", 128), ("wv_t", 128), ("mu_r", 1), ("mu_k", 1),
    ("q3_t", 128), ("k3_t", 128), ("v3", 128), ("p3", 128),
    ("fr", 128), ("fi", 128),
]
EARLY = sum(n for _, n in PACK[:18])
PACKED = sum(n for _, n in PACK)


def build(nc, x_in, ctx_t, pack, gate_in, down_in, out):
    x_rows = x_in.rearrange("b t d -> t b d")
    out_rows = out.rearrange("b t d -> t b d")
    with ExitStack() as ctx:
        def sb(name, shape, dt=F32):
            return ctx.enter_context(nc.sbuf_tensor(name, shape, dt))

        wp = sb("wp", [128, PACKED])
        w, at = {}, 0
        for name, n in PACK:
            w[name] = wp[:, at:at + n]
            at += n
        x = sb("x", [T, B, D])
        stats, mean, rstd = sb("stats", [T, B, 6]), sb("mean", [T, B]), sb("rstd", [T, B])
        tg = sb("tg", [128, 8])
        ident_bf, ones_bf = sb("ident_bf", [128, 128], BF16), sb("ones_bf", [128, 128], BF16)
        pick = sb("pick", [128, 8, 128], BF16)
        g = {"ident": w["ident"], "ident_bf": ident_bf, "ones_bf": ones_bf, "pick": pick}

        x_loaded = [ctx.enter_context(nc.semaphore(f"x_loaded{i}")) for i in range(4)]
        w_loaded = ctx.enter_context(nc.semaphore("w_loaded"))
        late_loaded = ctx.enter_context(nc.semaphore("late_loaded"))
        setup = ctx.enter_context(nc.semaphore("setup"))
        biases = sb("biases", [3, 9, D], BF16)
        E, HID = gate_in.shape[0], down_in.shape[0]
        gate_t, sd = sb("gate_t", [D, E]), sb("sd", [2 * HID, D])
        gr, gsq, gn = sb("gr", [E, D]), sb("gsq", [E, D]), sb("gn", [E, 4])
        gate_loaded, gate_step, gate_turned = (ctx.enter_context(nc.semaphore(k)) for k in ("gate_loaded", "gate_step", "gate_turned"))
        first = ExitStack()
        ps_gate = first.enter_context(nc.psum_tensor("ps_gate", [D, 128], F32))
        with nc.Block() as block:
            @block.sync
            def _(sp):
                sp.dma_start(gr[:], gate_in).then_inc(gate_loaded, 16)
                sp.dma_start(sd[HID:2 * HID], down_in).then_inc(gate_loaded, 16)
                for i in range(4):
                    sp.dma_start(x[:, 8 * i:8 * i + 8], x_rows[:, 8 * i:8 * i + 8]).then_inc(x_loaded[i], 16)

            @block.scalar
            def _(act):
                act.dma_start(wp[:, 0:EARLY], pack[:, 0:EARLY]).then_inc(w_loaded, 16)
                act.wait_ge(gate_step, 2)
                act.activation(gn[:, 1:2], gn[:, 0:1], ACT.Sqrt).then_inc(gate_step, 1)
                act.wait_ge(w_loaded, 16)
                act.wait_ge(x_loaded[3], 16)
                act.dma_start(wp[:, EARLY:], pack[:, EARLY:]).then_inc(late_loaded, 16)
                act.activation(pick[:].rearrange("p a b -> p (a b)"), w["pick"], ACT.Copy).then_inc(setup, 1)
                act.activation(tg[:], w["gates"], ACT.Tanh).then_inc(setup, 1)

            @block.gpsimd
            def _(pool):
                pool.memset(ones_bf[:], 1.0).then_inc(setup, 1)
                pool.wait_ge(w_loaded, 16)
                pool.tensor_copy(ident_bf[:], w["ident"]).then_inc(setup, 1)

            @block.tensor
            def _(pe):
                pe.wait_ge(w_loaded, 16)
                pe.wait_ge(gate_step, 9)
                pe.transpose(ps_gate[:, 0:E], gr[:], w["ident"][0:E, 0:E]).then_inc(gate_turned, 1)

            @block.vector
            def _(dve):
                dve.wait_ge(gate_loaded, 32)
                dve.tensor_tensor(gsq[:], gr[:], gr[:], ALU.mult).then_inc(gate_step, 1)
                dve.wait_ge(gate_step, 1)
                dve.tensor_reduce(gn[:, 0:1], gsq[:], AX.X, ALU.add).then_inc(gate_step, 1)
                dve.wait_ge(gate_step, 3)
                dve.tensor_scalar(gn[:, 1:2], gn[:, 1:2], 1e-12, None, ALU.max).then_inc(gate_step, 1)
                dve.wait_ge(gate_step, 4)
                dve.reciprocal(gn[:, 2:3], gn[:, 1:2]).then_inc(gate_step, 1)
                dve.wait_ge(gate_step, 5)
                dve.scalar_tensor_tensor(gn[:, 2:3], gn[:, 2:3], gn[:, 0:1], gn[:, 1:2], ALU.mult, ALU.add).then_inc(gate_step, 1)
                dve.wait_ge(gate_step, 6)
                dve.tensor_scalar(gn[:, 2:3], gn[:, 2:3], 0.5, 1e-12, ALU.mult, ALU.max).then_inc(gate_step, 1)
                dve.wait_ge(gate_step, 7)
                dve.reciprocal(gn[:, 3:4], gn[:, 2:3]).then_inc(gate_step, 1)
                dve.wait_ge(gate_step, 8)
                dve.tensor_scalar(gr[:], gr[:], gn[:, 3:4], None, ALU.mult).then_inc(gate_step, 1)
                for n in range(B):
                    if n % 8 == 0:
                        dve.wait_ge(x_loaded[n // 8], 16)
                    dve.bn_stats(stats[:, n, :], x[:, n, :]).then_inc(setup, 1)
                dve.wait_ge(gate_turned, 1)
                dve.tensor_copy(gate_t[:], ps_gate[:, 0:E]).then_inc(gate_step, 1)

        first.close()
        bias_parts(nc, "bias", g, [w["bq0"], w["bk0"], (w["bo0"], w["wo0"], w["bv0"]),
                                   w["bq2"], w["bk2"], (w["bo2"], w["wo2"], w["bv2"]), w["ob"], w["bp"], w["fb"]], biases[:])

        def att(i):
            return {"wq_t": w[f"wq{i}"], "wkv_t": w[f"wkv{i}"], "wo_t": w[f"wo{i}"], "bq": w[f"bq{i}"],
                    "bk": w[f"bk{i}"], "bv": w[f"bv{i}"], "bo": w[f"bo{i}"]}

        many_head_attention(nc, "a0", g, x, stats, mean, rstd, tg[:, 0:1], ctx_t, att(0), biases[:, 0:3])
        mixture_of_experts(nc, "m0", g, x, stats, mean, rstd, tg[:, 4:5], w, gate_t, sd, late_loaded)
        made = ctx.enter_context(nc.sbuf_tensor("made", [D, 3 * D + 3], F32))
        fused = {"wq": made[:, 0:D], "wk": made[:, D:2 * D], "wv": made[:, 2 * D:3 * D], "bq": made[:, 384:385],
                 "bk": made[:, 385:386], "bv": made[:, 386:387], "wo": w["ow_t"]}
        with ExitStack() as inner:
            layernorm_statistics(nc, "n1a", g, stats, mean, rstd, beside=fused_projections(nc, inner, "f1", w, fused))
        single_head_attention(nc, "a1", g, x, stats, mean, rstd, tg[:, 1:2], ctx_t, fused, biases[:, 6],
                              float(D) ** -0.5, False)
        layernorm_statistics(nc, "n1b", g, stats, mean, rstd)
        quantised_mlp(nc, "m1", g, x, stats, mean, rstd, tg[:, 5:6], w)
        used = sorted(nc.released_uncleared_semaphores)
        with nc.Block() as block:
            @block.gpsimd
            def _(pool):
                for number in used:
                    if number - 1 not in used:
                        end = number
                        while end in used:
                            end += 1
                        pool.sem_clear(range(number, end))
        many_head_attention(nc, "a2", g, x, stats, mean, rstd, tg[:, 2:3], ctx_t, att(2), biases[:, 3:6])
        layernorm_statistics(nc, "n2b", g, stats, mean, rstd)
        channel_mix(nc, "m2", g, x, stats, mean, rstd, tg[:, 6:7], w)
        none = made[:, 386:387]
        with ExitStack() as inner:
            ps_a = inner.enter_context(nc.psum_tensor("f3_ps", [D, D], F32))
            multiplied = inner.enter_context(nc.semaphore("f3_multiplied"))

            def product(pe):
                pe.matmul(ps_a[:], w["q3_t"], w["k3_t"], start=True, stop=True).then_inc(multiplied, 1)

            def copy(act):
                act.wait_ge(multiplied, 1)
                act.activation(made[:, 0:D], ps_a[:], ACT.Copy)

            layernorm_statistics(nc, "n3a", g, stats, mean, rstd, beside={
                "gpsimd": lambda pool: pool.memset(none, 0.0), "tensor": product, "scalar": copy})
        plain = {"wq": made[:, 0:D], "wk": None, "wv": w["v3"], "wo": w["p3"], "bq": none, "bk": none}
        single_head_attention(nc, "a3", g, x, stats, mean, rstd, tg[:, 3:4], ctx_t, plain, biases[:, 7], 0.25, True)
        spectral_map(nc, "m3", g, x, stats, mean, rstd, tg[:, 7:8], w, biases[:, 8], out_rows)


def kernel(**inputs):
    import numpy as np
    import concourse.bacc as bacc
    from concourse.bass_utils import run_bass_kernel_spmd

    a = {k: np.asarray(v) for k, v in inputs.items()}
    p = {}
    p["ident"] = np.eye(128)
    pick = np.zeros((128, 8, 128))
    for row in range(128):
        if row % 64 < 24:
            pick[row, row % 8] = 1.0
    p["pick"] = pick
    spread = np.zeros((128, 8, 128))
    for row in range(48):
        e = row % 16
        spread[row, e // 2, 64 * (e % 2):64 * (e % 2) + 64] = 1.0
    p["spread"] = spread
    k = np.arange(128)
    turn = 2 * np.pi * (np.outer(k, k) % 128) / 128
    p["dft_cos"], p["dft_sin"], p["dft_nsin"] = np.cos(turn), np.sin(turn), -np.sin(turn)
    for i in (0, 2):
        q = f"L{i}_xattn_"
        p[f"wq{i}"] = a[q + "Wq"].T
        p[f"wkv{i}"] = np.concatenate([a[q + "Wk"].T, a[q + "Wv"].T], 1)
        p[f"wo{i}"] = a[q + "Wo"].T
        for b in "qkvo":
            p[f"b{b}{i}"] = a[q + "b" + b]
    q = "L0_ffn_"
    p["eg"] = a[q + "w_gate"].transpose(1, 0, 2)
    p["eu"] = a[q + "w_up"].transpose(1, 0, 2)
    p["es"] = np.concatenate([a[q + "sw_gate"], a[q + "sw_up"]], 1)
    p["ed"] = a[q + "w_down"].reshape(8, 128, 128).transpose(1, 0, 2)
    q = "L1_xattn_"
    p["hw"], p["cw"] = a[q + "hW"], a[q + "cW"]
    for n in "qkvo":
        p[n + "w_t"] = a[q + n + "W"].T
    for n in "hcqkvo":
        p[n + "b"] = a[q + n + "b"]
    q = "L1_ffn_"
    p["w1"] = a[q + "w1"].reshape(4, 128, 128).transpose(1, 0, 2)
    p["b1"] = a[q + "b1"].reshape(4, 128).T
    p["w2"], p["b2"] = a[q + "w2"], a[q + "b2"]
    q = "L2_ffn_"
    for n in "rkv":
        p[f"w{n}_t"] = a[q + "W_" + n].T
    p["mu_r"], p["mu_k"] = a[q + "mu_r"], a[q + "mu_k"]
    q = "L3_xattn_"
    p["q3_t"], p["k3_t"] = a[q + "Wq"].T, a[q + "Wk"].T
    p["v3"], p["p3"] = a[q + "Wv"], a[q + "Wp"]
    p["bp"] = a[q + "bp"]
    q = "L3_ffn_"
    p["fr"], p["fi"], p["fb"] = a[q + "w_freq_real"], a[q + "w_freq_imag"], a[q + "bias"]
    p["gates"] = np.broadcast_to(np.concatenate([a["g_xattn"], a["g_ffn"]]), (128, 8))
    pack = np.concatenate([np.asarray(p[n], np.float32).reshape(128, c) for n, c in PACK], 1)
    arrays = {
        "x_in": np.ascontiguousarray(a["x"]),
        "ctx_t": np.ascontiguousarray(a["ctx_1024"].transpose(0, 2, 1)),
        "pack": np.ascontiguousarray(pack),
        "gate_in": np.ascontiguousarray(a["L0_ffn_gate_w"]),
        "down_in": np.ascontiguousarray(a["L0_ffn_sw_down"]),
    }
    nc = bacc.Bacc("TRN2", target_bir_lowering=False, num_devices=1)
    args = [nc.dram_tensor(n, v.shape, mybir.dt.from_np(v.dtype), kind="ExternalInput").ap() for n, v in arrays.items()]
    args.append(nc.dram_tensor("out", (B, T, D), F32, kind="ExternalOutput").ap())
    build(nc, *args)
    return run_bass_kernel_spmd(nc, [arrays], core_ids=[0]).results[0]["out"]
```
